# Optimizing a Trainium2 kernel written in Bass

```python
import numpy as np
import jax
import jax.numpy as jnp

def _softmax(x, axis=-1):
    return jax.nn.softmax(x, axis=axis)

def _gelu(x):
    return jax.nn.gelu(x, approximate=True)

def _silu(x):
    return jax.nn.silu(x)

def _sigmoid(x):
    return jax.nn.sigmoid(x)

def _layernorm(x, axis=-1, eps=1e-05):
    m = jnp.mean(x, axis=axis, keepdims=True)
    v = jnp.var(x, axis=axis, keepdims=True)
    return (x - m) / jnp.sqrt(v + eps)

def _scatter_add(tgt, idx, src, axis=0):
    return tgt.at[idx].add(src)

def _segment_sum(src, seg, n):
    return jax.ops.segment_sum(src, seg, n)
kernel_name = 'mk_gnn_ffn_d1_gnn_r8_c4d39d'

def setup_inputs(seed: int=0):
    np.random.seed(seed)
    _w = jnp.asarray

    def _rec_inputs():
        import jax
        import jax.numpy as jnp
        _gk = jax.random.key(seed)
        x = -0.0003713 + 1 * jax.random.normal(jax.random.fold_in(_gk, 1), (6250, 256), jnp.float32)
        _s = jax.random.randint(jax.random.fold_in(_gk, 2), (100000,), 0, 6250, jnp.int32)
        _d = jax.random.randint(jax.random.fold_in(_gk, 3), (100000,), 0, 6250, jnp.int32)
        _loop = jnp.arange(6250, dtype=jnp.int32)
        src = jnp.concatenate([_s, _d, _loop])
        dst = jnp.concatenate([_d, _s, _loop])
        _o = jnp.argsort(dst, stable=True)
        src = src[_o]
        dst = dst[_o]
        return (x, src, dst)
    x, src, dst = _rec_inputs()

    def _L0_gnn_setup():
        import jax, jax.numpy as jnp
        import numpy as np
        N = 6250
        E = 100000
        H = 8
        CPH = 16
        IN = 256
        OUT = 256
        NEG = 0.2
        EPS = 1e-05

        def _gat_conv(x, W, att_src, att_dst, bias, src, dst):
            xw = (x @ W).reshape(N, H, CPH)
            a_s = jnp.einsum('nhc,hc->nh', xw, att_src)
            a_d = jnp.einsum('nhc,hc->nh', xw, att_dst)
            loop = jnp.arange(N)
            src = jnp.concatenate([src, loop])
            dst = jnp.concatenate([dst, loop])
            e = jax.nn.leaky_relu(a_s[src] + a_d[dst], NEG)
            m = jax.ops.segment_max(e, dst, num_segments=N)
            p = jnp.exp(e - m[dst])
            s = jax.ops.segment_sum(p, dst, num_segments=N)
            alpha = p / s[dst]
            out = jax.ops.segment_sum(xw[src] * alpha[:, :, None], dst, num_segments=N)
            return out.reshape(N, H * CPH) + bias
        key = jax.random.key(seed)
        ks = jax.random.split(key, 12)
        x = jax.random.normal(ks[0], (N, IN), dtype=jnp.float32)
        row = jax.random.randint(ks[1], (E,), 0, N)
        off = jax.random.randint(ks[2], (E,), 1, N)
        col = (row + off) % N
        edge_index = jnp.stack([row, col], axis=0).astype(jnp.int64)
        g = 1.0 / np.sqrt(IN)

        def gat_params(k):
            k1, k2, k3 = jax.random.split(k, 3)
            W = jax.random.normal(k1, (IN, H * CPH), dtype=jnp.float32) * g
            a_s = jax.random.normal(k2, (H, CPH), dtype=jnp.float32) * 0.1
            a_d = jax.random.normal(k3, (H, CPH), dtype=jnp.float32) * 0.1
            b = jnp.zeros((H * CPH,), dtype=jnp.float32)
            return (W, a_s, a_d, b)
        W0, as0, ad0, b0 = gat_params(ks[3])
        W1, as1, ad1, b1 = gat_params(ks[4])
        gamma = jnp.ones((OUT,), dtype=jnp.float32)
        beta = jnp.zeros((OUT,), dtype=jnp.float32)
        return {'x': x, 'edge_index': edge_index, 'W0': W0, 'as0': as0, 'ad0': ad0, 'b0': b0, 'W1': W1, 'as1': as1, 'ad1': ad1, 'b1': b1, 'gamma': gamma, 'beta': beta}
    _L0_gnn_all = _L0_gnn_setup()
    _L0_gnn_in = {k: v for k, v in _L0_gnn_all.items() if k in ('W0', 'as0', 'ad0', 'b0', 'W1', 'as1', 'ad1', 'b1', 'gamma', 'beta')}
    del _L0_gnn_all

    def _L0_ffn_setup():
        import jax, jax.numpy as jnp
        import numpy as np
        TOP_K = 2
        key = jax.random.key(seed)
        ks = jax.random.split(key, 4)
        B, L, D, H, E = (8, 512, 256, 1024, 8)
        s = 0.02
        return {'x': jax.random.normal(ks[0], (B, L, D), jnp.float32), 'Wg': jax.random.normal(ks[1], (D, E), jnp.float32) * s, 'bg': jnp.zeros((E,), jnp.float32), 'W1': jax.random.normal(ks[2], (E, D, H), jnp.float32) * s, 'b1': jnp.zeros((E, H), jnp.float32), 'W2': jax.random.normal(ks[3], (E, H, D), jnp.float32) * s, 'b2': jnp.zeros((E, D), jnp.float32)}
    _L0_ffn_all = _L0_ffn_setup()
    _L0_ffn_in = {k: v for k, v in _L0_ffn_all.items() if k in ('Wg', 'bg', 'W1', 'b1', 'W2', 'b2')}
    del _L0_ffn_all
    return {'x': x, 'src': src, 'dst': dst, 'L0_gnn_W0': _L0_gnn_in['W0'], 'L0_gnn_as0': _L0_gnn_in['as0'], 'L0_gnn_ad0': _L0_gnn_in['ad0'], 'L0_gnn_b0': _L0_gnn_in['b0'], 'L0_gnn_W1': _L0_gnn_in['W1'], 'L0_gnn_as1': _L0_gnn_in['as1'], 'L0_gnn_ad1': _L0_gnn_in['ad1'], 'L0_gnn_b1': _L0_gnn_in['b1'], 'L0_gnn_gamma': _L0_gnn_in['gamma'], 'L0_gnn_beta': _L0_gnn_in['beta'], 'L0_ffn_Wg': _L0_ffn_in['Wg'], 'L0_ffn_bg': _L0_ffn_in['bg'], 'L0_ffn_W1': _L0_ffn_in['W1'], 'L0_ffn_b1': _L0_ffn_in['b1'], 'L0_ffn_W2': _L0_ffn_in['W2'], 'L0_ffn_b2': _L0_ffn_in['b2']}

def reference(x, src, dst, L0_gnn_W0, L0_gnn_as0, L0_gnn_ad0, L0_gnn_b0, L0_gnn_W1, L0_gnn_as1, L0_gnn_ad1, L0_gnn_b1, L0_gnn_gamma, L0_gnn_beta, L0_ffn_Wg, L0_ffn_bg, L0_ffn_W1, L0_ffn_b1, L0_ffn_W2, L0_ffn_b2):
    import jax
    import jax.numpy as jnp

    def _L0_gnn_ref(x, edge_index, W0, as0, ad0, b0, W1, as1, ad1, b1, gamma, beta):
        import jax, jax.numpy as jnp
        import numpy as np
        N = 6250
        E = 100000
        H = 8
        CPH = 16
        IN = 256
        OUT = 256
        NEG = 0.2
        EPS = 1e-05

        def _gat_conv(x, W, att_src, att_dst, bias, src, dst):
            xw = (x @ W).reshape(N, H, CPH)
            a_s = jnp.einsum('nhc,hc->nh', xw, att_src)
            a_d = jnp.einsum('nhc,hc->nh', xw, att_dst)
            loop = jnp.arange(N)
            src = jnp.concatenate([src, loop])
            dst = jnp.concatenate([dst, loop])
            e = jax.nn.leaky_relu(a_s[src] + a_d[dst], NEG)
            m = jax.ops.segment_max(e, dst, num_segments=N)
            p = jnp.exp(e - m[dst])
            s = jax.ops.segment_sum(p, dst, num_segments=N)
            alpha = p / s[dst]
            out = jax.ops.segment_sum(xw[src] * alpha[:, :, None], dst, num_segments=N)
            return out.reshape(N, H * CPH) + bias
        row, col = (edge_index[0], edge_index[1])
        h0 = _gat_conv(x, W0, as0, ad0, b0, row, col)
        nr, nc = (row[col], col[col])
        loop = jnp.arange(N)
        nr = jnp.concatenate([nr, loop])
        nc = jnp.concatenate([nc, loop])
        h1 = _gat_conv(x, W1, as1, ad1, b1, nr, nc)
        out = jnp.concatenate([h0, h1], axis=-1)
        out = out + x
        mu = out.mean(-1, keepdims=True)
        var = out.var(-1, keepdims=True)
        return (out - mu) / jnp.sqrt(var + EPS) * gamma + beta

    def _L0_ffn_ref(x, Wg, bg, W1, b1, W2, b2):
        import jax, jax.numpy as jnp
        import numpy as np
        TOP_K = 2
        B, L, D = x.shape
        E = W1.shape[0]
        xf = x.reshape(-1, D)
        gate_logits = xf @ Wg + bg
        top_w, top_i = jax.lax.top_k(gate_logits, TOP_K)
        top_w = jax.nn.softmax(top_w, axis=-1)
        w_dense = jnp.sum(jax.nn.one_hot(top_i, E, dtype=xf.dtype) * top_w[..., None], axis=1)
        out = jnp.zeros_like(xf)
        for e in range(E):
            h = jax.nn.gelu(xf @ W1[e] + b1[e], approximate=False)
            out = out + w_dense[:, e:e + 1] * (h @ W2[e] + b2[e])
        return out.reshape(B, L, D)
    edge_index = jnp.stack([src, dst])
    x = x + _L0_gnn_ref(_layernorm(x, axis=-1), edge_index, L0_gnn_W0, L0_gnn_as0, L0_gnn_ad0, L0_gnn_b0, L0_gnn_W1, L0_gnn_as1, L0_gnn_ad1, L0_gnn_b1, L0_gnn_gamma, L0_gnn_beta)
    x = x + _L0_ffn_ref(_layernorm(x, axis=-1)[None], L0_ffn_Wg, L0_ffn_bg, L0_ffn_W1, L0_ffn_b1, L0_ffn_W2, L0_ffn_b2)[0]
    return x

_drawn_inputs = setup_inputs


def setup_inputs(seed=0):
    import zlib

    import numpy as np

    out = dict(_drawn_inputs(seed))
    spreads = {'L0_gnn_b0': (0.0, 0.1),
     'L0_gnn_b1': (0.0, 0.1),
     'L0_gnn_gamma': (1.0, 0.2),
     'L0_gnn_beta': (0.0, 0.1),
     'L0_ffn_bg': (0.0, 0.301),
     'L0_ffn_b1': (0.0, 0.575),
     'L0_ffn_b2': (0.0, 0.1)}
    factors = {'L0_gnn_ad0': 5.261, 'L0_gnn_as1': 8.0, 'L0_gnn_ad1': 8.0}
    for name, (base, spread) in spreads.items():
        noise = np.random.default_rng([zlib.crc32(name.encode()), seed]).standard_normal(out[name].shape)
        drawn = base * np.exp(spread * noise) if base else spread * noise
        out[name] = jnp.asarray(drawn.astype(out[name].dtype))
    for name, factor in factors.items():
        out[name] = (out[name] * factor).astype(out[name].dtype)
    return out
```

```python
from contextlib import ExitStack

import numpy as np
import concourse.bass as bass
from concourse import mybir

F32 = mybir.dt.float32
I32 = mybir.dt.int32
ALU = mybir.AluOpType
ACT = mybir.ActivationFunctionType
AX = mybir.AxisListType

P = 128
N = 6250
D = 256
NT = -(-N // P)
NP = NT * P
TAIL = N - (NT - 1) * P
E = 206250
HD = 8
CH = 16
F = HD * CH
C = -(-E // P)
EP = C * P
J = 62
NB = C // J
J1 = NP // P
ROWT = F + HD
ROWS = F + 2 * HD
BLK = 512
NBLK = EP // BLK
BIG = 1e30
NEX = 8
HID = 1024
KD = D // P
MH = HID // P
SLOTS = 2 * (-(-(2 * N + NEX * (P - 1)) // (2 * P)))
SKIP = 1 << 20
EPS = 1e-5
GRP = 7
NG = NT // GRP
GW = 2 * J * ROWS
AW = 37904
MAGIC = 12582912.0

assert NB * J == C and NBLK * BLK == EP and NG * GRP == NT and NB % 2 == 0 and J1 <= J


def bc(ap, shape):
    return ap.to_broadcast(shape)


def build(nc, x, src, dst, W0, as0, ad0, b0, W1, as1, ad1, b1, gamma, beta, Wg, bg, eW1, eb1, eW2, eb2, out):
    ctx = ExitStack()
    with ctx:
        def sb(name, shape, dt=F32):
            return ctx.enter_context(nc.sbuf_tensor(name, shape, dt))

        def sem(name):
            return ctx.enter_context(nc.semaphore(name))

        def dram(name, shape, dt=F32):
            return nc.dram_tensor(name, shape, dt, kind="Internal").ap()

        tab = [dram("tab0", [NP, ROWT]), dram("tab1", [NP, ROWT])]
        adt = [dram("adt0", [NP, HD]), dram("adt1", [NP, HD])]
        srcp = dram("srcp", [P, C], I32)
        dstp = dram("dstp", [P, C])
        adstart = dram("adstart", [EP, HD])
        state = [dram("state0", [EP, ROWS]), dram("state1", [NP, ROWS])]
        degd = dram("degd", [NP, 1])
        x1d = dram("x1d", [NP, D])
        placed = dram("placed", [(SLOTS + 2) * P, D])
        answered = dram("answered", [SLOTS * P, D])
        states0 = state[0].rearrange("(p j) r -> p (j r)", p=P)
        adstart_c = adstart.rearrange("(p j) r -> p (j r)", p=P)

        AR = sb("AR", [P, AW])
        G = [AR[:, s * J * ROWS:(s + 1) * J * ROWS].rearrange("p (j r) -> p j r", r=ROWS) for s in range(2)]
        X = AR[:, GW:GW + NT * D].rearrange("p (t d) -> p t d", d=D)
        FB = GW + NT * D
        zero = sb("zero", [P, 1024])
        ident = sb("ident", [P, P])
        ones = sb("ones", [P, P])
        shf = sb("shf", [P, P])
        wrap = sb("wrap", [P, P])
        tri = sb("tri", [P, P])
        pidx = sb("pidx", [P, 1])
        pcol = sb("pcol", [P, 1])
        nid = sb("nid", [P, NT])
        e8 = sb("e8", [P, HD])
        b01 = sb("b01", [P, D])
        gam = sb("gam", [P, D])
        bet = sb("bet", [P, D])
        wg = sb("wg", [P, KD, NEX])
        bgb = sb("bgb", [P, NEX])
        eb1T = sb("eb1T", [P, NEX, MH])
        eb2b = sb("eb2b", [P, NEX, D])
        mv = sb("mv", [P, NT, 2])
        rstd = sb("rstd", [P, NT])
        nmr = sb("nmr", [P, NT])
        hrow = sb("hrow", [P, 2, D])
        hT = sb("hT", [P, 2, D])
        row = sb("row", [P, 2, 288])
        asr = sb("asr", [P, NT, 16])
        adr = sb("adr", [P, NT, 16])
        same1 = sb("same1", [P, J1])
        ends = sb("ends", [P, 8])
        idx = sb("idx", [P, 2, J], I32)
        neg = sb("neg", [P, J])
        carry = sb("carry", [P, ROWS])
        adc = sb("adc", [P, HD])
        adf = sb("adf", [P, HD])
        idx1 = sb("idx1", [P, 2, J1], I32)
        dst1 = sb("dst1", [P, J1])
        deg1 = sb("deg1", [P, J1])
        dneg = sb("dneg", [P, J1])
        ifirst = sb("ifirst", [P, 1], I32)
        cnt = sb("cnt", [P, 8, NT])
        icnt = sb("icnt", [P, 8, NT], I32)
        At = sb("At", [P, 2, ROWS])
        blk = sb("blk", [1, NBLK])
        sml = sb("sml", [P, 16])
        reg = sb("reg", [1, SLOTS], I32)
        bcur = sb("bcur", [P, MH])

        ps = [ctx.enter_context(nc.psum_tensor(f"ps{i}", [P, 512], F32)) for i in range(8)]

        s_hold = [sem(f"s_hold{i}") for i in range(5)]
        s_const = sem("s_const")
        s_clear = sem("s_clear")
        s_x = sem("s_x")
        s_w = sem("s_w")
        s_edge = sem("s_edge")
        s_par = sem("s_par")
        s_zero = sem("s_zero")
        s_wc = sem("s_wc")
        s_var = sem("s_var")
        s_std = sem("s_std")
        s_h = sem("s_h")
        s_tr = sem("s_tr")
        s_ht = sem("s_ht")
        s_xw = sem("s_xw")
        s_row = sem("s_row")
        s_res = sem("s_res")
        s_tab = [sem("s_tab0"), sem("s_tab1")]
        s_adt = sem("s_adt")
        s_dstf = sem("s_dstf")
        s_dstd = sem("s_dstd")
        s_blks = sem("s_blks")
        s_blkp = sem("s_blkp")
        s_bidx = sem("s_bidx")
        s_blk = [sem(f"s_blk{i}") for i in range(7)]
        s_blkc = sem("s_blkc")
        s_cnt = sem("s_cnt")
        s_cntp = sem("s_cntp")
        s_start = sem("s_start")
        s_scat = sem("s_scat")
        s_adf = sem("s_adf")
        s_adm = sem("s_adm")
        s_degd = sem("s_degd")
        s_deg1 = sem("s_deg1")
        s_g1 = sem("s_g1")
        s_c1 = sem("s_c1")
        s_e1 = sem("s_e1")
        s_d1 = sem("s_d1")
        s_st1 = sem("s_st1")
        s_idx = [sem("s_idxa"), sem("s_idxb")]
        s_ad = [sem("s_ada"), sem("s_adb")]
        s_g = [sem("s_ga"), sem("s_gb")]
        s_st = [sem("s_sta"), sem("s_stb")]
        s_dif = sem("s_dif")
        s_exp = sem("s_exp")
        s_done = sem("s_done")
        s_link = sem("s_link")
        s_rep = sem("s_rep")
        s_linkp = sem("s_linkp")
        s_cp = sem("s_cp")
        s_cps = sem("s_cps")
        s_cdif = sem("s_cdif")
        s_cexp = sem("s_cexp")
        s_cs = sem("s_cs")
        s_cb = sem("s_cb")
        s_A = sem("s_A")
        s_fidx = sem("s_fidx")
        s_fg = [sem("s_fga"), sem("s_fgb")]
        s_fx = [sem("s_fxa"), sem("s_fxb")]
        s_oh = sem("s_oh")
        s_ohs = sem("s_ohs")
        s_cg = sem("s_cg")
        s_cgs = sem("s_cgs")
        s_fe = sem("s_fe")
        s_fexp = sem("s_fexp")
        s_fs = sem("s_fs")
        s_fsq = sem("s_fsq")
        s_fgrp = sem("s_fgrp")
        s_x1 = sem("s_x1")
        s_xnT = sem("s_xnT")
        s_xnc = sem("s_xnc")
        s_lg = sem("s_lg")
        s_lgc = sem("s_lgc")
        s_m2 = sem("s_m2")
        s_m2e = sem("s_m2e")
        s_mask = sem("s_mask")
        s_rank = sem("s_rank")
        s_pos = sem("s_pos")
        s_place = sem("s_place")
        s_ew = sem("s_ew")
        s_xs = [sem("s_xsa"), sem("s_xsb")]
        s_tx = sem("s_tx")
        s_xt = sem("s_xt")
        s_m1 = sem("s_m1")
        s_hc = sem("s_hc")
        s_th = sem("s_th")
        s_bc = sem("s_bc")
        s_gl = sem("s_gl")
        s_mm2 = sem("s_mm2")
        s_y = sem("s_y")
        s_yo = [sem("s_yoa"), sem("s_yob")]
        s_ans = [sem("s_ansa"), sem("s_ansb")]
        s_x1l = [sem("s_x1la"), sem("s_x1lb")]
        s_fin = sem("s_fin")
        s_out = sem("s_out")

        def hold(eng, which, s, value):
            eng.wait_ge(s, value)
            if not isinstance(value, int):
                eng.sem_inc(s_hold[which], 1)

        V = nc.vector
        srcI = AR[:, 0:C].bitcast(I32)
        dstI = AR[:, C:2 * C].bitcast(I32)
        dstF = AR[:, 2 * C:3 * C]
        blkrow = [AR[:, J * ROWS + i * BLK:J * ROWS + (i + 1) * BLK] for i in range(7)]
        scr = AR[:, FB:FB + 1024]
        def cut(a, n):
            return AR[:, FB + a:FB + a + n]

        adin = cut(2048, 2 * J * HD).rearrange("p (s j) -> p s j", s=2)
        adx = cut(3040, J * HD).rearrange("p (j h) -> p j h", h=HD)
        Z = cut(3536, J * HD).rearrange("p (j h) -> p j h", h=HD)
        DW = cut(4032, 2 * J * HD).rearrange("p (k j h) -> p k j h", k=2, h=HD)
        att = cut(5024, 4 * F).rearrange("p (k f) -> p k f", k=4)
        same = cut(5600, C)
        Wc = AR[:, J * ROWS + 4000:J * ROWS + 4576].rearrange("p (k f) -> p k f", k=KD)
        ln = AR[:, J * ROWS + 4600:J * ROWS + 4600 + 6 * NT].rearrange("p (t s) -> p t s", s=6)
        rk = cut(0, 4 * NT * NEX).rearrange("p (k t e) -> p k t e", k=4, e=NEX)
        oneh = cut(1568, 2 * NT * NEX).rearrange("p (k t e) -> p k t e", k=2, e=NEX)
        tix = cut(2352, NT * 8).bitcast(mybir.dt.uint32).rearrange("p (t e) -> p t e", e=8)
        top = cut(2744, NT * 8).rearrange("p (t e) -> p t e", e=8)
        last1 = cut(1152, ROWS)
        rep = cut(1300, 4 * F).rearrange("p (k q f) -> p k q f", k=2, q=2)
        cT = AR[:, FB:FB + 512].rearrange("p (k e) -> p k e", k=4)
        cD = AR[:, FB + 512:FB + 768].rearrange("p (k e) -> p k e", k=2)
        cS = AR[:, FB + 768:FB + 1152].rearrange("p (k e) -> p k e", k=3)
        XN = AR[:, 0:NT * D].rearrange("p (t d) -> p t d", d=D)
        at = NT * D
        stg = AR[:, at:at + 4 * GRP * ROWS].rearrange("p (s k t r) -> p s k t r", s=2, k=2, r=ROWS)
        at += 4 * GRP * ROWS
        assert at <= GW
        at = FB
        cgr = AR[:, at:at + 2 * GRP * ROWS].rearrange("p (k t r) -> p k t r", k=2, r=ROWS)
        at += 2 * GRP * ROWS
        xwg = AR[:, at:at + 2 * GRP * ROWT].rearrange("p (k t r) -> p k t r", k=2, r=ROWT)
        at += 2 * GRP * ROWT
        og = AR[:, at:at + GRP * D].rearrange("p (t d) -> p t d", d=D)
        at += GRP * D
        tg = AR[:, at:at + GRP * D].rearrange("p (t d) -> p t d", d=D)
        at += GRP * D
        assert at <= AW, at
        fz = sb("fz", [P, 6, 2, GRP, HD])
        oh = sb("oh", [P, 2, P])
        zs = sb("zs", [P, NT, 16])
        fln = sb("fln", [P, GRP, 6])
        fmv = sb("fmv", [P, GRP, 2])
        frs = sb("frs", [P, 3, GRP])
        lgt = sb("lgt", [P, NT, NEX])
        wts = sb("wts", [P, 3, NT])
        pos = sb("pos", [P, 2, NT])
        ipos = sb("ipos", [P, 2, NT], I32)
        bare = sb("bare", [P, 2, 2, NT])
        toff = sb("toff", [P, 4, NEX])
        tile_e = sb("tile_e", [P, 2, SLOTS])
        slot_id = sb("slot_id", [P, SLOTS])
        w1s = AR[:, 0:NEX * KD * HID].rearrange("p (e k h) -> p e k h", e=NEX, k=KD)
        w2s = AR[:, NEX * KD * HID:2 * NEX * KD * HID].rearrange("p (e m d) -> p e m d", e=NEX, m=MH)
        at = 2 * NEX * KD * HID
        xs = AR[:, at:at + 2 * D].rearrange("p (s d) -> p s d", s=2)
        at += 2 * D
        xsT = AR[:, at:at + 2 * D].rearrange("p (s k t) -> p s k t", s=2, k=KD)
        at += 2 * D
        hs = AR[:, at:at + HID]
        at += HID
        hsT = AR[:, at:at + HID].rearrange("p (m t) -> p m t", m=MH)
        at += HID
        ys = AR[:, at:at + 2 * D].rearrange("p (s d) -> p s d", s=2)
        at += 2 * D
        assert at <= AW
        ansb = AR[:, 0:4 * GRP * D].rearrange("p (s k t d) -> p s k t d", s=2, k=2, d=D)
        x1b = AR[:, 4 * GRP * D:6 * GRP * D].rearrange("p (s t d) -> p s t d", s=2, d=D)

        block = ctx.enter_context(nc.Block())

        @block.sync
        def _(sp):
            with nc.allow_non_contiguous_dma(reason="small tables, once"):
                sp.wait_ge(s_clear, 1)
                sp.dma_start(dstI[0:P - 1, :], dst[0:(P - 1) * C].rearrange("(p j) -> p j", j=C)).then_inc(s_edge, 16)
                sp.dma_start(dstI[P - 1:P, 0:E - (P - 1) * C], dst[(P - 1) * C:E].rearrange("(a j) -> a j", a=1)).then_inc(s_edge, 16)
                for g in range(NG):
                    full = min(GRP, NT - 1 - g * GRP)
                    sp.dma_start(X[:, g * GRP:g * GRP + full, :],
                                 x[g * GRP * P:(g * GRP + full) * P, :].rearrange("(t p) d -> p t d", p=P)).then_inc(s_x, 16)
                sp.dma_start(X[0:TAIL, NT - 1, :], x[(NT - 1) * P:N, :]).then_inc(s_x, 16)
                for k, w in enumerate((W0, W1)):
                    sp.dma_start(Wc[:, :, ROWT * k:ROWT * k + F], w.rearrange("(k p) f -> p k f", p=P)).then_inc(s_w, 16)
                for k, a in enumerate((as0, as1, ad0, ad1)):
                    sp.dma_start(att[:, k, :], a.rearrange("h c -> (h c)").partition_broadcast(P)).then_inc(s_w, 16)
                sp.dma_start(srcI[0:P - 1, :], src[0:(P - 1) * C].rearrange("(p j) -> p j", j=C)).then_inc(s_edge, 16)
                sp.dma_start(srcI[P - 1:P, 0:E - (P - 1) * C], src[(P - 1) * C:E].rearrange("(a j) -> a j", a=1)).then_inc(s_edge, 16)
                sp.dma_start(idx1[:, 0, :], src[0:NP].rearrange("(p j) -> p j", j=J1)).then_inc(s_edge, 16)
                sp.dma_start(idx1[:, 1, :], dst[0:NP].rearrange("(p j) -> p j", j=J1)).then_inc(s_edge, 16)
                sp.wait_ge(s_const, 1)
                for k in range(4):
                    n = C * HD // 4
                    for a in range(0, n, 1024):
                        w = min(1024, n - a)
                        sp.dma_start(adstart_c[:, k * n + a:k * n + a + w], zero[:, 0:w]).then_inc(s_zero, 16)
                sp.wait_ge(s_edge, 96)
                sp.dma_start(srcp, srcI).then_inc(s_dstd, 16)
                sp.wait_ge(s_dstf, 1)
                sp.dma_start(dstp, dstF).then_inc(s_dstd, 16)
                sp.wait_ge(s_dstd, 32)
                sp.dma_start(blk[:, :], dstp.rearrange("p j -> (p j)").rearrange("(a b) -> a b", b=BLK)[:, 0:1].rearrange("a b -> b a")).then_inc(s_blks, 16)
                for dstt, v in ((b01[:, 0:F], b0), (b01[:, F:D], b1), (gam[:, :], gamma), (bet[:, :], beta), (bgb[:, :], bg)):
                    sp.dma_start(dstt, v.partition_broadcast(P)).then_inc(s_par, 16)
                sp.dma_start(wg[:, :, :], Wg.rearrange("(k p) e -> p k e", p=P)).then_inc(s_par, 16)
                sp.dma_start(eb2b[:, :, :], eb2.rearrange("e d -> (e d)").partition_broadcast(P)).then_inc(s_par, 16)
                for e in range(NEX):
                    sp.dma_start(eb1T[:, e, :], eb1[e].rearrange("(m p) -> p m", p=P)).then_inc(s_par, 16)
                for t in range(NT):
                    sp.wait_ge(s_row, t + 1)
                    for k in range(2):
                        sp.dma_start(tab[k][t * P:(t + 1) * P, :], row[:, t % 2, ROWT * k:ROWT * (k + 1)]).then_inc(s_tab[t % 2], 16)
                sp.wait_ge(s_res, NT)
                for k in range(2):
                    sp.dma_start(adt[k].rearrange("(t p) h -> p t h", p=P), adr[:, :, 8 * k:8 * k + 8]).then_inc(s_adt, 16)
                sp.wait_ge(s_start, 1)
                sp.dma_start(degd.rearrange("(t p) a -> p (t a)", p=P), cnt[:, 4, :]).then_inc(s_degd, 16)
                sp.wait_ge(s_degd, 16)
                sp.dma_start(deg1[:, :], degd.rearrange("(p j) a -> p (j a)", p=P)).then_inc(s_deg1, 16)
                sp.wait_ge(s_adf, 16)
                sp.wait_ge(s_scat, 16 * NT)
                sp.dma_start(adstart.rearrange("(p j) h -> p j h", p=P)[:, 0, :], adf[:, :]).then_inc(s_adm, 16)
                sp.wait_ge(s_d1, 1)
                sp.dma_start(state[1].rearrange("(p j) r -> p j r", p=P), G[0][:, 0:J1, :]).then_inc(s_st1, 16)
                sp.wait_ge(s_adm, 16)
                sp.wait_ge(s_st1, 16)
                sp.dma_start(idx[:, 0, :], srcp[:, 0:J]).then_inc(s_idx[0], 16)
                sp.dma_start(adin[:, 0, :], adstart_c[:, 0:J * HD]).then_inc(s_ad[0], 16)
                for r in range(0, SLOTS + 2, 4):
                    w = min(4, SLOTS + 2 - r)
                    sp.dma_start(placed[r * P:(r + w) * P, :].rearrange("(t p) d -> p (t d)", p=P) if w == 1 else
                                 placed[r * P:(r + w) * P, :].rearrange("(p t) d -> p (t d)", p=P), zero[:, 0:w * D]).then_inc(s_zero, 16)

                def fetch(s, b):
                    sp.dma_start(idx[:, s, :], srcp[:, bass.ds(b * J, J)]).then_inc(s_idx[s], 16)
                    sp.dma_start(adin[:, s, :], adstart_c[:, bass.ds(b * (J * HD), J * HD)]).then_inc(s_ad[s], 16)

                with sp.Fori(0, NB // 2 - 1) as i:
                    for s in range(2):
                        fetch(1 - s, i * 2 + (s + 1))
                        hold(sp, 0, s_done, i * 2 + (s + 1))
                        sp.dma_start(states0[:, bass.ds((i * 2 + s) * (J * ROWS), J * ROWS)], G[s].rearrange("p j r -> p (j r)")).then_inc(s_st[s], 16)
                sp.dma_start(idx[:, 1, :], srcp[:, (NB - 1) * J:]).then_inc(s_idx[1], 16)
                sp.dma_start(adin[:, 1, :], adstart_c[:, (NB - 1) * J * HD:]).then_inc(s_ad[1], 16)
                for s in range(2):
                    sp.wait_ge(s_done, NB - 1 + s)
                    sp.dma_start(states0[:, (NB - 2 + s) * J * ROWS:(NB - 1 + s) * J * ROWS], G[s].rearrange("p j r -> p (j r)")).then_inc(s_st[s], 16)
                for g in range(NG):
                    if g >= 1:
                        sp.wait_ge(s_fgrp, g)
                    else:
                        sp.wait_ge(s_A, 2)
                    for k in range(2):
                        sp.dma_start(xwg[:, k, :, :], tab[k][g * GRP * P:(g + 1) * GRP * P, :].rearrange("(t p) r -> p t r", p=P)).then_inc(s_fx[g % 2], 16)
                    sp.wait_ge(s_x1, g + 1)
                    sp.dma_start(x1d[g * GRP * P:(g + 1) * GRP * P, :].rearrange("(t p) d -> p t d", p=P), X[:, g * GRP:(g + 1) * GRP, :]).then_inc(s_st1, 16)
                sp.wait_ge(s_place, 32 * NT)
                sp.wait_ge(s_st1, 16 * (NG + 1))
                for e in range(NEX):
                    sp.dma_start(w1s[:, e, :, :], eW1[e].rearrange("(k p) h -> p k h", p=P)).then_inc(s_ew, 16)
                    sp.dma_start(w2s[:, e, :, :], eW2[e].rearrange("(m p) d -> p m d", p=P)).then_inc(s_ew, 16)
                for s in range(2):
                    sp.dma_start(xs[:, s, :], placed[s * P:(s + 1) * P, :]).then_inc(s_xs[s], 16)
                with sp.Fori(0, SLOTS // 2) as i:
                    for s in range(2):
                        hold(sp, 0, s_tx, i * 2 + (s + 1))
                        sp.dma_start(xs[:, s, :], placed[bass.ds((i * 2 + (s + 2)) * P, P), :]).then_inc(s_xs[s], 16)
                        hold(sp, 0, s_y, i * 2 + (s + 1))
                        sp.dma_start(answered[bass.ds((i * 2 + s) * P, P), :], ys[:, s, :]).then_inc(s_yo[s], 16)
                for s in range(2):
                    sp.wait_ge(s_yo[s], 16 * (SLOTS // 2))
                for g in range(NG):
                    if g >= 2:
                        sp.wait_ge(s_fin, g - 1)
                    sp.dma_start(x1b[:, g % 2, :, :], x1d[g * GRP * P:(g + 1) * GRP * P, :].rearrange("(t p) d -> p t d", p=P)).then_inc(s_x1l[g % 2], 16)
                    if g >= 1:
                        sp.wait_ge(s_fin, g)
                        sp.dma_start(out[(g - 1) * GRP * P:g * GRP * P, :].rearrange("(t p) d -> p t d", p=P), x1b[:, (g - 1) % 2, :, :]).then_inc(s_out, 16)
                        sp.wait_ge(s_out, 16 * g)
                g = NG - 1
                sp.wait_ge(s_fin, NG)
                sp.dma_start(out[g * GRP * P:(NT - 1) * P, :].rearrange("(t p) d -> p t d", p=P), x1b[:, g % 2, 0:GRP - 1, :]).then_inc(s_out, 16)
                sp.dma_start(out[(NT - 1) * P:N, :], x1b[0:TAIL, g % 2, GRP - 1, :]).then_inc(s_out, 16)
                sp.wait_ge(s_out, 16 * (NG + 1))

        @block.gpsimd
        def _(pool):
            g = nc.gpsimd
            g.memset(ones[:, :], 1.0)
            g.memset(ident[:, :], 0.0)
            g.memset(shf[:, :], 0.0)
            g.memset(wrap[:, :], 0.0)
            g.memset(zero[:, :], 0.0).then_inc(s_const, 1)
            pool.wait_ge(s_const, 1)
            g.affine_select(out=ident[:, :], in_=ident[:, :], compare_op=ALU.not_equal, fill=1.0, base=0, pattern=[[-1, P]], channel_multiplier=1)
            g.affine_select(out=shf[:, :], in_=shf[:, :], compare_op=ALU.not_equal, fill=1.0, base=1, pattern=[[-1, P]], channel_multiplier=1)
            g.affine_select(out=wrap[:, :], in_=wrap[:, :], compare_op=ALU.not_equal, fill=1.0, base=-(P - 1), pattern=[[-P, P]], channel_multiplier=1)
            g.affine_select(out=tri[:, :], in_=ones[:, :], compare_op=ALU.is_gt, fill=0.0, base=0, pattern=[[1, P]], channel_multiplier=-1)
            g.iota(pidx[:, :], pattern=[[0, 1]], base=0, channel_multiplier=1, allow_small_or_imprecise_dtypes=True)
            g.iota(nid[:, :], pattern=[[P, NT]], base=0, channel_multiplier=1, allow_small_or_imprecise_dtypes=True)
            g.iota(e8[:, :], pattern=[[1, HD]], base=0, channel_multiplier=0, allow_small_or_imprecise_dtypes=True)
            g.iota(slot_id[:, :], pattern=[[P, SLOTS]], base=0, channel_multiplier=0, allow_small_or_imprecise_dtypes=True).then_inc(s_const, 1)
            pool.wait_ge(s_bidx, 1)
            pool.wait_ge(s_dstd, 32)
            dblk = dstp.rearrange("p j -> (p j)").rearrange("(a b) -> a b", b=BLK)
            for t in range(NT):
                if t >= 7:
                    pool.wait_ge(s_blkc, t - 6)
                pool.indirect_dma_start(out=blkrow[t % 7], out_offset=None, in_=dblk,
                                        in_offset=bass.IndirectOffsetOnAxis(ap=icnt[:, 0, t:t + 1], axis=0)).then_inc(s_blk[t % 7], 16)
            pool.wait_ge(s_start, 1)
            pool.wait_ge(s_res, NT)
            pool.wait_ge(s_zero, 16 * 16)
            for t in range(NT):
                pool.indirect_dma_start(out=adstart, out_offset=bass.IndirectOffsetOnAxis(ap=icnt[:, 1, t:t + 1], axis=0),
                                        in_=adr[:, t, 0:8], in_offset=None, bounds_check=EP - 1, oob_is_err=False).then_inc(s_scat, 16)
            pool.wait_ge(s_adt, 32)
            pool.indirect_dma_start(out=adf[:, :], out_offset=None, in_=adt[0],
                                    in_offset=bass.IndirectOffsetOnAxis(ap=ifirst[:, :], axis=0)).then_inc(s_adf, 16)
            for q in range(2):
                pool.wait_ge(s_tab[q], 32 * ((NT + 1 - q) // 2))
            pool.wait_ge(s_edge, 96)
            pool.wait_ge(s_dstd, 32)
            for j in range(J1):
                pool.indirect_dma_start(out=G[0][:, j, 0:ROWT], out_offset=None, in_=tab[1],
                                        in_offset=bass.IndirectOffsetOnAxis(ap=idx1[:, 0, j:j + 1], axis=0)).then_inc(s_g1, 16)
                pool.indirect_dma_start(out=adin[:, 0, HD * j:HD * (j + 1)], out_offset=None, in_=adt[1],
                                        in_offset=bass.IndirectOffsetOnAxis(ap=idx1[:, 1, j:j + 1], axis=0)).then_inc(s_g1, 16)
            pool.wait_ge(s_blkc, NT)
            pool.wait_ge(s_st1, 16)

            def gather(s):
                for j in range(J):
                    pool.indirect_dma_start(out=G[s][:, j, 0:ROWT], out_offset=None, in_=tab[0],
                                            in_offset=bass.IndirectOffsetOnAxis(ap=idx[:, s, j:j + 1], axis=0)).then_inc(s_g[s], 16)

            for s in range(2):
                pool.wait_ge(s_idx[s], 16)
                gather(s)
            with pool.Fori(1, NB // 2) as i:
                for s in range(2):
                    hold(pool, 1, s_idx[s], i * 16 + 16)
                    hold(pool, 1, s_st[s], i * 16)
                    gather(s)
            pool.wait_ge(s_fidx, 1)
            for s in range(2):
                pool.wait_ge(s_st[s], 16 * (NB // 2))
            for g_ in range(NG):
                if g_ >= 2:
                    pool.wait_ge(s_fgrp, g_ - 1)
                for k in range(2):
                    for t in range(GRP):
                        pool.indirect_dma_start(out=stg[:, g_ % 2, k, t, :], out_offset=None, in_=state[k],
                                                in_offset=bass.IndirectOffsetOnAxis(ap=icnt[:, 2 + k, g_ * GRP + t:g_ * GRP + t + 1], axis=0)).then_inc(s_fg[g_ % 2], 16)
            pool.wait_ge(s_pos, 1)
            pool.wait_ge(s_zero, 16 * (16 + -(-(SLOTS + 2) // 4)))
            for t in range(NT):
                for k in range(2):
                    pool.indirect_dma_start(out=placed, out_offset=bass.IndirectOffsetOnAxis(ap=ipos[:, k, t:t + 1], axis=0),
                                            in_=XN[:, t, :], in_offset=None, bounds_check=(SLOTS + 2) * P - 1, oob_is_err=False).then_inc(s_place, 16)
            for s in range(2):
                pool.wait_ge(s_yo[s], 16 * (SLOTS // 2))
            for g_ in range(NG):
                if g_ >= 2:
                    pool.wait_ge(s_fin, g_ - 1)
                for k in range(2):
                    for t in range(GRP):
                        pool.indirect_dma_start(out=ansb[:, g_ % 2, k, t, :], out_offset=None, in_=answered,
                                                in_offset=bass.IndirectOffsetOnAxis(ap=icnt[:, 4 + k, g_ * GRP + t:g_ * GRP + t + 1], axis=0)).then_inc(s_ans[g_ % 2], 16)

        @block.scalar
        def _(act):
            S = nc.scalar
            act.wait_ge(s_var, 1)
            S.activation(rstd[:, :], mv[:, :, 1], ACT.Sqrt).then_inc(s_std, 1)
            for t in range(NT):
                act.wait_ge(s_tr, t + 1)
                if t >= 2:
                    act.wait_ge(s_xw, t - 1)
                S.copy(hT[:, t % 2, :], ps[t % 2][:, 0:D]).then_inc(s_ht, 1)
            act.wait_ge(s_c1, 1)
            S.activation(DW[:, :, 0:J1, :], DW[:, :, 0:J1, :], ACT.Exp).then_inc(s_e1, 1)
            with act.Fori(0, NB) as b:
                hold(act, 2, s_dif, b + 1)
                S.activation(DW[:, :, :, :], DW[:, :, :, :], ACT.Exp).then_inc(s_exp, 1)
            for k in range(2):
                act.wait_ge(s_cdif, k + 1)
                S.activation(cD[:, :, :], cD[:, :, :], ACT.Exp).then_inc(s_cexp, 1)
            for g in range(NG):
                for k in range(2):
                    for t in range(GRP):
                        n = (g * 2 + k) * GRP + t
                        act.wait_ge(s_cg, n + 1)
                        if n % (2 * GRP) == 0 and g >= 1:
                            act.wait_ge(s_fgrp, g)
                        S.copy(cgr[:, k, t, :], ps[4 + n % 2][:, 0:ROWS]).then_inc(s_cgs, 1)
                act.wait_ge(s_fe, g + 1)
                S.activation(fz[:, 0:3, :, :, :], fz[:, 0:3, :, :, :], ACT.Exp).then_inc(s_fexp, 1)
                for q in range(2):
                    act.wait_ge(s_fs, 2 * g + q + 1)
                    S.activation(frs[:, 0, :], fmv[:, :, 1], ACT.Sqrt).then_inc(s_fsq, 1)
                for t in range(GRP):
                    n = g * GRP + t
                    act.wait_ge(s_xnT, n + 1)
                    if n >= 2:
                        act.wait_ge(s_lg, n - 1)
                    S.copy(hT[:, n % 2, :], ps[n % 2][:, 0:D]).then_inc(s_xnc, 1)
            act.wait_ge(s_m2, 1)
            S.activation(wts[:, 0, :], wts[:, 0, :], ACT.Exp).then_inc(s_m2e, 1)
            def turned(s, value):
                if value is None:
                    act.wait_ge(s_tx, 1)
                else:
                    hold(act, 2, s_tx, value)
                S.copy(xsT[:, s, :, :], ps[4][:, 0:D].rearrange("p (k t) -> p k t", k=KD)).then_inc(s_xt, 1)

            turned(0, None)
            with act.Fori(0, SLOTS // 2) as i:
                for s in range(2):
                    turned(1 - s, i * 2 + (s + 2))
                    hold(act, 2, s_th, i * 2 + (s + 1))
                    hold(act, 2, s_bc, i * 2 + (s + 1))
                    for m in range(MH):
                        last = S.activation(hsT[:, m, :], ps[2 + m // 4][:, (m % 4) * P:(m % 4 + 1) * P], ACT.Gelu, bias=bcur[:, m:m + 1])
                    last.then_inc(s_gl, 1)

        @block.tensor
        def _(pe):
            T = nc.tensor
            pe.wait_ge(s_const, 2)
            pe.wait_ge(s_blks, 16)
            T.matmul(ps[6][:, 0:NBLK], ones[0:1, :], blk[:, :], start=True, stop=True).then_inc(s_blkp, 1)
            pe.wait_ge(s_wc, 1)

            def project(t):
                pe.wait_ge(s_ht, t + 1)
                if t >= 2:
                    pe.wait_ge(s_res, t - 1)
                for k in range(KD):
                    mm = T.matmul(ps[2 + t % 2][:, 0:288], hT[:, t % 2, k * P:(k + 1) * P], Wc[:, k, :], start=(k == 0), stop=(k == KD - 1))
                mm.then_inc(s_xw, 1)

            for t in range(NT):
                pe.wait_ge(s_h, t + 1)
                if t >= 2:
                    pe.wait_ge(s_ht, t - 1)
                for k in range(KD):
                    mm = T.transpose(ps[t % 2][:, k * P:(k + 1) * P], hrow[:, t % 2, k * P:(k + 1) * P], ident[:, :])
                mm.then_inc(s_tr, 1)
                if t >= 1:
                    project(t - 1)
            project(NT - 1)
            pe.wait_ge(s_cnt, 1)
            T.matmul(ps[7][:, 0:NT], shf[:, :], cnt[:, 2, :], start=True, stop=False)
            T.matmul(ps[7][:, 1:NT], wrap[:, :], cnt[:, 2, 0:NT - 1], start=False, stop=True).then_inc(s_cntp, 1)
            T.matmul(ps[6][:, 0:2], shf[:, :], ends[:, 0:2], start=True, stop=True).then_inc(s_linkp, 1)
            for k in range(2):
                if k == 0:
                    pe.wait_ge(s_rep, 1)
                    pe.wait_ge(s_link, 1)
                else:
                    pe.wait_ge(s_A, 1)
                last = carry if k == 0 else last1
                lk = sml[:, 8 + k:9 + k]
                T.matmul(ps[0][:, 0:P], bc(lk, [P, P]), ident[:, :], start=True, stop=True)
                T.matmul(ps[0][:, P:2 * P], rep[:, k, 1, :], ident[:, :], start=True, stop=True)
                T.matmul(ps[0][:, 2 * P:3 * P], rep[:, k, 0, :], ident[:, :], start=True, stop=True)
                T.matmul(ps[0][:, 3 * P:4 * P], last[:, 0:F], ident[:, :], start=True, stop=True).then_inc(s_cp, 1)
                pe.wait_ge(s_cs, k + 1)
                for q in range(3):
                    mm = T.transpose(ps[1][:, q * P:(q + 1) * P], cS[:, q, :], ident[:, :])
                mm.then_inc(s_cb, 1)
            pe.wait_ge(s_A, 2)
            for g in range(NG):
                for k in range(2):
                    for t in range(GRP):
                        n = (g * 2 + k) * GRP + t
                        if n >= 2:
                            pe.wait_ge(s_ohs, n - 1)
                        T.matmul(ps[2 + n % 2][:, 0:P], bc(cnt[:, 5 + k, g * GRP + t:g * GRP + t + 1], [P, P]), ident[:, :], start=True, stop=True).then_inc(s_oh, 1)
                        pe.wait_ge(s_ohs, n + 1)
                        if n >= 2:
                            pe.wait_ge(s_cgs, n - 1)
                        T.matmul(ps[4 + n % 2][:, 0:ROWS], oh[:, n % 2, :], At[:, k, :], start=True, stop=True).then_inc(s_cg, 1)
                pe.wait_ge(s_fgrp, g + 1)

                def logits(n):
                    pe.wait_ge(s_xnc, n + 1)
                    if n >= 2:
                        pe.wait_ge(s_lgc, n - 1)
                    for k in range(KD):
                        mm = T.matmul(ps[6 + n % 2][:, 0:NEX], hT[:, n % 2, k * P:(k + 1) * P], wg[:, k, :], start=(k == 0), stop=(k == KD - 1))
                    mm.then_inc(s_lg, 1)

                for t in range(GRP):
                    n = g * GRP + t
                    if n >= 2:
                        pe.wait_ge(s_xnc, n - 1)
                    for k in range(KD):
                        mm = T.transpose(ps[n % 2][:, k * P:(k + 1) * P], XN[:, n, k * P:(k + 1) * P], ident[:, :])
                    mm.then_inc(s_xnT, 1)
                    logits(n)
            pe.wait_ge(s_mask, 1)
            mk = rk[:, 0, :, :].rearrange("p t e -> p (t e)")
            T.matmul(ps[0][:, 0:NT * NEX], tri[:, :], mk, start=True, stop=True)
            T.matmul(ps[1][:, 0:NT * NEX], ones[:, :], mk, start=True, stop=True).then_inc(s_rank, 1)
            def turn(s):
                for k in range(KD):
                    mm = T.transpose(ps[4][:, k * P:(k + 1) * P], xs[:, s, k * P:(k + 1) * P], ident[:, :])
                mm.then_inc(s_tx, 1)

            def up(s, e):
                for h in range(2):
                    for k in range(KD):
                        mm = T.matmul(ps[h][:, :], xsT[:, s, k, :], AR[:, bass.ds(e * (KD * HID) + (k * HID + h * 512), 512)],
                                      start=(k == 0), stop=(k == KD - 1))
                mm.then_inc(s_m1, 1)

            def turn_hidden():
                for m in range(MH):
                    mm = T.transpose(ps[2 + m // 4][:, (m % 4) * P:(m % 4 + 1) * P], hs[:, m * P:(m + 1) * P], ident[:, :])
                mm.then_inc(s_th, 1)

            def down(s, e):
                for m in range(MH):
                    mm = T.matmul(ps[5][:, 0:D], hsT[:, m, :], AR[:, bass.ds(e * (MH * D) + (NEX * KD * HID + m * D), D)],
                                  start=(m == 0), stop=(m == MH - 1))
                mm.then_inc(s_mm2, 1)

            pe.wait_ge(s_ew, 32 * NEX)
            pe.wait_ge(s_pos, 2)
            pe.wait_ge(s_xs[0], 16)
            turn(0)
            pe.wait_ge(s_xt, 1)
            e0 = pe.value_load(reg[0:1, 0:1], min_val=0, max_val=NEX - 1)
            up(0, e0)
            pe.wait_ge(s_xs[1], 16)
            turn(1)

            def two_tiles(i):
                for s in range(2):
                    t = i * 2 + s
                    e = pe.value_load(reg[0:1, bass.ds(t, 1)], min_val=0, max_val=NEX - 1)
                    en = pe.value_load(reg[0:1, bass.ds(i * 2 + (s + 1), 1)], min_val=0, max_val=NEX - 1)
                    hold(pe, 3, s_hc, i * 2 + (s + 1))
                    turn_hidden()
                    hold(pe, 3, s_xt, i * 2 + (s + 2))
                    up(1 - s, en)
                    hold(pe, 3, s_xs[s], i * 16 + 32)
                    turn(s)
                    hold(pe, 3, s_gl, i * 2 + (s + 1))
                    if not (isinstance(t, int) and t == 0):
                        hold(pe, 3, s_y, t)
                    down(s, e)

            two_tiles(0)
            with pe.Fori(1, SLOTS // 2 - 1) as i:
                two_tiles(i)
            for s in range(2):
                t = SLOTS - 2 + s
                e = pe.value_load(reg[0:1, t:t + 1], min_val=0, max_val=NEX - 1)
                pe.wait_ge(s_hc, t + 1)
                turn_hidden()
                if s == 0:
                    en = pe.value_load(reg[0:1, t + 1:t + 2], min_val=0, max_val=NEX - 1)
                    pe.wait_ge(s_xt, t + 2)
                    up(1, en)
                    pe.wait_ge(s_xs[0], 16 * (SLOTS // 2 + 1))
                    turn(0)
                pe.wait_ge(s_gl, t + 1)
                pe.wait_ge(s_y, t)
                down(s, e)

        @block.vector
        def _(dve):
            dd = dve.drain
            V.memset(X[:, NT - 1, :], 0.0)
            V.memset(dstI[:, :], NP)
            V.memset(srcI[:, :], 0)
            V.memset(carry[:, :], 0.0)
            V.memset(adc[:, :], 0.0)
            V.memset(same[:, 0:1], 0.0)
            V.memset(same1[:, 0:1], 0.0)
            dd()
            V.memset(cnt[:, :, :], 0.0).then_inc(s_clear, 1)
            dve.wait_ge(s_edge, 32)
            dve.wait_ge(s_edge, 96)
            V.tensor_copy(dstF, dstI).then_inc(s_dstf, 1)
            V.tensor_copy(dst1[:, :], idx1[:, 1, :])
            dd()
            V.tensor_tensor(same[:, 1:C], dstF[:, 1:C], dstF[:, 0:C - 1], ALU.is_equal)
            V.tensor_tensor(same1[:, 1:J1], dst1[:, 1:J1], dst1[:, 0:J1 - 1], ALU.is_equal)
            for c, a in enumerate((dstF[:, C - 1:C], dst1[:, J1 - 1:J1], dstF[:, 0:1], dst1[:, 0:1])):
                V.tensor_scalar(ends[:, c:c + 1], a, 1.0, None, ALU.add)
            V.tensor_scalar(sml[:, 0:1], dstF[:, 0:1], float(NP - 1), None, ALU.min)
            dd()
            V.tensor_copy(ifirst[:, :], sml[:, 0:1])
            dve.wait_ge(s_w, 96)
            for c, (w, a) in enumerate(((0, 0), (1, 1), (0, 2), (1, 3))):
                to = (F, 2 * F + HD, 272, 280)[c]
                for k in range(KD):
                    dd()
                    V.tensor_tensor(scr[:, 0:F], Wc[:, k, ROWT * w:ROWT * w + F], att[:, a, :], ALU.mult)
                    dd()
                    V.tensor_reduce(Wc[:, k, to:to + HD], scr[:, 0:F].rearrange("p (h c) -> p h c", h=HD), AX.X, ALU.add)
            dd()
            dve.wait_ge(s_x, 16 * (NG + 1))
            for t in range(NT):
                V.bn_stats(ln[:, t, :], X[:, t, :])
            dd()
            for t in range(NT):
                V.bn_aggr(mv[:, t, :], ln[:, t, :])
            dd()
            V.tensor_scalar(mv[:, :, 1], mv[:, :, 1], EPS, None, ALU.add).then_inc(s_wc, 1)
            dd()
            V.tensor_scalar(sml[:, 1:2], mv[:, 0, 1:2], 0.0, None, ALU.add).then_inc(s_var, 1)
            dve.wait_ge(s_std, 1)
            V.reciprocal(rstd[:, :], rstd[:, :])
            dd()
            V.scalar_tensor_tensor(nmr[:, :], mv[:, :, 0], -1.0, rstd[:, :], ALU.mult, ALU.mult)
            dd()

            def keep(t):
                dve.wait_ge(s_xw, t + 1)
                if t >= 2:
                    dve.wait_ge(s_tab[t % 2], 32 * (t // 2))
                V.tensor_copy(row[:, t % 2, 0:272], ps[2 + t % 2][:, 0:272]).then_inc(s_row, 1)
                V.tensor_copy(asr[:, t, 0:8], ps[2 + t % 2][:, F:F + HD])
                V.tensor_copy(asr[:, t, 8:16], ps[2 + t % 2][:, 2 * F + HD:2 * F + 2 * HD])
                V.tensor_copy(adr[:, t, :], ps[2 + t % 2][:, 272:288]).then_inc(s_res, 1)

            for t in range(NT):
                if t >= 2:
                    dve.wait_ge(s_tr, t - 1)
                V.tensor_scalar(hrow[:, t % 2, :], X[:, t, :], rstd[:, t:t + 1], nmr[:, t:t + 1], ALU.mult, ALU.add).then_inc(s_h, 1)
                if t >= 2:
                    keep(t - 2)
            keep(NT - 2)
            keep(NT - 1)
            dve.wait_ge(s_blkp, 1)
            for t in range(NT):
                dd()
                V.tensor_scalar(scr[:, 0:NBLK], ps[6][:, 0:NBLK], nid[:, t:t + 1], None, ALU.is_le, ALU.add, accum_out=cnt[:, 0, t:t + 1])
            dd()
            V.tensor_scalar(cnt[:, 0, :], cnt[:, 0, :], -1.0, 0.0, ALU.add, ALU.max)
            dd()
            V.tensor_copy(icnt[:, 0, :], cnt[:, 0, :]).then_inc(s_bidx, 1)
            for t in range(NT):
                dve.wait_ge(s_blk[t % 7], 16 * (t // 7 + 1))
                V.tensor_scalar(blkrow[t % 7], blkrow[t % 7], nid[:, t:t + 1], None, ALU.is_le, ALU.add, accum_out=cnt[:, 1, t:t + 1]).then_inc(s_blkc, 1)
            dd()
            V.scalar_tensor_tensor(cnt[:, 2, :], cnt[:, 0, :], float(BLK), cnt[:, 1, :], ALU.mult, ALU.add).then_inc(s_cnt, 1)
            dve.wait_ge(s_cntp, 1)
            V.tensor_copy(cnt[:, 3, :], ps[7][:, 0:NT])
            dd()
            V.tensor_tensor(cnt[:, 4, :], cnt[:, 2, :], cnt[:, 3, :], ALU.subtract)
            dd()
            V.tensor_scalar(scr[:, 0:NT], cnt[:, 4, :], 0.0, float(SKIP), ALU.is_equal, ALU.mult)
            dd()
            V.tensor_tensor(scr[:, 0:NT], scr[:, 0:NT], cnt[:, 3, :], ALU.add)
            dd()
            V.tensor_copy(icnt[:, 1, :], scr[:, 0:NT]).then_inc(s_start, 1)
            dd()
            fin_ = scr[:, 64:64 + 8 * NT].rearrange("p (k t) -> p k t", k=8)
            for k in range(2):
                top_ = float(EP if k == 0 else N)
                cc = C if k == 0 else J1
                V.tensor_scalar(fin_[:, 0, :], cnt[:, 2, :], top_, None, ALU.min)
                V.tensor_scalar(fin_[:, 1, :], cnt[:, 3, :], top_, None, ALU.min)
                dd()
                V.tensor_tensor(fin_[:, 2, :], fin_[:, 0, :], fin_[:, 1, :], ALU.is_gt)
                V.tensor_scalar(fin_[:, 3, :], fin_[:, 0, :], -1.0, 0.0, ALU.add, ALU.max)
                dd()
                V.tensor_copy(icnt[:, 2 + k, :], fin_[:, 3, :])
                V.tensor_scalar(bare[:, k, 0, :], fin_[:, 2, :], -1.0, BIG, ALU.add, ALU.mult)
                V.tensor_scalar(fin_[:, 4, :], fin_[:, 3, :], 1.0 / cc, -0.5 + 0.5 / cc, ALU.mult, ALU.add)
                dd()
                V.tensor_scalar(fin_[:, 4, :], fin_[:, 4, :], MAGIC, None, ALU.add)
                dd()
                V.tensor_scalar(fin_[:, 4, :], fin_[:, 4, :], MAGIC, None, ALU.subtract)
                dd()
                V.tensor_scalar(fin_[:, 5, :], fin_[:, 4, :], float(cc), None, ALU.mult)
                dd()
                V.tensor_tensor(fin_[:, 5, :], fin_[:, 1, :], fin_[:, 5, :], ALU.is_lt)
                dd()
                V.tensor_tensor(fin_[:, 5, :], fin_[:, 5, :], fin_[:, 2, :], ALU.mult)
                dd()
                V.tensor_scalar(bare[:, k, 1, :], fin_[:, 5, :], -1.0, BIG, ALU.add, ALU.mult)
                V.tensor_tensor(fin_[:, 5, :], fin_[:, 5, :], fin_[:, 4, :], ALU.mult)
                dd()
                V.tensor_scalar(cnt[:, 5 + k, :], fin_[:, 5, :], -1.0, None, ALU.add)
                dd()
            dve.wait_ge(s_linkp, 1)
            V.tensor_tensor(sml[:, 2:4], ps[6][:, 0:2], ends[:, 2:4], ALU.is_equal)
            V.tensor_tensor(sml[:, 4:6], ends[:, 0:2], ends[:, 2:4], ALU.is_equal)
            dd()
            V.tensor_tensor(sml[:, 8:10], sml[:, 2:4], sml[:, 4:6], ALU.mult).then_inc(s_link, 1)
            V.tensor_tensor(zs[:, :, :], asr[:, :, :], adr[:, :, :], ALU.add)
            dd()
            V.scalar_tensor_tensor(zs[:, :, :], zs[:, :, :], 0.2, zs[:, :, :], ALU.mult, ALU.max)

            def scan_batch(Gs, n, smask, adv, b_exp, s_in, s_up, weight):
                z, r, w = Z[:, 0:n, :], DW[:, 0, 0:n, :], DW[:, 1, 0:n, :]
                ng = neg[:, 0:n]
                V.tensor_scalar(ng, smask, -1.0, BIG, ALU.add, ALU.mult)
                V.tensor_tensor(z, Gs[:, :, F:ROWT], adv, ALU.add)
                dd()
                V.scalar_tensor_tensor(z, z, 0.2, z, ALU.mult, ALU.max)
                dd()
                if weight is not None:
                    V.tensor_tensor(z, z, bc(dneg[:, 0:n].unsqueeze(2), [P, n, HD]), ALU.add)
                    dd()
                for h in range(HD):
                    V.tensor_tensor_scan(Gs[:, :, ROWT + h], ng, z[:, :, h], carry[:, ROWT + h:ROWT + h + 1], ALU.add, ALU.max)
                dd()
                m = Gs[:, :, ROWT:ROWS]
                V.tensor_tensor(r[:, 1:n, :], m[:, 0:n - 1, :], m[:, 1:n, :], ALU.subtract)
                V.tensor_tensor(r[:, 0, :], carry[:, ROWT:ROWS], m[:, 0, :], ALU.subtract)
                V.tensor_tensor(w, z, m, ALU.subtract)
                dd()
                V.tensor_tensor(r, r, bc(ng.unsqueeze(2), [P, n, HD]), ALU.add).then_inc(s_up, 1)
                b_exp()
                if weight is not None:
                    V.tensor_tensor(w, w, bc(weight.unsqueeze(2), [P, n, HD]), ALU.mult)
                    dd()
                V.tensor_tensor(Gs[:, :, 0:F].rearrange("p j (h c) -> p j h c", h=HD), Gs[:, :, 0:F].rearrange("p j (h c) -> p j h c", h=HD),
                                bc(w.unsqueeze(3), [P, n, HD, CH]), ALU.mult)
                for h in range(HD):
                    V.tensor_tensor_scan(Gs[:, :, F + h], r[:, :, h], w[:, :, h], carry[:, F + h:F + h + 1], ALU.mult, ALU.add)
                dd()
                for f in range(F):
                    V.tensor_tensor_scan(Gs[:, :, f], r[:, :, f // CH], Gs[:, :, f], carry[:, f:f + 1], ALU.mult, ALU.add)
                dd()

            dve.wait_ge(s_deg1, 16)
            V.tensor_scalar(dneg[:, :], deg1[:, :], 0.0, -BIG, ALU.is_equal, ALU.mult)
            dve.wait_ge(s_g1, 32 * J1)
            scan_batch(G[0][:, 0:J1, :], J1, same1[:, :], adin[:, 0, 0:J1 * HD].rearrange("p (j h) -> p j h", h=HD),
                       lambda: dve.wait_ge(s_e1, 1), None, s_c1, deg1[:, :])
            V.tensor_copy(last1, G[0][:, J1 - 1, :]).then_inc(s_d1, 1)

            with dve.Fori(0, NB // 2) as i:
                for s in range(2):
                    b = i * 2 + s
                    hold(dve, 4, s_ad[s], i * 16 + 16)
                    ain = adin[:, s, :].rearrange("p (j h) -> p j h", h=HD)
                    sm = same[:, bass.ds(b * J, J)]
                    V.tensor_copy(neg[:, :], sm)
                    dd()
                    for h in range(HD):
                        V.tensor_tensor_scan(adx[:, :, h], neg[:, :], ain[:, :, h], adc[:, h:h + 1], ALU.mult, ALU.add)
                    dd()
                    V.tensor_copy(adc[:, :], adx[:, J - 1, :])
                    hold(dve, 4, s_g[s], (i + 1) * (16 * J))
                    scan_batch(G[s], J, neg[:, :], adx[:, :, :], lambda: hold(dve, 4, s_exp, i * 2 + (s + 1)), None, s_dif, None)
                    V.tensor_copy(carry[:, :], G[s][:, J - 1, :]).then_inc(s_done, 1)
                    dd()

            for k, a in enumerate((carry, last1)):
                for q in range(2):
                    V.tensor_copy(rep[:, k, q, :].rearrange("p (h c) -> p h c", h=HD),
                                  bc(a[:, F + HD * q:F + HD * (q + 1)].unsqueeze(2), [P, HD, CH]))
            dd()
            V.memset(sml[:, 1:2], 0.0).then_inc(s_rep, 1)
            for k in range(2):
                dve.wait_ge(s_cp, k + 1)
                V.tensor_copy(cT.rearrange("p k e -> p (k e)"), ps[0][:, :])
                dd()
                V.tensor_scalar(cT[:, 0, :], cT[:, 0, :], -1.0, BIG, ALU.add, ALU.mult)
                dd()
                V.tensor_tensor_scan(cS[:, 0, :], cT[:, 0, :], cT[:, 1, :], 0.0, ALU.add, ALU.max)
                V.memset(cD[:, 0, 0:1], 0.0)
                dd()
                V.tensor_tensor(cD[:, 0, 1:P], cS[:, 0, 0:P - 1], cS[:, 0, 1:P], ALU.subtract)
                V.tensor_tensor(cD[:, 1, :], cT[:, 1, :], cS[:, 0, :], ALU.subtract)
                dd()
                V.tensor_tensor(cD[:, 0, :], cD[:, 0, :], cT[:, 0, :], ALU.add).then_inc(s_cdif, 1)
                dve.wait_ge(s_cexp, k + 1)
                for q in (2, 3):
                    V.tensor_tensor(cT[:, q, :], cT[:, q, :], cD[:, 1, :], ALU.mult)
                dd()
                V.tensor_tensor_scan(cS[:, 1, :], cD[:, 0, :], cT[:, 2, :], 0.0, ALU.mult, ALU.add)
                V.tensor_tensor_scan(cS[:, 2, :], cD[:, 0, :], cT[:, 3, :], 0.0, ALU.mult, ALU.add)
                dd()
                V.memset(sml[:, 1:2], 0.0).then_inc(s_cs, 1)
                dve.wait_ge(s_cb, k + 1)
                V.tensor_copy(At[:, k, 0:F], ps[1][:, 2 * P:3 * P])
                V.tensor_copy(At[:, k, F:ROWT], ps[1][:, P:2 * P].rearrange("p (h c) -> p h c", h=HD)[:, :, 0])
                V.tensor_copy(At[:, k, ROWT:ROWS], ps[1][:, 0:P].rearrange("p (h c) -> p h c", h=HD)[:, :, 0])
                dd()
                if k == 0:
                    V.tensor_copy(sml[:, 1:2], sml[:, 8:9]).then_inc(s_fidx, 1)
                V.tensor_copy(sml[:, 2:3], sml[:, 8:9]).then_inc(s_A, 1)
                dd()

            dve.wait_ge(s_par, 16 * (7 + NEX))

            def layer_stats(src_, g, q):
                for t in range(GRP):
                    V.bn_stats(fln[:, t, :], src_[:, t, :])
                dd()
                for t in range(GRP):
                    V.bn_aggr(fmv[:, t, :], fln[:, t, :])
                dd()
                V.tensor_scalar(fmv[:, :, 1], fmv[:, :, 1], EPS, None, ALU.add).then_inc(s_fs, 1)
                dve.wait_ge(s_fsq, 2 * g + q + 1)
                V.reciprocal(frs[:, 1, :], frs[:, 0, :])
                dd()
                V.scalar_tensor_tensor(frs[:, 2, :], fmv[:, :, 0], -1.0, frs[:, 1, :], ALU.mult, ALU.mult)
                dd()

            for g in range(NG):
                gt = slice(g * GRP, (g + 1) * GRP)
                for k in range(2):
                    for t in range(GRP):
                        n = (g * 2 + k) * GRP + t
                        dve.wait_ge(s_oh, n + 1)
                        if n >= 2:
                            dve.wait_ge(s_cg, n - 1)
                        V.tensor_scalar(oh[:, n % 2, :], ps[2 + n % 2][:, 0:P], pidx[:, 0:1], None, ALU.is_equal).then_inc(s_ohs, 1)
                dve.wait_ge(s_fg[g % 2], 16 * 2 * GRP * (g // 2 + 1))
                dve.wait_ge(s_cgs, 2 * GRP * (g + 1))
                dve.wait_ge(s_fx[g % 2], 32 * (g // 2 + 1))
                sg = stg[:, g % 2]
                for k in range(2):
                    zk = zs[:, gt, 8 * k:8 * k + 8]
                    for q, a in enumerate((sg[:, k, :, ROWT:ROWS], cgr[:, k, :, ROWT:ROWS])):
                        V.tensor_tensor(fz[:, q, k, :, :], a, bc(bare[:, k, q, gt].unsqueeze(2), [P, GRP, HD]), ALU.add)
                    dd()
                    V.tensor_tensor(fz[:, 3, k, :, :], fz[:, 0, k, :, :], fz[:, 1, k, :, :], ALU.max)
                    dd()
                    V.tensor_tensor(fz[:, 3, k, :, :], fz[:, 3, k, :, :], zk, ALU.max)
                    dd()
                    for q in range(2):
                        V.tensor_tensor(fz[:, q, k, :, :], fz[:, q, k, :, :], fz[:, 3, k, :, :], ALU.subtract)
                    V.tensor_tensor(fz[:, 2, k, :, :], zk, fz[:, 3, k, :, :], ALU.subtract)
                    dd()
                V.memset(sml[:, 3:4], 0.0).then_inc(s_fe, 1)
                dve.wait_ge(s_fexp, g + 1)
                V.tensor_scalar(fz[:, 2, 1, :, :], fz[:, 2, 1, :, :], 2.0, None, ALU.mult)
                dd()
                for k in range(2):
                    V.tensor_tensor(fz[:, 3, k, :, :], sg[:, k, :, F:ROWT], fz[:, 0, k, :, :], ALU.mult)
                    V.tensor_tensor(fz[:, 4, k, :, :], cgr[:, k, :, F:ROWT], fz[:, 1, k, :, :], ALU.mult)
                    dd()
                    V.tensor_tensor(fz[:, 3, k, :, :], fz[:, 3, k, :, :], fz[:, 4, k, :, :], ALU.add)
                    dd()
                    V.tensor_tensor(fz[:, 3, k, :, :], fz[:, 3, k, :, :], fz[:, 2, k, :, :], ALU.add)
                    dd()
                    V.reciprocal(fz[:, 4, k, :, :], fz[:, 3, k, :, :])
                    dd()
                    for q in range(3):
                        V.tensor_tensor(fz[:, q, k, :, :], fz[:, q, k, :, :], fz[:, 4, k, :, :], ALU.mult)
                dd()
                for k in range(2):
                    o = og[:, :, k * F:(k + 1) * F].rearrange("p t (h c) -> p t h c", h=HD)
                    for q, a in enumerate((sg[:, k, :, 0:F], cgr[:, k, :, 0:F], xwg[:, k, :, 0:F])):
                        to = o if q == 0 else tg[:, :, k * F:(k + 1) * F].rearrange("p t (h c) -> p t h c", h=HD)
                        V.tensor_tensor(to, a.rearrange("p t (h c) -> p t h c", h=HD), bc(fz[:, q, k, :, :].unsqueeze(3), [P, GRP, HD, CH]), ALU.mult)
                        dd()
                        if q:
                            V.tensor_tensor(o, o, to, ALU.add)
                            dd()
                V.tensor_tensor(og[:, :, :], og[:, :, :], bc(b01[:, :].unsqueeze(1), [P, GRP, D]), ALU.add)
                for t in range(GRP):
                    n = g * GRP + t
                    V.tensor_scalar(tg[:, t, :], X[:, n, :], rstd[:, n:n + 1], nmr[:, n:n + 1], ALU.mult, ALU.add)
                dd()
                V.tensor_tensor(og[:, :, :], og[:, :, :], tg[:, :, :], ALU.add)
                dd()
                layer_stats(og, g, 0)
                for t in range(GRP):
                    V.tensor_scalar(og[:, t, :], og[:, t, :], frs[:, 1, t:t + 1], frs[:, 2, t:t + 1], ALU.mult, ALU.add)
                dd()
                V.tensor_tensor(og[:, :, :], og[:, :, :], bc(gam[:, :].unsqueeze(1), [P, GRP, D]), ALU.mult)
                dd()
                V.tensor_tensor(og[:, :, :], og[:, :, :], bc(bet[:, :].unsqueeze(1), [P, GRP, D]), ALU.add)
                dd()
                V.tensor_tensor(X[:, gt, :], X[:, gt, :], og[:, :, :], ALU.add)
                dd()
                V.memset(sml[:, 4:5], 0.0).then_inc(s_x1, 1)
                layer_stats(X[:, gt, :], g, 1)
                for t in range(GRP):
                    V.tensor_scalar(XN[:, g * GRP + t, :], X[:, g * GRP + t, :], frs[:, 1, t:t + 1], frs[:, 2, t:t + 1], ALU.mult, ALU.add)
                dd()
                V.memset(sml[:, 5:6], 0.0).then_inc(s_fgrp, 1)
                for t in range(GRP):
                    n = g * GRP + t
                    dve.wait_ge(s_lg, n + 1)
                    V.tensor_tensor(lgt[:, n, :], ps[6 + n % 2][:, 0:NEX], bgb[:, :], ALU.add).then_inc(s_lgc, 1)
            dd()
            for t in range(NT):
                V.max(top[:, t, :], lgt[:, t, :])
            dd()
            for t in range(NT):
                V.max_index(tix[:, t, :], top[:, t, :], lgt[:, t, :])
            V.tensor_tensor(wts[:, 0, :], top[:, :, 1], top[:, :, 0], ALU.subtract)
            dd()
            V.memset(sml[:, 5:6], 0.0).then_inc(s_m2, 1)
            V.tensor_copy(pos[:, :, :], tix[:, :, 0:2].rearrange("p t k -> p k t"))
            dve.wait_ge(s_m2e, 1)
            V.tensor_scalar(wts[:, 1, :], wts[:, 0, :], 1.0, None, ALU.add)
            dd()
            V.reciprocal(wts[:, 1, :], wts[:, 1, :])
            dd()
            V.tensor_tensor(wts[:, 2, :], wts[:, 0, :], wts[:, 1, :], ALU.mult)
            for k in range(2):
                V.tensor_tensor(oneh[:, k, :, :], bc(pos[:, k, :].unsqueeze(2), [P, NT, NEX]), bc(e8[:, :].unsqueeze(1), [P, NT, NEX]), ALU.is_equal)
            dd()
            V.tensor_tensor(rk[:, 0, :, :], oneh[:, 0, :, :], oneh[:, 1, :, :], ALU.add)
            dd()
            V.tensor_scalar(pcol[:, :], pidx[:, :], float(TAIL), None, ALU.is_lt)
            dd()
            V.tensor_scalar(rk[:, 0, NT - 1, :], rk[:, 0, NT - 1, :], pcol[:, 0:1], None, ALU.mult)
            dd()
            V.memset(sml[:, 5:6], 0.0).then_inc(s_mask, 1)
            dve.wait_ge(s_rank, 1)
            V.tensor_copy(rk[:, 1, :, :].rearrange("p t e -> p (t e)"), ps[1][:, 0:NT * NEX])
            V.memset(toff[:, 3, :], 0.0)
            V.memset(rk[:, 2, 0, :], 0.0)
            dd()
            for e in range(NEX):
                V.tensor_tensor_scan(rk[:, 3, :, e], rk[:, 1, :, e], rk[:, 1, :, e], 0.0, ALU.add, ALU.bypass) if False else \
                    V.tensor_tensor_scan(rk[:, 3, :, e], bc(ones[:, 0:1], [P, NT]), rk[:, 1, :, e], 0.0, ALU.mult, ALU.add)
            dd()
            V.tensor_copy(rk[:, 2, 1:NT, :], rk[:, 3, 0:NT - 1, :])
            V.tensor_scalar(toff[:, 0, :], rk[:, 3, NT - 1, :], 1.0 / P, 0.5 - 0.5 / P, ALU.mult, ALU.add)
            dd()
            V.tensor_scalar(toff[:, 0, :], toff[:, 0, :], MAGIC, None, ALU.add)
            dd()
            V.tensor_scalar(toff[:, 0, :], toff[:, 0, :], MAGIC, None, ALU.subtract)
            dd()
            V.tensor_scalar(toff[:, 0, :], toff[:, 0, :], float(P), None, ALU.mult)
            dd()
            V.tensor_tensor_scan(toff[:, 1, :], bc(ones[:, 0:1], [P, NEX]), toff[:, 0, :], 0.0, ALU.mult, ALU.add)
            dd()
            V.tensor_tensor(toff[:, 2, :], toff[:, 1, :], toff[:, 0, :], ALU.subtract)
            V.tensor_tensor(rk[:, 2, :, :].rearrange("p t e -> p (t e)"), rk[:, 2, :, :].rearrange("p t e -> p (t e)"), ps[0][:, 0:NT * NEX], ALU.add)
            dd()
            V.tensor_tensor(rk[:, 2, :, :], rk[:, 2, :, :], bc(toff[:, 2, :].unsqueeze(1), [P, NT, NEX]), ALU.add)
            dd()
            for k in range(2):
                V.tensor_tensor(oneh[:, k, :, :], oneh[:, k, :, :], rk[:, 2, :, :], ALU.mult)
            dd()
            for k in range(2):
                V.tensor_reduce(pos[:, k, :], oneh[:, k, :, :], AX.X, ALU.add)
            dd()
            V.tensor_copy(icnt[:, 4:6, :], pos[:, :, :])
            V.tensor_scalar(pcol[:, :], pcol[:, :], -1.0, -float(SKIP), ALU.add, ALU.mult)
            dd()
            V.tensor_scalar(pos[:, :, NT - 1], pos[:, :, NT - 1], pcol[:, 0:1], None, ALU.add)
            dd()
            V.tensor_copy(ipos[:, :, :], pos[:, :, :]).then_inc(s_pos, 1)
            V.memset(tile_e[:, 0, :], 0.0)
            dd()
            for e in range(NEX - 1):
                V.tensor_scalar(tile_e[:, 1, :], slot_id[:, :], toff[:, 1, e:e + 1], None, ALU.is_ge)
                dd()
                V.tensor_tensor(tile_e[:, 0, :], tile_e[:, 0, :], tile_e[:, 1, :], ALU.add)
                dd()
            V.tensor_copy(reg[0:1, :], tile_e[0:1, 0, :]).then_inc(s_pos, 1)
            dd()

            def two_answers(i):
                for s in range(2):
                    t = i * 2 + s
                    e = dve.value_load(reg[0:1, bass.ds(t, 1)], min_val=0, max_val=NEX - 1)
                    if not (isinstance(t, int) and t == 0):
                        hold(dve, 4, s_gl, t)
                    V.tensor_copy(bcur[:, :], eb1T[:, bass.ds(e, 1), :].rearrange("p a m -> p (a m)")).then_inc(s_bc, 1)
                    hold(dve, 4, s_m1, i * 2 + (s + 1))
                    V.tensor_copy(hs[:, 0:512], ps[0][:, :])
                    V.tensor_copy(hs[:, 512:1024], ps[1][:, :]).then_inc(s_hc, 1)
                    hold(dve, 4, s_mm2, i * 2 + (s + 1))
                    if not isinstance(i, int):
                        hold(dve, 4, s_yo[s], i * 16)
                    V.tensor_tensor(ys[:, s, :], ps[5][:, 0:D], eb2b[:, bass.ds(e, 1), :].rearrange("p a d -> p (a d)"), ALU.add).then_inc(s_y, 1)

            two_answers(0)
            with dve.Fori(1, SLOTS // 2) as i:
                two_answers(i)

            for g in range(NG):
                dve.wait_ge(s_ans[g % 2], 16 * 2 * GRP * (g // 2 + 1))
                dve.wait_ge(s_x1l[g % 2], 16 * (g // 2 + 1))
                for k in range(2):
                    for t in range(GRP):
                        n = g * GRP + t
                        V.scalar_tensor_tensor(x1b[:, g % 2, t, :], ansb[:, g % 2, k, t, :], wts[:, 1 + k, n:n + 1], x1b[:, g % 2, t, :], ALU.mult, ALU.add)
                    dd()
                V.memset(sml[:, 5:6], 0.0).then_inc(s_fin, 1)


_INS = ["x", "src", "dst", "L0_gnn_W0", "L0_gnn_as0", "L0_gnn_ad0", "L0_gnn_b0", "L0_gnn_W1", "L0_gnn_as1", "L0_gnn_ad1",
        "L0_gnn_b1", "L0_gnn_gamma", "L0_gnn_beta", "L0_ffn_Wg", "L0_ffn_bg", "L0_ffn_W1", "L0_ffn_b1", "L0_ffn_W2", "L0_ffn_b2"]


def kernel(**inputs):
    import concourse.bacc as bacc
    from concourse.bass_utils import run_bass_kernel_spmd as run

    nc = bacc.Bacc("TRN2", target_bir_lowering=False, num_devices=1)
    arrays, args = {}, []
    for name in _INS:
        a = np.ascontiguousarray(inputs[name])
        arrays[f"in_{name}"] = a
        args.append(nc.dram_tensor(f"in_{name}", a.shape, mybir.dt.from_np(a.dtype), kind="ExternalInput").ap())
    args.append(nc.dram_tensor("out_0", (N, D), F32, kind="ExternalOutput").ap())
    build(nc, *args)
    r = run(nc, [arrays], core_ids=[0])
    return r.results[0]["out_0"]
```

```python
from contextlib import ExitStack

import numpy as np
import concourse.bass as bass
from concourse import mybir

F32 = mybir.dt.float32
I32 = mybir.dt.int32
ALU = mybir.AluOpType
ACT = mybir.ActivationFunctionType
AX = mybir.AxisListType

P = 128
N = 6250
D = 256
NT = -(-N // P)
NP = NT * P
TAIL = N - (NT - 1) * P
E = 206250
HD = 8
CH = 16
F = HD * CH
C = -(-E // P)
EP = C * P
J = 62
NB = C // J
J1 = NP // P
ROWT = F + HD
ROWS = F + 2 * HD
BLK = 512
NBLK = EP // BLK
BIG = 1e30
NEX = 8
HID = 1024
KD = D // P
MH = HID // P
SLOTS = 2 * (-(-(2 * N + NEX * (P - 1)) // (2 * P)))
SKIP = 1 << 20
EPS = 1e-5
GRP = 7
NG = NT // GRP
GW = 2 * J * ROWS
REG = NP + P
ROWP = D + 2
AW = 37904
MAGIC = 12582912.0

assert NB * J == C and NBLK * BLK == EP and NG * GRP == NT and NB % 2 == 0 and J1 <= J


def bc(ap, shape):
    return ap.to_broadcast(shape)


def build(nc, x, src, dst, W0, as0, ad0, b0, W1, as1, ad1, b1, gamma, beta, Wg, bg, eW1, eb1, eW2, eb2, out):
    ctx = ExitStack()
    with ctx:
        def sb(name, shape, dt=F32):
            return ctx.enter_context(nc.sbuf_tensor(name, shape, dt))

        def sem(name):
            return ctx.enter_context(nc.semaphore(name))

        def dram(name, shape, dt=F32):
            return nc.dram_tensor(name, shape, dt, kind="Internal").ap()

        tab = [dram("tab0", [NP, ROWT]), dram("tab1", [NP, ROWT])]
        adt = dram("adt", [NP, 2 * HD])
        srcp = dram("srcp", [P, C], I32)
        dstp = dram("dstp", [P, C])
        adstart = dram("adstart", [EP, 2 * HD])
        state = [dram("state0", [EP, ROWS]), dram("state1", [NP, ROWS])]
        degd = dram("degd", [NP, 1])
        acc = dram("acc", [NP + P, D])
        placed = dram("placed", [NEX * REG + P, ROWP])
        states0 = state[0].rearrange("(p j) r -> p (j r)", p=P)
        adstart_c = adstart.rearrange("(p j) r -> p (j r)", p=P)

        AR = sb("AR", [P, AW])
        G = [AR[:, s * J * ROWS:(s + 1) * J * ROWS].rearrange("p (j r) -> p j r", r=ROWS) for s in range(2)]
        X = AR[:, GW:GW + NT * D].rearrange("p (t d) -> p t d", d=D)
        FB = GW + NT * D
        zero = sb("zero", [P, 1024])
        ident = sb("ident", [P, P])
        ones = sb("ones", [P, P])
        shf = sb("shf", [P, P])
        wrap = sb("wrap", [P, P])
        tri = sb("tri", [P, P])
        pidx = sb("pidx", [P, 1])
        pcol = sb("pcol", [P, 1])
        nid = sb("nid", [P, NT])
        e8 = sb("e8", [P, HD])
        b01 = sb("b01", [P, D])
        gam = sb("gam", [P, D])
        bet = sb("bet", [P, D])
        wg = sb("wg", [P, KD, NEX])
        bgb = sb("bgb", [P, NEX])
        eb1T = sb("eb1T", [P, NEX, MH])
        eb2b = sb("eb2b", [P, NEX, D])
        mv = sb("mv", [P, NT, 2])
        rstd = sb("rstd", [P, NT])
        nmr = sb("nmr", [P, NT])
        hT4 = sb("hT4", [P, 2, 2 * D])
        hT = hT4[:, :, 0:D]
        row = sb("row", [P, 2, 288])
        asr = sb("asr", [P, NT, 16])
        adr = sb("adr", [P, NT, 16])
        same1 = sb("same1", [P, J1])
        ends = sb("ends", [P, 8])
        idx = sb("idx", [P, 2, J], I32)
        neg = sb("neg", [P, J])
        carry = sb("carry", [P, ROWS])
        idx1 = sb("idx1", [P, 2, J1], I32)
        dst1 = sb("dst1", [P, J1])
        deg1 = sb("deg1", [P, J1])
        dneg = sb("dneg", [P, J1])
        ifirst = sb("ifirst", [P, 1], I32)
        cnt = sb("cnt", [P, 8, NT])
        At = sb("At", [P, 2, ROWS])
        blk = sb("blk", [1, NBLK])
        sml = sb("sml", [P, 16])
        bcur = sb("bcur", [P, MH])

        hrow = sb("hrow", [P, 2, D])
        icnt = sb("icnt", [P, 4, NT], I32)
        adc = sb("adc", [P, HD])
        adf = sb("adf", [P, 2, 2 * HD])
        ifirst1 = sb("ifirst1", [P, 1], I32)
        oh = sb("oh", [P, 2, 2 * P])
        fz = sb("fz", [P, 2, 5, 2, GRP, HD])
        fln = sb("fln", [P, GRP, 6])
        fmv = sb("fmv", [P, GRP, 2])
        frs = sb("frs", [P, 3, GRP])
        wts = sb("wts", [P, 3, GRP])
        pos = sb("pos", [P, 2, GRP])
        ipos = sb("ipos", [P, 2, 2, GRP], I32)
        tot = sb("tot", [P, NEX])
        toff = sb("toff", [P, 4, NEX])
        ipad = sb("ipad", [P, NEX], I32)
        padrow = sb("padrow", [P, ROWP])
        e8r = sb("e8r", [P, NEX])
        slot_id = sb("slot_id", [1, SLOTS])
        tile_e = sb("tile_e", [1, 3, SLOTS])
        reg = sb("reg", [1, 2, SLOTS], I32)
        idb = sb("idb", [P, 2, 1], I32)
        wb = sb("wb", [P, 2, 1])

        ps = [ctx.enter_context(nc.psum_tensor(f"ps{i}", [P, 512], F32)) for i in range(8)]

        s_hold = [sem(f"s_hold{i}") for i in range(5)]
        s_const = sem("s_const")
        s_clear = sem("s_clear")
        s_x = sem("s_x")
        s_w = sem("s_w")
        s_edge = sem("s_edge")
        s_par = sem("s_par")
        s_zero = sem("s_zero")
        s_wc = sem("s_wc")
        s_var = sem("s_var")
        s_std = sem("s_std")
        s_h = sem("s_h")
        s_tr = sem("s_tr")
        s_ht = sem("s_ht")
        s_xw = sem("s_xw")
        s_row = sem("s_row")
        s_res = sem("s_res")
        s_tab = [sem("s_tab0"), sem("s_tab1")]
        s_adt = sem("s_adt")
        s_dstf = sem("s_dstf")
        s_dstd = sem("s_dstd")
        s_blks = sem("s_blks")
        s_blkp = sem("s_blkp")
        s_bidx = sem("s_bidx")
        s_blk = [sem(f"s_blk{i}") for i in range(7)]
        s_blkc = sem("s_blkc")
        s_cnt = sem("s_cnt")
        s_cntp = sem("s_cntp")
        s_start = sem("s_start")
        s_scat = sem("s_scat")
        s_adf = sem("s_adf")
        s_adm = sem("s_adm")
        s_degd = sem("s_degd")
        s_deg1 = sem("s_deg1")
        s_g1 = sem("s_g1")
        s_c1 = sem("s_c1")
        s_e1 = sem("s_e1")
        s_d1 = sem("s_d1")
        s_st1 = sem("s_st1")
        s_idx = [sem("s_idxa"), sem("s_idxb")]
        s_ad = [sem("s_ada"), sem("s_adb")]
        s_g = [sem("s_ga"), sem("s_gb")]
        s_st = [sem("s_sta"), sem("s_stb")]
        s_dif = sem("s_dif")
        s_exp = sem("s_exp")
        s_done = sem("s_done")
        s_link = sem("s_link")
        s_rep = sem("s_rep")
        s_linkp = sem("s_linkp")
        s_cp = sem("s_cp")
        s_cps = sem("s_cps")
        s_cdif = sem("s_cdif")
        s_cexp = sem("s_cexp")
        s_cs = sem("s_cs")
        s_cb = sem("s_cb")
        s_A = sem("s_A")
        s_fidx = sem("s_fidx")
        s_fg = [sem("s_fga"), sem("s_fgb")]
        s_fx = [sem("s_fxa"), sem("s_fxb")]
        s_oh = sem("s_oh")
        s_ohs = sem("s_ohs")
        s_cg = sem("s_cg")
        s_cgs = sem("s_cgs")
        s_fe = sem("s_fe")
        s_fexp = sem("s_fexp")
        s_fs = sem("s_fs")
        s_fsq = sem("s_fsq")
        s_fgrp = sem("s_fgrp")
        s_x1 = sem("s_x1")
        s_xnT = sem("s_xnT")
        s_xnc = sem("s_xnc")
        s_lg = sem("s_lg")
        s_lgc = sem("s_lgc")
        s_m2 = sem("s_m2")
        s_m2e = sem("s_m2e")
        s_mask = sem("s_mask")
        s_rank = sem("s_rank")
        s_pos = sem("s_pos")
        s_tiles = sem("s_tiles")
        s_pads = sem("s_pads")
        s_padt = sem("s_padt")
        s_pz = sem("s_pz")
        s_hb = sem("s_hb")
        s_acc = sem("s_acc")
        s_xb = sem("s_xb")
        s_prx = sem("s_prx")
        s_m2w = sem("s_m2w")
        s_idw = sem("s_idw")
        s_add = sem("s_add")
        s_ad1 = sem("s_ad1")
        s_wat = sem("s_wat")
        s_place = [sem("s_placea"), sem("s_placeb")]
        s_ew = sem("s_ew")
        s_xs = [sem("s_xsa"), sem("s_xsb")]
        s_tx = sem("s_tx")
        s_xt = sem("s_xt")
        s_m1 = sem("s_m1")
        s_hc = sem("s_hc")
        s_th = sem("s_th")
        s_bc = sem("s_bc")
        s_gl = sem("s_gl")
        s_mm2 = sem("s_mm2")
        s_y = sem("s_y")
        s_out = sem("s_out")

        def hold(eng, which, s, value):
            eng.wait_ge(s, value)
            if not isinstance(value, int):
                eng.sem_inc(s_hold[which], 1)

        V = nc.vector
        srcI = AR[:, 0:C].bitcast(I32)
        dstI = AR[:, C:2 * C].bitcast(I32)
        dstF = AR[:, 2 * C:3 * C]
        blkrow = [AR[:, J * ROWS + i * BLK:J * ROWS + (i + 1) * BLK] for i in range(7)]
        scr = AR[:, FB:FB + 1024]
        def cut(a, n):
            return AR[:, FB + a:FB + a + n]

        adin = cut(1820, 4 * J * HD).rearrange("p (s j k h) -> p s j k h", s=2, k=2, h=HD)
        adx = cut(3804, J * HD).rearrange("p (j h) -> p j h", h=HD)
        Z = cut(4300, J * HD).rearrange("p (j h) -> p j h", h=HD)
        DW = cut(4796, 2 * J * HD).rearrange("p (k j h) -> p k j h", k=2, h=HD)
        same = cut(5788, C)
        Wc = AR[:, J * ROWS + 4000:J * ROWS + 4576].rearrange("p (k f) -> p k f", k=KD)
        att = AR[:, J * ROWS + 5000:J * ROWS + 5000 + 4 * F].rearrange("p (k f) -> p k f", k=4)
        ln = AR[:, J * ROWS + 4600:J * ROWS + 4600 + 6 * NT].rearrange("p (t s) -> p t s", s=6)
        rt = sb("rt", [P, 6, GRP, NEX])
        tix = sb("tix", [P, GRP, 8], mybir.dt.uint32)
        top = sb("top", [P, GRP, 8])
        last1 = cut(1152, ROWS)
        rep = cut(1300, 4 * F).rearrange("p (k q f) -> p k q f", k=2, q=2)
        cT = AR[:, FB:FB + 512].rearrange("p (k e) -> p k e", k=4)
        cD = AR[:, FB + 512:FB + 768].rearrange("p (k e) -> p k e", k=2)
        cS = AR[:, FB + 768:FB + 1152].rearrange("p (k e) -> p k e", k=3)
        at = 0
        stg = AR[:, at:at + 4 * GRP * ROWS].rearrange("p (s k t r) -> p s k t r", s=2, k=2, r=ROWS)
        at += 4 * GRP * ROWS
        cgr = AR[:, at:at + 4 * GRP * ROWS].rearrange("p (s k t r) -> p s k t r", s=2, k=2, r=ROWS)
        at += 4 * GRP * ROWS
        xwg = AR[:, at:at + 4 * GRP * ROWT].rearrange("p (s k t r) -> p s k t r", s=2, k=2, r=ROWT)
        at += 4 * GRP * ROWT
        hb = AR[:, at:at + GRP * D].rearrange("p (t d) -> p t d", d=D)
        at += GRP * D
        pr = [AR[:, at:at + 2 * GRP * ROWP].rearrange("p (k t r) -> p k t r", k=2, r=ROWP)]
        at += 2 * GRP * ROWP
        assert at <= GW
        at = FB
        og = AR[:, at:at + GRP * D].rearrange("p (t d) -> p t d", d=D)
        at += GRP * D
        tg = AR[:, at:at + GRP * D].rearrange("p (t d) -> p t d", d=D)
        at += GRP * D
        pr.append(AR[:, at:at + 2 * GRP * ROWP].rearrange("p (k t r) -> p k t r", k=2, r=ROWP))
        at += 2 * GRP * ROWP
        assert at <= AW, at
        zs = sb("zs", [P, NT, 16])
        bare = sb("bare", [P, 2, 2, NT])
        w1s = AR[:, 0:NEX * KD * HID].rearrange("p (e k h) -> p e k h", e=NEX, k=KD)
        w2s = AR[:, NEX * KD * HID:2 * NEX * KD * HID].rearrange("p (e m d) -> p e m d", e=NEX, m=MH)
        at = 2 * NEX * KD * HID
        xs = AR[:, at:at + 2 * ROWP].rearrange("p (s d) -> p s d", s=2)
        at += 2 * ROWP
        xsT = AR[:, at:at + 2 * D].rearrange("p (s k t) -> p s k t", s=2, k=KD)
        at += 2 * D
        hs = AR[:, at:at + HID]
        at += HID
        hsT = AR[:, at:at + HID].rearrange("p (m t) -> p m t", m=MH)
        at += HID
        ys = AR[:, at:at + 2 * D].rearrange("p (s d) -> p s d", s=2)
        at += 2 * D
        assert at <= AW
        block = ctx.enter_context(nc.Block())

        @block.sync
        def _(sp):
            with nc.allow_non_contiguous_dma(reason="small tables, once"):
                sp.wait_ge(s_clear, 1)
                sp.dma_start(dstI[0:P - 1, :], dst[0:(P - 1) * C].rearrange("(p j) -> p j", j=C)).then_inc(s_edge, 16)
                sp.dma_start(dstI[P - 1:P, 0:E - (P - 1) * C], dst[(P - 1) * C:E].rearrange("(a j) -> a j", a=1)).then_inc(s_edge, 16)
                for g in range(NG):
                    full = min(GRP, NT - 1 - g * GRP)
                    sp.dma_start(X[:, g * GRP:g * GRP + full, :],
                                 x[g * GRP * P:(g * GRP + full) * P, :].rearrange("(t p) d -> p t d", p=P)).then_inc(s_x, 16)
                sp.dma_start(X[0:TAIL, NT - 1, :], x[(NT - 1) * P:N, :]).then_inc(s_x, 16)
                for k, w in enumerate((W0, W1)):
                    sp.dma_start(Wc[:, :, ROWT * k:ROWT * k + F], w.rearrange("(k p) f -> p k f", p=P)).then_inc(s_w, 16)
                for k, a in enumerate((as0, as1, ad0, ad1)):
                    sp.dma_start(att[:, k, :], a.rearrange("h c -> (h c)").partition_broadcast(P)).then_inc(s_w, 16)
                sp.dma_start(srcI[0:P - 1, :], src[0:(P - 1) * C].rearrange("(p j) -> p j", j=C)).then_inc(s_edge, 16)
                sp.dma_start(srcI[P - 1:P, 0:E - (P - 1) * C], src[(P - 1) * C:E].rearrange("(a j) -> a j", a=1)).then_inc(s_edge, 16)
                sp.dma_start(idx1[:, 0, :], src[0:NP].rearrange("(p j) -> p j", j=J1)).then_inc(s_edge, 16)
                sp.dma_start(idx1[:, 1, :], dst[0:NP].rearrange("(p j) -> p j", j=J1)).then_inc(s_edge, 16)
                sp.wait_ge(s_const, 1)
                n = C * 2 * HD
                for a in range(0, n, 1024):
                    w = min(1024, n - a)
                    sp.dma_start(adstart_c[:, a:a + w], zero[:, 0:w]).then_inc(s_zero, 16)
                sp.dma_start(acc[NP:NP + P, :], zero[:, 0:D]).then_inc(s_zero, 16)
                sp.wait_ge(s_edge, 96)
                sp.dma_start(srcp, srcI).then_inc(s_dstd, 16)
                sp.wait_ge(s_dstf, 1)
                sp.dma_start(dstp, dstF).then_inc(s_dstd, 16)
                sp.wait_ge(s_dstd, 32)
                sp.dma_start(blk[:, :], dstp.rearrange("p j -> (p j)").rearrange("(a b) -> a b", b=BLK)[:, 0:1].rearrange("a b -> b a")).then_inc(s_blks, 16)
                for dstt, v in ((b01[:, 0:F], b0), (b01[:, F:D], b1), (gam[:, :], gamma), (bet[:, :], beta), (bgb[:, :], bg)):
                    sp.dma_start(dstt, v.partition_broadcast(P)).then_inc(s_par, 16)
                sp.dma_start(wg[:, :, :], Wg.rearrange("(k p) e -> p k e", p=P)).then_inc(s_par, 16)
                sp.dma_start(eb2b[:, :, :], eb2.rearrange("e d -> (e d)").partition_broadcast(P)).then_inc(s_par, 16)
                for e in range(NEX):
                    sp.dma_start(eb1T[:, e, :], eb1[e].rearrange("(m p) -> p m", p=P)).then_inc(s_par, 16)
                sp.dma_start(idx[:, 0, :], srcp[:, 0:J]).then_inc(s_idx[0], 16)
                for t in range(NT):
                    sp.wait_ge(s_row, t + 1)
                    for k in range(2):
                        sp.dma_start(tab[k][t * P:(t + 1) * P, :], row[:, t % 2, ROWT * k:ROWT * (k + 1)]).then_inc(s_tab[t % 2], 16)
                sp.wait_ge(s_res, NT)
                sp.dma_start(adt.rearrange("(t p) h -> p t h", p=P), adr[:, :, :]).then_inc(s_adt, 16)
                sp.wait_ge(s_start, 1)
                sp.dma_start(degd.rearrange("(t p) a -> p (t a)", p=P), cnt[:, 4, :]).then_inc(s_degd, 16)
                sp.wait_ge(s_degd, 16)
                sp.dma_start(deg1[:, :], degd.rearrange("(p j) a -> p (j a)", p=P)).then_inc(s_deg1, 16)
                sp.wait_ge(s_adf, 32)
                sp.wait_ge(s_scat, 16 * NT)
                sp.dma_start(adin[:, 1, 0:J1].rearrange("p j k h -> p (j k h)"), adstart[0:NP, :].rearrange("(p j) h -> p (j h)", p=P)).then_inc(s_ad1, 16)
                sp.wait_ge(s_ad1, 16)
                sp.dma_start(adstart.rearrange("(p j) h -> p j h", p=P)[:, 0, 0:HD], adf[:, 0, 0:HD]).then_inc(s_adm, 16)
                sp.wait_ge(s_adm, 16)
                sp.dma_start(adin[:, 0].rearrange("p j k h -> p (j k h)"), adstart_c[:, 0:J * 2 * HD]).then_inc(s_ad[0], 16)
                sp.wait_ge(s_d1, 1)
                sp.dma_start(state[1].rearrange("(p j) r -> p j r", p=P), G[1][:, 0:J1, :]).then_inc(s_st1, 16)
                def fetch(s, b):
                    sp.dma_start(idx[:, s, :], srcp[:, bass.ds(b * J, J)]).then_inc(s_idx[s], 16)
                    sp.dma_start(adin[:, s].rearrange("p j k h -> p (j k h)"), adstart_c[:, bass.ds(b * (J * 2 * HD), J * 2 * HD)]).then_inc(s_ad[s], 16)

                with sp.Fori(0, NB // 2 - 1) as i:
                    for s in range(2):
                        fetch(1 - s, i * 2 + (s + 1))
                        hold(sp, 0, s_done, i * 2 + (s + 1))
                        sp.dma_start(states0[:, bass.ds((i * 2 + s) * (J * ROWS), J * ROWS)], G[s].rearrange("p j r -> p (j r)")).then_inc(s_st[s], 16)
                sp.dma_start(idx[:, 1, :], srcp[:, (NB - 1) * J:]).then_inc(s_idx[1], 16)
                sp.dma_start(adin[:, 1].rearrange("p j k h -> p (j k h)"), adstart_c[:, (NB - 1) * J * 2 * HD:]).then_inc(s_ad[1], 16)
                for s in range(2):
                    sp.wait_ge(s_done, NB - 1 + s)
                    sp.dma_start(states0[:, (NB - 2 + s) * J * ROWS:(NB - 1 + s) * J * ROWS], G[s].rearrange("p j r -> p (j r)")).then_inc(s_st[s], 16)
                def own(g):
                    if g >= 2:
                        sp.wait_ge(s_fgrp, g - 1)
                    for k in range(2):
                        sp.dma_start(xwg[:, g % 2, k, :, :], tab[k][g * GRP * P:(g + 1) * GRP * P, :].rearrange("(t p) r -> p t r", p=P)).then_inc(s_fx[g % 2], 16)

                for s in range(2):
                    sp.wait_ge(s_st[s], 16 * (NB // 2))
                own(0)
                for g in range(NG):
                    if g + 1 < NG:
                        own(g + 1)
                    sp.wait_ge(s_x1, g + 1)
                    sp.dma_start(acc[g * GRP * P:(g + 1) * GRP * P, :].rearrange("(t p) d -> p t d", p=P), X[:, g * GRP:(g + 1) * GRP, :]).then_inc(s_acc, 16)
                sp.wait_ge(s_pz, 1)
                sp.dma_start(placed[NEX * REG:NEX * REG + P, :], padrow[:, :]).then_inc(s_padt, 16)
                for s in range(2):
                    sp.wait_ge(s_place[s], 16 * 2 * GRP * ((NG + 1 - s) // 2))
                sp.wait_ge(s_acc, 16 * NG)
                sp.wait_ge(s_fgrp, NG)
                sp.wait_ge(s_lgc, NG)
                for e in range(NEX):
                    sp.dma_start(w1s[:, e, :, :], eW1[e].rearrange("(k p) h -> p k h", p=P)).then_inc(s_ew, 16)
                    sp.dma_start(w2s[:, e, :, :], eW2[e].rearrange("(m p) d -> p m d", p=P)).then_inc(s_ew, 16)
                sp.wait_ge(s_tiles, 1)
                sp.wait_ge(s_pads, 16 * NEX)
                sp.wait_ge(s_padt, 16)

                def place_row(t):
                    return sp.value_load(reg[0:1, 1, t], min_val=0, max_val=NEX * REG)

                for s in range(2):
                    sp.dma_start(xs[:, s, :], placed[bass.ds(place_row(slice(s, s + 1)), P), :]).then_inc(s_xs[s], 16)
                with sp.Fori(0, SLOTS // 2 - 1) as i:
                    for s in range(2):
                        r = place_row(bass.ds(i * 2 + (s + 2), 1))
                        hold(sp, 0, s_tx, i * 2 + (s + 1))
                        hold(sp, 0, s_idw, i * 2 + (s + 1))
                        sp.dma_start(xs[:, s, :], placed[bass.ds(r, P), :]).then_inc(s_xs[s], 16)
                sp.wait_ge(s_add, 16 * SLOTS)
                sp.dma_start(out.rearrange("n d -> (n d)").rearrange("(a b) -> a b", a=160), acc[0:N, :].rearrange("n d -> (n d)").rearrange("(a b) -> a b", a=160)).then_inc(s_out, 16)
                sp.wait_ge(s_out, 16)

        @block.gpsimd
        def _(pool):
            g = nc.gpsimd
            g.memset(ones[:, :], 1.0)
            g.memset(ident[:, :], 0.0)
            g.memset(shf[:, :], 0.0)
            g.memset(wrap[:, :], 0.0)
            g.memset(zero[:, :], 0.0).then_inc(s_const, 1)
            pool.wait_ge(s_const, 1)
            g.affine_select(out=ident[:, :], in_=ident[:, :], compare_op=ALU.not_equal, fill=1.0, base=0, pattern=[[-1, P]], channel_multiplier=1)
            g.affine_select(out=shf[:, :], in_=shf[:, :], compare_op=ALU.not_equal, fill=1.0, base=1, pattern=[[-1, P]], channel_multiplier=1)
            g.affine_select(out=wrap[:, :], in_=wrap[:, :], compare_op=ALU.not_equal, fill=1.0, base=-(P - 1), pattern=[[-P, P]], channel_multiplier=1)
            g.affine_select(out=tri[:, :], in_=ones[:, :], compare_op=ALU.is_gt, fill=0.0, base=0, pattern=[[1, P]], channel_multiplier=-1)
            g.iota(pidx[:, :], pattern=[[0, 1]], base=0, channel_multiplier=1, allow_small_or_imprecise_dtypes=True)
            g.iota(nid[:, :], pattern=[[P, NT]], base=0, channel_multiplier=1, allow_small_or_imprecise_dtypes=True)
            g.iota(e8[:, :], pattern=[[1, HD]], base=0, channel_multiplier=0, allow_small_or_imprecise_dtypes=True)
            g.memset(padrow[:, :], 0.0)
            g.memset(tot[:, :], 0.0)
            g.iota(slot_id[:, :], pattern=[[P, SLOTS]], base=0, channel_multiplier=0, allow_small_or_imprecise_dtypes=True).then_inc(s_const, 1)
            pool.wait_ge(s_bidx, 1)
            pool.wait_ge(s_dstd, 32)
            dblk = dstp.rearrange("p j -> (p j)").rearrange("(a b) -> a b", b=BLK)
            for t in range(NT):
                if t >= 7:
                    pool.wait_ge(s_blkc, t - 6)
                pool.indirect_dma_start(out=blkrow[t % 7], out_offset=None, in_=dblk,
                                        in_offset=bass.IndirectOffsetOnAxis(ap=icnt[:, 0, t:t + 1], axis=0)).then_inc(s_blk[t % 7], 16)
            for q in range(2):
                pool.wait_ge(s_tab[q], 32 * ((NT + 1 - q) // 2))
            pool.wait_ge(s_edge, 96)
            pool.wait_ge(s_blkc, NT)
            for j in range(J1):
                pool.indirect_dma_start(out=G[1][:, j, 0:ROWT], out_offset=None, in_=tab[1],
                                        in_offset=bass.IndirectOffsetOnAxis(ap=idx1[:, 0, j:j + 1], axis=0)).then_inc(s_g1, 16)
            pool.wait_ge(s_start, 1)
            pool.wait_ge(s_res, NT)
            pool.wait_ge(s_zero, 16 * (-(-C * 2 * HD // 1024) + 1))
            for t in range(NT):
                pool.indirect_dma_start(out=adstart, out_offset=bass.IndirectOffsetOnAxis(ap=icnt[:, 1, t:t + 1], axis=0),
                                        in_=adr[:, t, :], in_offset=None, bounds_check=EP - 1, oob_is_err=False).then_inc(s_scat, 16)
            pool.wait_ge(s_adt, 16)
            for k, a in enumerate((ifirst, ifirst1)):
                pool.indirect_dma_start(out=adf[:, k, :], out_offset=None, in_=adt,
                                        in_offset=bass.IndirectOffsetOnAxis(ap=a[:, :], axis=0)).then_inc(s_adf, 16)

            def gather(s):
                for j in range(J):
                    pool.indirect_dma_start(out=G[s][:, j, 0:ROWT], out_offset=None, in_=tab[0],
                                            in_offset=bass.IndirectOffsetOnAxis(ap=idx[:, s, j:j + 1], axis=0)).then_inc(s_g[s], 16)

            for s in range(2):
                pool.wait_ge(s_idx[s], 16)
                if s == 1:
                    pool.wait_ge(s_st1, 16)
                gather(s)
            with pool.Fori(1, NB // 2) as i:
                for s in range(2):
                    hold(pool, 1, s_idx[s], i * 16 + 16)
                    hold(pool, 1, s_st[s], i * 16)
                    gather(s)
            pool.wait_ge(s_fidx, 1)
            for s in range(2):
                pool.wait_ge(s_st[s], 16 * (NB // 2))
            def last_states(n):
                if n >= 2:
                    pool.wait_ge(s_fgrp, n - 1)
                for k in range(2):
                    for t in range(GRP):
                        pool.indirect_dma_start(out=stg[:, n % 2, k, t, :], out_offset=None, in_=state[k],
                                                in_offset=bass.IndirectOffsetOnAxis(ap=icnt[:, 2 + k, n * GRP + t:n * GRP + t + 1], axis=0)).then_inc(s_fg[n % 2], 16)

            def place(n):
                pool.wait_ge(s_pos, n + 1)
                for k in range(2):
                    for t in range(GRP):
                        pool.indirect_dma_start(out=placed, out_offset=bass.IndirectOffsetOnAxis(ap=ipos[:, n % 2, k, t:t + 1], axis=0),
                                                in_=pr[n % 2][:, k, t, :], in_offset=None, bounds_check=NEX * REG + P - 1, oob_is_err=False).then_inc(s_place[n % 2], 16)

            last_states(0)
            for n in range(NG):
                if n + 1 < NG:
                    last_states(n + 1)
                if n >= 1:
                    place(n - 1)
            place(NG - 1)
            pool.wait_ge(s_tiles, 1)
            for e in range(NEX):
                pool.indirect_dma_start(out=placed, out_offset=bass.IndirectOffsetOnAxis(ap=ipad[:, e:e + 1], axis=0),
                                        in_=padrow[:, :], in_offset=None, bounds_check=NEX * REG + P - 1, oob_is_err=False).then_inc(s_pads, 16)
            def add_answer(s):
                pool.indirect_dma_start(out=acc, out_offset=bass.IndirectOffsetOnAxis(ap=idb[:, s, :], axis=0),
                                        in_=ys[:, s, :], in_offset=None, bounds_check=NP + P - 1, oob_is_err=True, compute_op=ALU.add).then_inc(s_add, 16)

            for s in range(2):
                pool.wait_ge(s_y, s + 1)
                if s:
                    pool.wait_ge(s_add, 16)
                add_answer(s)
            with pool.Fori(1, SLOTS // 2) as i:
                for s in range(2):
                    hold(pool, 1, s_y, i * 2 + (s + 1))
                    hold(pool, 1, s_add, i * 32 + 16 * s)
                    add_answer(s)

        @block.scalar
        def _(act):
            S = nc.scalar
            act.wait_ge(s_var, 1)
            S.activation(rstd[:, :], mv[:, :, 1], ACT.Sqrt).then_inc(s_std, 1)
            def rows(t):
                act.wait_ge(s_xw, t + 1)
                if t >= 2:
                    act.wait_ge(s_tab[t % 2], 32 * (t // 2))
                    act.wait_ge(s_res, t - 1)
                S.copy(row[:, t % 2, :], ps[2 + t % 2][:, 0:288]).then_inc(s_row, 1)

            for t in range(NT):
                act.wait_ge(s_tr, t + 1)
                if t >= 2:
                    act.wait_ge(s_xw, t - 1)
                S.copy(hT[:, t % 2, :], ps[t % 2][:, 0:D]).then_inc(s_ht, 1)
                if t >= 1:
                    rows(t - 1)
            rows(NT - 1)
            act.wait_ge(s_c1, 1)
            S.activation(DW[:, :, 0:J1, :], DW[:, :, 0:J1, :], ACT.Exp).then_inc(s_e1, 1)
            with act.Fori(0, NB) as b:
                hold(act, 2, s_dif, b + 1)
                S.activation(DW[:, :, :, :], DW[:, :, :, :], ACT.Exp).then_inc(s_exp, 1)
            for k in range(2):
                act.wait_ge(s_cdif, k + 1)
                S.activation(cD[:, :, :], cD[:, :, :], ACT.Exp).then_inc(s_cexp, 1)
            def carries(g):
                for m in range(GRP):
                    n = g * GRP + m
                    act.wait_ge(s_cg, n + 1)
                    S.copy(cgr[:, g % 2].rearrange("p k t r -> p (k t r)")[:, 2 * m * ROWS:2 * (m + 1) * ROWS], ps[4 + n % 2][:, 0:2 * ROWS]).then_inc(s_cgs, 1)
                act.wait_ge(s_fe, g + 1)
                S.activation(fz[:, g % 2, 0:3, :, :, :], fz[:, g % 2, 0:3, :, :, :], ACT.Exp).then_inc(s_fexp, 1)

            for s in range(2):
                act.wait_ge(s_st[s], 16 * (NB // 2))
            carries(0)
            for g in range(NG):
                if g >= 1:
                    act.wait_ge(s_xb, g)
                for t in range(GRP):
                    n = g * GRP + t
                    last = S.activation(hb[:, t, :], X[:, n, :], ACT.Identity, bias=nmr[:, n:n + 1], scale=rstd[:, n:n + 1])
                last.then_inc(s_hb, 1)
                if g + 1 < NG:
                    if g >= 1:
                        act.wait_ge(s_fgrp, g)
                    carries(g + 1)
                if g >= 1:
                    act.wait_ge(s_m2, g)
                    S.activation(wts[:, 0, :], wts[:, 0, :], ACT.Exp).then_inc(s_m2e, 1)
                for q in range(2):
                    act.wait_ge(s_fs, 2 * g + q + 1)
                    S.activation(frs[:, 0, :], fmv[:, :, 1], ACT.Sqrt).then_inc(s_fsq, 1)
                    act.wait_ge(s_m2w, 2 * g + q + 1)
                    if q == 0:
                        for t in range(GRP):
                            last = S.activation(og[:, t, :], og[:, t, :], ACT.Identity, bias=frs[:, 2, t:t + 1], scale=frs[:, 1, t:t + 1])
                        last.then_inc(s_prx, 1)
                    else:
                        if g >= 2:
                            act.wait_ge(s_place[g % 2], 16 * 2 * GRP * (g // 2))
                        for k in range(2):
                            for t in range(GRP):
                                n = g * GRP + t
                                last = S.activation(pr[g % 2][:, k, t, 0:D], X[:, n, :], ACT.Identity, bias=frs[:, 2, t:t + 1], scale=frs[:, 1, t:t + 1])
                            if k == 0:
                                last.then_inc(s_wat, 1)
                        last.then_inc(s_prx, 1)
                for t in range(0, GRP, 2):
                    w = min(2, GRP - t)
                    act.wait_ge(s_xnT, g * 4 + t // 2 + 1)
                    S.copy(hT4[:, (t // 2) % 2, 0:w * D], ps[(t // 2) % 2][:, 0:w * D]).then_inc(s_xnc, 1)
            act.wait_ge(s_m2, NG)
            S.activation(wts[:, 0, :], wts[:, 0, :], ACT.Exp).then_inc(s_m2e, 1)
            with act.Fori(0, SLOTS // 2) as i:
                for s in range(2):
                    act.wait_ge(s_th, i * 2 + (s + 1))
                    act.wait_ge(s_bc, i * 2 + (s + 1))
                    for m in range(MH):
                        last = S.activation(hsT[:, m, :], ps[2 + m // 4][:, (m % 4) * P:(m % 4 + 1) * P], ACT.Gelu, bias=bcur[:, m:m + 1])
                    last.then_inc(s_gl, 1)

        @block.tensor
        def _(pe):
            T = nc.tensor
            pe.wait_ge(s_const, 2)
            pe.wait_ge(s_blks, 16)
            T.matmul(ps[6][:, 0:NBLK], ones[0:1, :], blk[:, :], start=True, stop=True).then_inc(s_blkp, 1)
            pe.wait_ge(s_wc, 1)

            def project(t):
                pe.wait_ge(s_ht, t + 1)
                if t >= 2:
                    pe.wait_ge(s_row, t - 1)
                for k in range(KD):
                    mm = T.matmul(ps[2 + t % 2][:, 0:288], hT[:, t % 2, k * P:(k + 1) * P], Wc[:, k, :], start=(k == 0), stop=(k == KD - 1))
                mm.then_inc(s_xw, 1)

            for t in range(NT):
                pe.wait_ge(s_h, t + 1)
                if t >= 2:
                    pe.wait_ge(s_ht, t - 1)
                for k in range(KD):
                    mm = T.transpose(ps[t % 2][:, k * P:(k + 1) * P], hrow[:, t % 2, k * P:(k + 1) * P], ident[:, :])
                mm.then_inc(s_tr, 1)
                if t >= 1:
                    project(t - 1)
            project(NT - 1)
            pe.wait_ge(s_cnt, 1)
            T.matmul(ps[7][:, 0:NT], shf[:, :], cnt[:, 2, :], start=True, stop=False)
            T.matmul(ps[7][:, 1:NT], wrap[:, :], cnt[:, 2, 0:NT - 1], start=False, stop=True).then_inc(s_cntp, 1)
            T.matmul(ps[6][:, 0:2], shf[:, :], ends[:, 0:2], start=True, stop=True).then_inc(s_linkp, 1)
            for k in range(2):
                if k == 0:
                    pe.wait_ge(s_rep, 1)
                    pe.wait_ge(s_link, 1)
                else:
                    pe.wait_ge(s_A, 1)
                last = carry if k == 0 else last1
                lk = sml[:, 8 + k:9 + k]
                T.matmul(ps[0][:, 0:P], bc(lk, [P, P]), ident[:, :], start=True, stop=True)
                T.matmul(ps[0][:, P:2 * P], rep[:, k, 1, :], ident[:, :], start=True, stop=True)
                T.matmul(ps[0][:, 2 * P:3 * P], rep[:, k, 0, :], ident[:, :], start=True, stop=True)
                T.matmul(ps[0][:, 3 * P:4 * P], last[:, 0:F], ident[:, :], start=True, stop=True).then_inc(s_cp, 1)
                pe.wait_ge(s_cs, k + 1)
                for q in range(3):
                    mm = T.transpose(ps[1][:, q * P:(q + 1) * P], cS[:, q, :], ident[:, :])
                mm.then_inc(s_cb, 1)
            def carries(g):
                for m in range(GRP):
                    n = g * GRP + m
                    if n >= 2:
                        pe.wait_ge(s_ohs, n - 1)
                    for q in range(2):
                        k, t = divmod(2 * m + q, GRP)
                        mm = T.matmul(ps[2 + n % 2][:, q * P:(q + 1) * P], bc(cnt[:, 5 + k, g * GRP + t:g * GRP + t + 1], [P, P]), ident[:, :], start=True, stop=True)
                    mm.then_inc(s_oh, 1)
                    if m >= 1:
                        pick(n - 1)
                pick(g * GRP + GRP - 1)

            def pick(n):
                pe.wait_ge(s_ohs, n + 1)
                if n >= 2:
                    pe.wait_ge(s_cgs, n - 1)
                for q in range(2):
                    k = (2 * (n % GRP) + q) // GRP
                    mm = T.matmul(ps[4 + n % 2][:, q * ROWS:(q + 1) * ROWS], oh[:, n % 2, q * P:(q + 1) * P], At[:, k, :], start=True, stop=True)
                mm.then_inc(s_cg, 1)

            def ranks(g):
                pe.wait_ge(s_mask, g + 1)
                mk = rt[:, 3, :, :].rearrange("p t e -> p (t e)")
                T.matmul(ps[7][:, 0:GRP * NEX], tri[:, :], mk, start=True, stop=True)
                T.matmul(ps[7][:, GRP * NEX:2 * GRP * NEX], ones[:, :], mk, start=True, stop=True).then_inc(s_rank, 1)

            def logits(g, t):
                w = min(2, GRP - t)
                pe.wait_ge(s_xnc, g * 4 + t // 2 + 1)
                for q in range(w):
                    for k in range(KD):
                        mm = T.matmul(ps[6][:, (t + q) * NEX:(t + q + 1) * NEX], hT4[:, (t // 2) % 2, (q * KD + k) * P:(q * KD + k + 1) * P], wg[:, k, :],
                                      start=(k == 0), stop=(k == KD - 1))
                return mm

            pe.wait_ge(s_A, 2)
            carries(0)
            for g in range(NG):
                if g + 1 < NG:
                    carries(g + 1)
                if g >= 1:
                    ranks(g - 1)
                pe.wait_ge(s_wat, g + 1)
                for t in range(0, GRP, 2):
                    w = min(2, GRP - t)
                    for q in range(w):
                        for k in range(KD):
                            mm = T.transpose(ps[(t // 2) % 2][:, (q * KD + k) * P:(q * KD + k + 1) * P], pr[g % 2][:, 0, t + q, k * P:(k + 1) * P], ident[:, :])
                    mm.then_inc(s_xnT, 1)
                    if t >= 2:
                        logits(g, t - 2)
                logits(g, GRP - 1).then_inc(s_lg, 1)
            ranks(NG - 1)
            def turn(s):
                for k in range(KD):
                    mm = T.transpose(ps[4][:, k * P:(k + 1) * P], xs[:, s, k * P:(k + 1) * P], ident[:, :])
                mm.then_inc(s_tx, 1)

            def up(s, e):
                for h in range(2):
                    for k in range(KD):
                        mm = T.matmul(ps[h][:, :], xsT[:, s, k, :], AR[:, bass.ds(e * (KD * HID) + (k * HID + h * 512), 512)],
                                      start=(k == 0), stop=(k == KD - 1))
                mm.then_inc(s_m1, 1)

            def turn_hidden():
                for m in range(MH):
                    mm = T.transpose(ps[2 + m // 4][:, (m % 4) * P:(m % 4 + 1) * P], hs[:, m * P:(m + 1) * P], ident[:, :])
                mm.then_inc(s_th, 1)

            def down(s, e):
                for m in range(MH):
                    mm = T.matmul(ps[5][:, 0:D], hsT[:, m, :], AR[:, bass.ds(e * (MH * D) + (NEX * KD * HID + m * D), D)],
                                  start=(m == 0), stop=(m == MH - 1))
                mm.then_inc(s_mm2, 1)

            pe.wait_ge(s_ew, 32 * NEX)
            pe.wait_ge(s_tiles, 1)
            pe.wait_ge(s_xs[0], 16)
            turn(0)
            pe.wait_ge(s_xt, 1)
            e0 = pe.value_load(reg[0:1, 0, 0:1], min_val=0, max_val=NEX - 1)
            up(0, e0)
            pe.wait_ge(s_xs[1], 16)
            turn(1)

            def two_tiles(i):
                for s in range(2):
                    t = i * 2 + s
                    e = pe.value_load(reg[0:1, 0, bass.ds(t, 1)], min_val=0, max_val=NEX - 1)
                    en = pe.value_load(reg[0:1, 0, bass.ds(i * 2 + (s + 1), 1)], min_val=0, max_val=NEX - 1)
                    pe.wait_ge(s_hc, i * 2 + (s + 1))
                    turn_hidden()
                    pe.wait_ge(s_xt, i * 2 + (s + 2))
                    up(1 - s, en)
                    pe.wait_ge(s_xs[s], i * 16 + 32)
                    turn(s)
                    pe.wait_ge(s_gl, i * 2 + (s + 1))
                    if not (isinstance(t, int) and t == 0):
                        pe.wait_ge(s_y, t)
                    down(s, e)

            two_tiles(0)
            with pe.Fori(1, SLOTS // 2 - 1) as i:
                two_tiles(i)
            for s in range(2):
                t = SLOTS - 2 + s
                e = pe.value_load(reg[0:1, 0, t:t + 1], min_val=0, max_val=NEX - 1)
                pe.wait_ge(s_hc, t + 1)
                turn_hidden()
                if s == 0:
                    en = pe.value_load(reg[0:1, 0, t + 1:t + 2], min_val=0, max_val=NEX - 1)
                    pe.wait_ge(s_xt, t + 2)
                    up(1, en)
                pe.wait_ge(s_gl, t + 1)
                pe.wait_ge(s_y, t)
                down(s, e)

        @block.vector
        def _(dve):
            dd = dve.drain
            V.memset(X[:, NT - 1, :], 0.0)
            V.memset(dstI[:, :], NP)
            V.memset(srcI[:, :], 0)
            V.memset(carry[:, :], 0.0)
            V.memset(adc[:, :], 0.0)
            V.memset(same[:, 0:1], 0.0)
            V.memset(same1[:, 0:1], 0.0)
            dd()
            V.memset(cnt[:, :, :], 0.0).then_inc(s_clear, 1)
            dve.wait_ge(s_edge, 32)
            dve.wait_ge(s_edge, 96)
            V.tensor_copy(dstF, dstI).then_inc(s_dstf, 1)
            V.tensor_copy(dst1[:, :], idx1[:, 1, :])
            dd()
            V.tensor_tensor(same[:, 1:C], dstF[:, 1:C], dstF[:, 0:C - 1], ALU.is_equal)
            V.tensor_tensor(same1[:, 1:J1], dst1[:, 1:J1], dst1[:, 0:J1 - 1], ALU.is_equal)
            for c, a in enumerate((dstF[:, C - 1:C], dst1[:, J1 - 1:J1], dstF[:, 0:1], dst1[:, 0:1])):
                V.tensor_scalar(ends[:, c:c + 1], a, 1.0, None, ALU.add)
            V.tensor_scalar(sml[:, 0:1], dstF[:, 0:1], float(NP - 1), None, ALU.min)
            dd()
            V.tensor_copy(ifirst[:, :], sml[:, 0:1])
            V.tensor_copy(ifirst1[:, :], dst1[:, 0:1])
            dve.wait_ge(s_w, 96)
            for c, (w, a) in enumerate(((0, 0), (1, 1), (0, 2), (1, 3))):
                to = (F, 2 * F + HD, 272, 280)[c]
                for k in range(KD):
                    dd()
                    V.tensor_tensor(scr[:, 0:F], Wc[:, k, ROWT * w:ROWT * w + F], att[:, a, :], ALU.mult)
                    dd()
                    V.tensor_reduce(Wc[:, k, to:to + HD], scr[:, 0:F].rearrange("p (h c) -> p h c", h=HD), AX.X, ALU.add)
            dd()
            dve.wait_ge(s_x, 16 * (NG + 1))
            for t in range(NT):
                V.bn_stats(ln[:, t, :], X[:, t, :])
            dd()
            for t in range(NT):
                V.bn_aggr(mv[:, t, :], ln[:, t, :])
            dd()
            V.tensor_scalar(mv[:, :, 1], mv[:, :, 1], EPS, None, ALU.add).then_inc(s_wc, 1)
            dd()
            V.tensor_scalar(sml[:, 1:2], mv[:, 0, 1:2], 0.0, None, ALU.add).then_inc(s_var, 1)
            dve.wait_ge(s_std, 1)
            V.reciprocal(rstd[:, :], rstd[:, :])
            dd()
            V.scalar_tensor_tensor(nmr[:, :], mv[:, :, 0], -1.0, rstd[:, :], ALU.mult, ALU.mult)
            dd()

            def keep(t):
                dve.wait_ge(s_row, t + 1)
                V.tensor_copy(asr[:, t, 0:8], row[:, t % 2, F:F + HD])
                V.tensor_copy(asr[:, t, 8:16], row[:, t % 2, 2 * F + HD:2 * F + 2 * HD])
                V.tensor_copy(adr[:, t, :], row[:, t % 2, 272:288]).then_inc(s_res, 1)

            def within(t):
                dve.wait_ge(s_blk[t % 7], 16 * (t // 7 + 1))
                V.tensor_scalar(blkrow[t % 7], blkrow[t % 7], nid[:, t:t + 1], None, ALU.is_le, ALU.add, accum_out=cnt[:, 1, t:t + 1]).then_inc(s_blkc, 1)

            dve.wait_ge(s_blkp, 1)
            for t in range(NT):
                if t >= 1:
                    dd()
                V.tensor_scalar(scr[:, 0:NBLK], ps[6][:, 0:NBLK], nid[:, t:t + 1], None, ALU.is_le, ALU.add, accum_out=cnt[:, 0, t:t + 1])
            dd()
            V.tensor_scalar(cnt[:, 0, :], cnt[:, 0, :], -1.0, 0.0, ALU.add, ALU.max)
            dd()
            V.tensor_copy(icnt[:, 0, :], cnt[:, 0, :]).then_inc(s_bidx, 1)
            for t in range(NT):
                if t >= 2:
                    dve.wait_ge(s_tr, t - 1)
                V.tensor_scalar(hrow[:, t % 2, :], X[:, t, :], rstd[:, t:t + 1], nmr[:, t:t + 1], ALU.mult, ALU.add).then_inc(s_h, 1)
                if t >= 2:
                    keep(t - 2)
                if t >= 3:
                    within(t - 3)
            keep(NT - 2)
            keep(NT - 1)
            for t in range(NT - 3, NT):
                within(t)
            dd()
            V.scalar_tensor_tensor(cnt[:, 2, :], cnt[:, 0, :], float(BLK), cnt[:, 1, :], ALU.mult, ALU.add).then_inc(s_cnt, 1)
            dve.wait_ge(s_cntp, 1)
            V.tensor_copy(cnt[:, 3, :], ps[7][:, 0:NT])
            dd()
            V.tensor_tensor(cnt[:, 4, :], cnt[:, 2, :], cnt[:, 3, :], ALU.subtract)
            dd()
            V.tensor_scalar(scr[:, 0:NT], cnt[:, 4, :], 0.0, float(SKIP), ALU.is_equal, ALU.mult)
            dd()
            V.tensor_tensor(scr[:, 0:NT], scr[:, 0:NT], cnt[:, 3, :], ALU.add)
            dd()
            V.tensor_copy(icnt[:, 1, :], scr[:, 0:NT]).then_inc(s_start, 1)
            dd()
            fin_ = scr[:, 64:64 + 8 * NT].rearrange("p (k t) -> p k t", k=8)
            for k in range(2):
                top_ = float(EP if k == 0 else N)
                cc = C if k == 0 else J1
                V.tensor_scalar(fin_[:, 0, :], cnt[:, 2, :], top_, None, ALU.min)
                V.tensor_scalar(fin_[:, 1, :], cnt[:, 3, :], top_, None, ALU.min)
                dd()
                V.tensor_tensor(fin_[:, 2, :], fin_[:, 0, :], fin_[:, 1, :], ALU.is_gt)
                V.tensor_scalar(fin_[:, 3, :], fin_[:, 0, :], -1.0, 0.0, ALU.add, ALU.max)
                dd()
                V.tensor_copy(icnt[:, 2 + k, :], fin_[:, 3, :])
                V.tensor_scalar(bare[:, k, 0, :], fin_[:, 2, :], -1.0, BIG, ALU.add, ALU.mult)
                V.tensor_scalar(fin_[:, 4, :], fin_[:, 3, :], 1.0 / cc, -0.5 + 0.5 / cc, ALU.mult, ALU.add)
                dd()
                V.tensor_scalar(fin_[:, 4, :], fin_[:, 4, :], MAGIC, None, ALU.add)
                dd()
                V.tensor_scalar(fin_[:, 4, :], fin_[:, 4, :], MAGIC, None, ALU.subtract)
                dd()
                V.tensor_scalar(fin_[:, 5, :], fin_[:, 4, :], float(cc), None, ALU.mult)
                dd()
                V.tensor_tensor(fin_[:, 5, :], fin_[:, 1, :], fin_[:, 5, :], ALU.is_lt)
                dd()
                V.tensor_tensor(fin_[:, 5, :], fin_[:, 5, :], fin_[:, 2, :], ALU.mult)
                dd()
                V.tensor_scalar(bare[:, k, 1, :], fin_[:, 5, :], -1.0, BIG, ALU.add, ALU.mult)
                V.tensor_tensor(fin_[:, 5, :], fin_[:, 5, :], fin_[:, 4, :], ALU.mult)
                dd()
                V.tensor_scalar(cnt[:, 5 + k, :], fin_[:, 5, :], -1.0, None, ALU.add)
                dd()
            dve.wait_ge(s_linkp, 1)
            V.tensor_tensor(sml[:, 2:4], ps[6][:, 0:2], ends[:, 2:4], ALU.is_equal)
            V.tensor_tensor(sml[:, 4:6], ends[:, 0:2], ends[:, 2:4], ALU.is_equal)
            dd()
            V.tensor_tensor(sml[:, 8:10], sml[:, 2:4], sml[:, 4:6], ALU.mult).then_inc(s_link, 1)
            V.tensor_tensor(zs[:, :, :], asr[:, :, :], adr[:, :, :], ALU.add)
            dd()
            V.scalar_tensor_tensor(zs[:, :, :], zs[:, :, :], 0.2, zs[:, :, :], ALU.mult, ALU.max)

            def scan_batch(Gs, n, smask, adv, b_exp, s_in, s_up, weight):
                z, r, w = Z[:, 0:n, :], DW[:, 0, 0:n, :], DW[:, 1, 0:n, :]
                ng = neg[:, 0:n]
                V.tensor_scalar(ng, smask, -1.0, BIG, ALU.add, ALU.mult)
                V.tensor_tensor(z, Gs[:, :, F:ROWT], adv, ALU.add)
                dd()
                V.scalar_tensor_tensor(z, z, 0.2, z, ALU.mult, ALU.max)
                dd()
                if weight is not None:
                    V.tensor_tensor(z, z, bc(dneg[:, 0:n].unsqueeze(2), [P, n, HD]), ALU.add)
                    dd()
                for h in range(HD):
                    V.tensor_tensor_scan(Gs[:, :, ROWT + h], ng, z[:, :, h], carry[:, ROWT + h:ROWT + h + 1], ALU.add, ALU.max)
                dd()
                m = Gs[:, :, ROWT:ROWS]
                V.tensor_tensor(r[:, 1:n, :], m[:, 0:n - 1, :], m[:, 1:n, :], ALU.subtract)
                V.tensor_tensor(r[:, 0, :], carry[:, ROWT:ROWS], m[:, 0, :], ALU.subtract)
                V.tensor_tensor(w, z, m, ALU.subtract)
                dd()
                V.tensor_tensor(r, r, bc(ng.unsqueeze(2), [P, n, HD]), ALU.add).then_inc(s_up, 1)
                b_exp()
                if weight is not None:
                    V.tensor_tensor(w, w, bc(weight.unsqueeze(2), [P, n, HD]), ALU.mult)
                    dd()
                V.tensor_tensor(Gs[:, :, 0:F].rearrange("p j (h c) -> p j h c", h=HD), Gs[:, :, 0:F].rearrange("p j (h c) -> p j h c", h=HD),
                                bc(w.unsqueeze(3), [P, n, HD, CH]), ALU.mult)
                for h in range(HD):
                    V.tensor_tensor_scan(Gs[:, :, F + h], r[:, :, h], w[:, :, h], carry[:, F + h:F + h + 1], ALU.mult, ALU.add)
                dd()
                for f in range(F):
                    V.tensor_tensor_scan(Gs[:, :, f], r[:, :, f // CH], Gs[:, :, f], carry[:, f:f + 1], ALU.mult, ALU.add)
                dd()

            def spread(k, s, n):
                for h in range(HD):
                    V.tensor_tensor_scan(adx[:, 0:n, h], neg[:, 0:n], adin[:, s, 0:n, k, h], adc[:, h:h + 1], ALU.mult, ALU.add)
                dd()

            dve.wait_ge(s_deg1, 16)
            V.tensor_scalar(dneg[:, :], deg1[:, :], 0.0, -BIG, ALU.is_equal, ALU.mult)
            V.tensor_copy(neg[:, 0:J1], same1[:, :])
            dve.wait_ge(s_ad1, 16)
            dve.wait_ge(s_adf, 32)
            V.tensor_copy(adin[:, 1, 0, 1, :], adf[:, 1, HD:2 * HD])
            dd()
            spread(1, 1, J1)
            dve.wait_ge(s_g1, 16 * J1)
            scan_batch(G[1][:, 0:J1, :], J1, same1[:, :], adx[:, 0:J1, :],
                       lambda: dve.wait_ge(s_e1, 1), None, s_c1, deg1[:, :])
            V.tensor_copy(last1, G[1][:, J1 - 1, :]).then_inc(s_d1, 1)
            dd()

            with dve.Fori(0, NB // 2) as i:
                for s in range(2):
                    b = i * 2 + s
                    hold(dve, 4, s_ad[s], i * 16 + 16)
                    sm = same[:, bass.ds(b * J, J)]
                    V.tensor_copy(neg[:, :], sm)
                    dd()
                    spread(0, s, J)
                    V.tensor_copy(adc[:, :], adx[:, J - 1, :])
                    hold(dve, 4, s_g[s], (i + 1) * (16 * J))
                    scan_batch(G[s], J, neg[:, :], adx[:, :, :], lambda: hold(dve, 4, s_exp, i * 2 + (s + 1)), None, s_dif, None)
                    V.tensor_copy(carry[:, :], G[s][:, J - 1, :]).then_inc(s_done, 1)
                    dd()

            for k, a in enumerate((carry, last1)):
                for q in range(2):
                    V.tensor_copy(rep[:, k, q, :].rearrange("p (h c) -> p h c", h=HD),
                                  bc(a[:, F + HD * q:F + HD * (q + 1)].unsqueeze(2), [P, HD, CH]))
            dd()
            V.memset(sml[:, 1:2], 0.0).then_inc(s_rep, 1)
            for k in range(2):
                dve.wait_ge(s_cp, k + 1)
                V.tensor_copy(cT.rearrange("p k e -> p (k e)"), ps[0][:, :])
                dd()
                V.tensor_scalar(cT[:, 0, :], cT[:, 0, :], -1.0, BIG, ALU.add, ALU.mult)
                dd()
                V.tensor_tensor_scan(cS[:, 0, :], cT[:, 0, :], cT[:, 1, :], 0.0, ALU.add, ALU.max)
                V.memset(cD[:, 0, 0:1], 0.0)
                dd()
                V.tensor_tensor(cD[:, 0, 1:P], cS[:, 0, 0:P - 1], cS[:, 0, 1:P], ALU.subtract)
                V.tensor_tensor(cD[:, 1, :], cT[:, 1, :], cS[:, 0, :], ALU.subtract)
                dd()
                V.tensor_tensor(cD[:, 0, :], cD[:, 0, :], cT[:, 0, :], ALU.add).then_inc(s_cdif, 1)
                dve.wait_ge(s_cexp, k + 1)
                for q in (2, 3):
                    V.tensor_tensor(cT[:, q, :], cT[:, q, :], cD[:, 1, :], ALU.mult)
                dd()
                V.tensor_tensor_scan(cS[:, 1, :], cD[:, 0, :], cT[:, 2, :], 0.0, ALU.mult, ALU.add)
                V.tensor_tensor_scan(cS[:, 2, :], cD[:, 0, :], cT[:, 3, :], 0.0, ALU.mult, ALU.add)
                dd()
                V.memset(sml[:, 1:2], 0.0).then_inc(s_cs, 1)
                dve.wait_ge(s_cb, k + 1)
                V.tensor_copy(At[:, k, 0:F], ps[1][:, 2 * P:3 * P])
                V.tensor_copy(At[:, k, F:ROWT], ps[1][:, P:2 * P].rearrange("p (h c) -> p h c", h=HD)[:, :, 0])
                V.tensor_copy(At[:, k, ROWT:ROWS], ps[1][:, 0:P].rearrange("p (h c) -> p h c", h=HD)[:, :, 0])
                dd()
                if k == 0:
                    V.tensor_copy(sml[:, 1:2], sml[:, 8:9]).then_inc(s_fidx, 1)
                V.tensor_copy(sml[:, 2:3], sml[:, 8:9]).then_inc(s_A, 1)
                dd()

            dve.wait_ge(s_par, 16 * (7 + NEX))

            def layer_stats(src_, g, q):
                for t in range(GRP):
                    V.bn_stats(fln[:, t, :], src_[:, t, :])
                dd()
                for t in range(GRP):
                    V.bn_aggr(fmv[:, t, :], fln[:, t, :])
                dd()
                V.tensor_scalar(fmv[:, :, 1], fmv[:, :, 1], EPS, None, ALU.add).then_inc(s_fs, 1)
                dve.wait_ge(s_fsq, 2 * g + q + 1)
                V.reciprocal(frs[:, 1, :], frs[:, 0, :])
                dd()
                V.scalar_tensor_tensor(frs[:, 2, :], fmv[:, :, 0], -1.0, frs[:, 1, :], ALU.mult, ALU.mult).then_inc(s_m2w, 1)

            def shares(g):
                z = fz[:, g % 2]
                sg, cg = stg[:, g % 2], cgr[:, g % 2]
                gt = slice(g * GRP, (g + 1) * GRP)
                for m in range(GRP):
                    n = g * GRP + m
                    dve.wait_ge(s_oh, n + 1)
                    if n >= 2:
                        dve.wait_ge(s_cg, n - 1)
                    V.tensor_scalar(oh[:, n % 2, :], ps[2 + n % 2][:, 0:2 * P], pidx[:, 0:1], None, ALU.is_equal).then_inc(s_ohs, 1)
                dve.wait_ge(s_fg[g % 2], 16 * 2 * GRP * (g // 2 + 1))
                dve.wait_ge(s_cgs, GRP * (g + 1))
                for k in range(2):
                    for q, a in enumerate((sg, cg)):
                        V.tensor_tensor(z[:, q, k, :, :], a[:, k, :, ROWT:ROWS], bc(bare[:, k, q, gt].unsqueeze(2), [P, GRP, HD]), ALU.add)
                dd()
                zk = zs[:, gt, :].rearrange("p t (k h) -> p k t h", k=2)
                V.tensor_tensor(z[:, 3], z[:, 0], z[:, 1], ALU.max)
                dd()
                V.tensor_tensor(z[:, 3], z[:, 3], zk, ALU.max)
                dd()
                for q in range(2):
                    V.tensor_tensor(z[:, q], z[:, q], z[:, 3], ALU.subtract)
                V.tensor_tensor(z[:, 2], zk, z[:, 3], ALU.subtract).then_inc(s_fe, 1)

            def choose(g):
                dve.wait_ge(s_lg, g + 1)
                V.tensor_tensor(rt[:, 0, :, :], ps[6][:, 0:GRP * NEX].rearrange("p (t e) -> p t e", e=NEX), bc(bgb[:, :].unsqueeze(1), [P, GRP, NEX]), ALU.add).then_inc(s_lgc, 1)
                dd()
                for t in range(GRP):
                    V.max(top[:, t, :], rt[:, 0, t, :])
                dd()
                for t in range(GRP):
                    V.max_index(tix[:, t, :], top[:, t, :], rt[:, 0, t, :])
                V.tensor_tensor(wts[:, 0, :], top[:, :, 1], top[:, :, 0], ALU.subtract).then_inc(s_m2, 1)
                dd()
                V.tensor_copy(pos[:, :, :], tix[:, :, 0:2].rearrange("p t k -> p k t"))
                dd()
                for k in range(2):
                    V.tensor_tensor(rt[:, 1 + k, :, :], bc(pos[:, k, :].unsqueeze(2), [P, GRP, NEX]), bc(e8[:, :].unsqueeze(1), [P, GRP, NEX]), ALU.is_equal)
                dd()
                V.tensor_tensor(rt[:, 3, :, :], rt[:, 1, :, :], rt[:, 2, :, :], ALU.add)
                dd()
                if g == NG - 1:
                    V.tensor_scalar(rt[:, 3, GRP - 1, :], rt[:, 3, GRP - 1, :], pcol[:, 0:1], None, ALU.mult)
                    dd()
                V.memset(sml[:, 5:6], 0.0).then_inc(s_mask, 1)

            def settle(g):
                dve.wait_ge(s_m2e, g + 1)
                V.tensor_scalar(wts[:, 1, :], wts[:, 0, :], 1.0, None, ALU.add)
                dve.wait_ge(s_rank, g + 1)
                for e in range(NEX):
                    V.tensor_tensor_scan(rt[:, 4, :, e], bc(ones[:, 0:1], [P, GRP]), ps[7][:, GRP * NEX:2 * GRP * NEX].rearrange("p (t e) -> p t e", e=NEX)[:, :, e],
                                         tot[:, e:e + 1], ALU.mult, ALU.add)
                dd()
                V.reciprocal(wts[:, 1, :], wts[:, 1, :])
                V.tensor_tensor(rt[:, 5, :, :], rt[:, 4, :, :], ps[7][:, GRP * NEX:2 * GRP * NEX].rearrange("p (t e) -> p t e", e=NEX), ALU.subtract)
                V.tensor_copy(tot[:, :], rt[:, 4, GRP - 1, :])
                dd()
                V.tensor_tensor(rt[:, 5, :, :], rt[:, 5, :, :], ps[7][:, 0:GRP * NEX].rearrange("p (t e) -> p t e", e=NEX), ALU.add)
                V.tensor_tensor(wts[:, 2, :], wts[:, 0, :], wts[:, 1, :], ALU.mult)
                dd()
                V.tensor_tensor(rt[:, 5, :, :], rt[:, 5, :, :], bc(e8r[:, :].unsqueeze(1), [P, GRP, NEX]), ALU.add)
                dd()
                for k in range(2):
                    V.tensor_tensor(rt[:, 1 + k, :, :], rt[:, 1 + k, :, :], rt[:, 5, :, :], ALU.mult)
                dd()
                V.tensor_reduce(pos[:, :, :], rt[:, 1:3, :, :], AX.X, ALU.add)
                dve.wait_ge(s_prx, 2 * g + 2)
                for k in range(2):
                    V.tensor_copy(pr[g % 2][:, k, :, D], nid[:, g * GRP:(g + 1) * GRP])
                    V.tensor_copy(pr[g % 2][:, k, :, D + 1], wts[:, 1 + k, :])
                dd()
                if g == NG - 1:
                    V.tensor_scalar(pcol[:, :], pcol[:, :], -1.0, -float(SKIP), ALU.add, ALU.mult)
                    dd()
                    V.tensor_scalar(pos[:, :, GRP - 1], pos[:, :, GRP - 1], pcol[:, 0:1], None, ALU.add)
                    dd()
                if g >= 2:
                    dve.wait_ge(s_place[g % 2], 16 * 2 * GRP * (g // 2))
                V.tensor_copy(ipos[:, g % 2, :, :], pos[:, :, :]).then_inc(s_pos, 1)
                dd()

            def combine(g):
                gt = slice(g * GRP, (g + 1) * GRP)
                z = fz[:, g % 2]
                sg, cg, xw = stg[:, g % 2], cgr[:, g % 2], xwg[:, g % 2]
                dve.wait_ge(s_fexp, g + 1)
                V.tensor_scalar(z[:, 2, 1], z[:, 2, 1], 2.0, None, ALU.mult)
                V.tensor_tensor(z[:, 3], sg[:, :, :, F:ROWT], z[:, 0], ALU.mult)
                V.tensor_tensor(z[:, 4], cg[:, :, :, F:ROWT], z[:, 1], ALU.mult)
                dd()
                V.tensor_tensor(z[:, 3], z[:, 3], z[:, 4], ALU.add)
                dd()
                V.tensor_tensor(z[:, 3], z[:, 3], z[:, 2], ALU.add)
                dd()
                V.reciprocal(z[:, 4], z[:, 3])
                dd()
                for q in range(3):
                    V.tensor_tensor(z[:, q], z[:, q], z[:, 4], ALU.mult)
                dd()
                dve.wait_ge(s_fx[g % 2], 32 * (g // 2 + 1))

                def heads(a, k):
                    return a.rearrange("p t (h c) -> p t h c", h=HD) if k is None else a[:, :, k * F:(k + 1) * F].rearrange("p t (h c) -> p t h c", h=HD)

                for q, (to, a) in enumerate(((og, sg), (tg, cg))):
                    for k in range(2):
                        V.tensor_tensor(heads(to, k), heads(a[:, k, :, 0:F], None), bc(z[:, q, k].unsqueeze(3), [P, GRP, HD, CH]), ALU.mult)
                dd()
                V.tensor_tensor(og, og, tg, ALU.add)
                dd()
                for k in range(2):
                    V.tensor_tensor(heads(tg, k), heads(xw[:, k, :, 0:F], None), bc(z[:, 2, k].unsqueeze(3), [P, GRP, HD, CH]), ALU.mult)
                dve.wait_ge(s_hb, g + 1)
                V.tensor_tensor(hb, hb, bc(b01[:, :].unsqueeze(1), [P, GRP, D]), ALU.add)
                dd()
                V.tensor_tensor(og, og, tg, ALU.add)
                dd()
                V.tensor_tensor(og, og, hb, ALU.add).then_inc(s_xb, 1)
                dd()
                layer_stats(og, g, 0)
                V.tensor_tensor(X[:, gt, :], X[:, gt, :], bc(bet[:, :].unsqueeze(1), [P, GRP, D]), ALU.add)
                dve.wait_ge(s_prx, 2 * g + 1)
                V.tensor_tensor(og, og, bc(gam[:, :].unsqueeze(1), [P, GRP, D]), ALU.mult)
                dd()
                V.tensor_tensor(X[:, gt, :], X[:, gt, :], og, ALU.add).then_inc(s_x1, 1)
                dd()
                layer_stats(X[:, gt, :], g, 1)
                dd()
                V.memset(sml[:, 5:6], 0.0).then_inc(s_fgrp, 1)

            V.tensor_scalar(pcol[:, :], pidx[:, :], float(TAIL), None, ALU.is_lt)
            V.tensor_scalar(e8r[:, :], e8[:, :], float(REG), None, ALU.mult)
            V.tensor_scalar(padrow[:, D:D + 1], pidx[:, :], float(NP), None, ALU.add).then_inc(s_pz, 1)
            shares(0)
            for g in range(NG):
                if g + 1 < NG:
                    shares(g + 1)
                if g >= 1:
                    choose(g - 1)
                    settle(g - 1)
                combine(g)
            choose(NG - 1)
            settle(NG - 1)
            V.tensor_scalar(toff[:, 0, :], tot[:, :], 1.0 / P, 0.5 - 0.5 / P, ALU.mult, ALU.add)
            V.tensor_tensor(toff[:, 3, :], tot[:, :], e8r[:, :], ALU.add)
            dd()
            V.tensor_scalar(toff[:, 3, :], toff[:, 3, :], pidx[:, 0:1], None, ALU.add)
            V.tensor_scalar(toff[:, 0, :], toff[:, 0, :], MAGIC, None, ALU.add)
            dd()
            V.tensor_copy(ipad[:, :], toff[:, 3, :])
            V.tensor_scalar(toff[:, 0, :], toff[:, 0, :], MAGIC, None, ALU.subtract)
            dd()
            V.tensor_scalar(toff[:, 0, :], toff[:, 0, :], float(P), None, ALU.mult)
            dd()
            V.tensor_tensor_scan(toff[:, 1, :], bc(ones[:, 0:1], [P, NEX]), toff[:, 0, :], 0.0, ALU.mult, ALU.add)
            V.tensor_scalar(toff[:, 2, :], toff[:, 0, :], -1.0, float(REG), ALU.mult, ALU.add)
            V.memset(tile_e[:, 0, :], 0.0)
            V.tensor_copy(tile_e[:, 1, :], slot_id[:, :])
            dd()
            for e in range(NEX):
                V.tensor_scalar(tile_e[:, 2, :], slot_id[:, :], toff[0:1, 1, e:e + 1], None, ALU.is_ge)
                dd()
                if e < NEX - 1:
                    V.tensor_tensor(tile_e[:, 0, :], tile_e[:, 0, :], tile_e[:, 2, :], ALU.add)
                    V.scalar_tensor_tensor(tile_e[:, 1, :], tile_e[:, 2, :], toff[0:1, 2, e:e + 1], tile_e[:, 1, :], ALU.mult, ALU.add)
                else:
                    V.scalar_tensor_tensor(tile_e[:, 2, :], tile_e[:, 2, :], float(NEX * REG), tile_e[:, 1, :], ALU.mult, ALU.max)
                dd()
            V.tensor_scalar(tile_e[:, 2, :], tile_e[:, 2, :], float(NEX * REG), None, ALU.min)
            dd()
            V.tensor_copy(reg[:, 0, :], tile_e[:, 0, :])
            V.tensor_copy(reg[:, 1, :], tile_e[:, 2, :]).then_inc(s_tiles, 1)
            dd()

            def turned(s, value):
                dve.wait_ge(s_tx, value)
                V.tensor_copy(xsT[:, s, :, :], ps[4][:, 0:D].rearrange("p (k t) -> p k t", k=KD)).then_inc(s_xt, 1)

            def hidden(value):
                dve.wait_ge(s_m1, value)
                V.tensor_copy(hs[:, 0:512], ps[0][:, :])
                V.tensor_copy(hs[:, 512:1024], ps[1][:, :]).then_inc(s_hc, 1)

            def bias_of(t):
                e = dve.value_load(reg[0:1, 0, t], min_val=0, max_val=NEX - 1)
                V.tensor_copy(bcur[:, :], eb1T[:, bass.ds(e, 1), :].rearrange("p a m -> p (a m)")).then_inc(s_bc, 1)

            def rows_of(s):
                V.tensor_copy(idb[:, s, :], xs[:, s, D:D + 1])
                V.tensor_copy(wb[:, s, :], xs[:, s, D + 1:D + 2]).then_inc(s_idw, 1)

            def two_answers(i, ends_here=False):
                first = isinstance(i, int) and i == 0
                for s in range(2):
                    t = i * 2 + s
                    last = ends_here and s == 1
                    if not last:
                        dve.wait_ge(s_th, t + 1)
                        hidden(t + 2)
                        if not ends_here:
                            turned(s, t + 3)
                        hold(dve, 4, s_gl, t + 1)
                        bias_of(slice(t + 1, t + 2) if isinstance(t, int) else bass.ds(t + 1, 1))
                    e = dve.value_load(reg[0:1, 0, slice(t, t + 1) if isinstance(t, int) else bass.ds(t, 1)], min_val=0, max_val=NEX - 1)
                    dve.wait_ge(s_mm2, t + 1)
                    if not first:
                        dve.wait_ge(s_add, (t - 1) * 16)
                    V.tensor_tensor(ys[:, s, :], ps[5][:, 0:D], eb2b[:, bass.ds(e, 1), :].rearrange("p a d -> p (a d)"), ALU.add)
                    dd()
                    V.tensor_scalar(ys[:, s, :], ys[:, s, :], wb[:, s, 0:1], None, ALU.mult).then_inc(s_y, 1)
                    if not last:
                        hold(dve, 4, s_xs[1 - s], (i + (1 + s)) * 16 if s or not first else 16)
                        if not (first and s == 0):
                            hold(dve, 4, s_add, t * 16)
                        rows_of(1 - s)

            turned(0, 1)
            hidden(1)
            turned(1, 2)
            bias_of(slice(0, 1))
            dve.wait_ge(s_xs[0], 16)
            rows_of(0)
            two_answers(0)
            with dve.Fori(1, SLOTS // 2 - 1) as i:
                two_answers(i)
            two_answers(SLOTS // 2 - 1, ends_here=True)


_INS = ["x", "src", "dst", "L0_gnn_W0", "L0_gnn_as0", "L0_gnn_ad0", "L0_gnn_b0", "L0_gnn_W1", "L0_gnn_as1", "L0_gnn_ad1",
        "L0_gnn_b1", "L0_gnn_gamma", "L0_gnn_beta", "L0_ffn_Wg", "L0_ffn_bg", "L0_ffn_W1", "L0_ffn_b1", "L0_ffn_W2", "L0_ffn_b2"]


def kernel(**inputs):
    import concourse.bacc as bacc
    from concourse.bass_utils import run_bass_kernel_spmd as run

    nc = bacc.Bacc("TRN2", target_bir_lowering=False, num_devices=1)
    arrays, args = {}, []
    for name in _INS:
        a = np.ascontiguousarray(inputs[name])
        arrays[f"in_{name}"] = a
        args.append(nc.dram_tensor(f"in_{name}", a.shape, mybir.dt.from_np(a.dtype), kind="ExternalInput").ap())
    args.append(nc.dram_tensor("out_0", (N, D), F32, kind="ExternalOutput").ap())
    build(nc, *args)
    r = run(nc, [arrays], core_ids=[0])
    return r.results[0]["out_0"]
```

```python
from contextlib import ExitStack

import numpy as np
import concourse.bass as bass
from concourse import mybir

F32 = mybir.dt.float32
I32 = mybir.dt.int32
ALU = mybir.AluOpType
ACT = mybir.ActivationFunctionType
AX = mybir.AxisListType

P = 128
N = 6250
D = 256
NT = -(-N // P)
NP = NT * P
TAIL = N - (NT - 1) * P
E = 206250
HD = 8
CH = 16
F = HD * CH
C = -(-E // P)
EP = C * P
J = 62
NB = C // J
PARTS = ((0, 38), (38, J - 38))
J1 = NP // P
ROWT = F + HD
ROWS = F + 2 * HD
BLK = 512
NBLK = EP // BLK
BIG = 1e30
NEX = 8
HID = 1024
KD = D // P
MH = HID // P
SLOTS = (2 * N + NEX * (P - 1)) // P
SKIP = 1 << 20
EPS = 1e-5
RB = 4
GRP = 7
NG = NT // GRP
GW = 2 * J * ROWS
REG = NP + P
ROWP = D + 2
AW = 37904
EARLY1 = 6
EARLY = 4
MAGIC = 12582912.0

LAG = GRP + 4

assert SLOTS % 2 == 1
assert NB * J == C and NBLK * BLK == EP and NG * GRP == NT and NB % 2 == 0 and J1 <= J


def bc(ap, shape):
    return ap.to_broadcast(shape)


def build(nc, x, src, dst, W0, as0, ad0, b0, W1, as1, ad1, b1, gamma, beta, Wg, bg, eW1, eb1, eW2, eb2, out):
    ctx = ExitStack()
    with ctx:
        def sb(name, shape, dt=F32):
            return ctx.enter_context(nc.sbuf_tensor(name, shape, dt))

        def sem(name):
            return ctx.enter_context(nc.semaphore(name))

        def dram(name, shape, dt=F32):
            return nc.dram_tensor(name, shape, dt, kind="Internal").ap()

        tab = [dram("tab0", [NP, ROWT]), dram("tab1", [NP, ROWT])]
        adt = dram("adt", [NP, 2 * HD])
        srcp = dram("srcp", [P, C], I32)
        dstp = dram("dstp", [P, C])
        adstart = dram("adstart", [EP, 2 * HD])
        state = [dram("state0", [EP, ROWS]), dram("state1", [NP, ROWS])]
        degd = dram("degd", [NP, 1])
        hbd = dram("hbd", [NP, D])
        placed = dram("placed", [NEX * REG + P, ROWP])
        states0 = state[0].rearrange("(p j) r -> p (j r)", p=P)
        adstart_c = adstart.rearrange("(p j) r -> p (j r)", p=P)

        AR = sb("AR", [P, AW])
        G = [AR[:, s * J * ROWS:(s + 1) * J * ROWS].rearrange("p (j r) -> p j r", r=ROWS) for s in range(2)]
        X = AR[:, GW:GW + NT * D].rearrange("p (t d) -> p t d", d=D)
        FB = GW + NT * D
        zero = sb("zero", [P, 1024])
        ident = sb("ident", [P, P])
        ones = sb("ones", [P, P])
        shf = sb("shf", [P, P])
        wrap = sb("wrap", [P, P])
        tri = sb("tri", [P, P])
        pidx = sb("pidx", [P, 1])
        pcol = sb("pcol", [P, 1])
        nid = sb("nid", [P, NT])
        nidh = sb("nidh", [P, NT])
        e8 = sb("e8", [P, HD])
        b01 = sb("b01", [P, D])
        gam = sb("gam", [P, D])
        bet = sb("bet", [P, D])
        wg = sb("wg", [P, KD, NEX])
        bgb = sb("bgb", [P, NEX])
        eb1T = sb("eb1T", [P, NEX, MH])
        eb2b = sb("eb2b", [P, NEX, D])
        mv = sb("mv", [P, NT, 2])
        rstd = sb("rstd", [P, NT])
        nmr = sb("nmr", [P, NT])
        hT4 = sb("hT4", [P, 2, 2 * D])
        hT = hT4[:, :, 0:D]
        asrc_all = sb("asrc_all", [P, NT, 16])
        adst_all = sb("adst_all", [P, NT, 16])
        same1 = sb("same1", [P, J1])
        ends = sb("ends", [P, 8])
        idx = sb("idx", [P, 2, J], I32)
        neg = sb("neg", [P, J])
        carry = sb("carry", [P, ROWS])
        idx1 = sb("idx1", [P, 2, J1], I32)
        dst1 = sb("dst1", [P, J1])
        deg1 = sb("deg1", [P, J1])
        dneg = sb("dneg", [P, J1])
        ifirst = sb("ifirst", [P, 1], I32)
        node_count = sb("node_count", [P, 8, NT])
        carry_tab = sb("carry_tab", [P, 2, ROWS])
        blk = sb("blk", [1, NBLK])
        sml = sb("sml", [P, 16])
        bcur = sb("bcur", [P, 2, MH])

        hrow = sb("hrow", [P, 2, D])
        node_index = sb("node_index", [P, 4, NT], I32)
        adst_carry = sb("adst_carry", [P, HD])
        chunk_adst = sb("chunk_adst", [P, 2, 2 * HD])
        ifirst1 = sb("ifirst1", [P, 1], I32)
        one_hot_of = sb("one_hot_of", [P, 2, 2 * P])
        share_of = sb("share_of", [P, 2, 5, 2, GRP, HD])
        group_stats = sb("group_stats", [P, GRP, 6])
        group_mv = sb("group_mv", [P, GRP, 2])
        group_scale = sb("group_scale", [P, 3, GRP])
        gate_w = sb("gate_w", [P, 3, GRP])
        pos = sb("pos", [P, 2, GRP])
        ipos = sb("ipos", [P, 2, 2, GRP], I32)
        tot = sb("tot", [P, NEX])
        toff = sb("toff", [P, 4, NEX])
        ipad = sb("ipad", [P, NEX], I32)
        padrow = sb("padrow", [P, ROWP])
        e8r = sb("e8r", [P, NEX])
        slot_id = sb("slot_id", [1, SLOTS])
        tile_e = sb("tile_e", [1, 3, SLOTS])
        reg = sb("reg", [1, 2, SLOTS], I32)
        idb = sb("idb", [P, 2, 1], I32)
        wb = sb("wb", [P, 2, 1])

        ps = [ctx.enter_context(nc.psum_tensor(f"ps{i}", [P, 512], F32)) for i in range(8)]

        held = [sem(f"held{i}") for i in range(5)]
        constants_made = sem("constants_made")
        inputs_cleared = sem("inputs_cleared")
        x_loaded = [sem(f"x_loaded{g}") for g in range(NG)]
        proj_weights_loaded = sem("proj_weights_loaded")
        dst_loaded = sem("dst_loaded")
        edges_loaded = sem("edges_loaded")
        norm_scales_ready = sem("norm_scales_ready")
        norm_again_ready = sem("norm_again_ready")
        node_half_ready = sem("node_half_ready")
        biased_ready = sem("biased_ready")
        biased_stored = [sem("biased_stored_a"), sem("biased_stored_b")]
        params_loaded = sem("params_loaded")
        zeros_stored = sem("zeros_stored")
        att_weights_ready = sem("att_weights_ready")
        variances_ready = sem("variances_ready")
        deviations_ready = sem("deviations_ready")
        norm_ready = sem("norm_ready")
        norm_turned = sem("norm_turned")
        norm_turned_copied = sem("norm_turned_copied")
        projected = sem("projected")
        row_copied = sem("row_copied")
        row_kept = sem("row_kept")
        row_stored = [sem(f"row_stored{q}") for q in range(RB)]
        adst_stored = sem("adst_stored")
        dst_numbers_ready = sem("dst_numbers_ready")
        dst_numbers_stored = sem("dst_numbers_stored")
        src_stored = sem("src_stored")
        block_firsts_loaded = sem("block_firsts_loaded")
        block_firsts_spread = sem("block_firsts_spread")
        block_found = sem("block_found")
        block_gathered = [sem(f"block_gathered{i}") for i in range(GRP)]
        block_counted = sem("block_counted")
        counts_ready = sem("counts_ready")
        counts_shifted = sem("counts_shifted")
        starts_ready = sem("starts_ready")
        adst_scattered = sem("adst_scattered")
        chunk_adst_gathered = sem("chunk_adst_gathered")
        chunk_adst_patched = sem("chunk_adst_patched")
        degrees_stored = sem("degrees_stored")
        degrees_loaded = sem("degrees_loaded")
        conv2_gathered = sem("conv2_gathered")
        last_part_gathered = sem("last_part_gathered")
        conv2_diffs_ready = sem("conv2_diffs_ready")
        conv2_exps_ready = sem("conv2_exps_ready")
        conv2_states_ready = sem("conv2_states_ready")
        conv2_stored = sem("conv2_stored")
        idx_loaded = [sem("idx_loaded_a"), sem("idx_loaded_b")]
        adst_loaded = [sem("adst_loaded_a"), sem("adst_loaded_b")]
        batch_gathered = [sem("batch_gathered_a"), sem("batch_gathered_b")]
        batch_stored = [sem("batch_stored_a"), sem("batch_stored_b")]
        batch_diffs_ready = sem("batch_diffs_ready")
        batch_exps_ready = sem("batch_exps_ready")
        batch_done = sem("batch_done")
        links_ready = sem("links_ready")
        last_states_spread = sem("last_states_spread")
        lasts_shifted = sem("lasts_shifted")
        chunks_turned = sem("chunks_turned")
        carry_diffs_ready = sem("carry_diffs_ready")
        carry_exps_ready = sem("carry_exps_ready")
        carries_summed = sem("carries_summed")
        carries_turned = sem("carries_turned")
        carry_table_ready = sem("carry_table_ready")
        last_states_gathered = [sem("last_states_gathered_a"), sem("last_states_gathered_b")]
        own_rows_loaded = [sem("own_rows_loaded_a"), sem("own_rows_loaded_b")]
        chunks_spread = sem("chunks_spread")
        one_hot_ready = sem("one_hot_ready")
        carry_picked = sem("carry_picked")
        carry_copied = sem("carry_copied")
        share_diffs_ready = sem("share_diffs_ready")
        share_exps_ready = sem("share_exps_ready")
        group_variance_ready = sem("group_variance_ready")
        group_deviation_ready = sem("group_deviation_ready")
        last_group_done = sem("last_group_done")
        x_gnn_ready = sem("x_gnn_ready")
        tokens_turned = sem("tokens_turned")
        tokens_turned_copied = sem("tokens_turned_copied")
        logits_ready = sem("logits_ready")
        logits_copied = sem("logits_copied")
        gate_diff_ready = sem("gate_diff_ready")
        gate_exp_ready = sem("gate_exp_ready")
        mask_ready = sem("mask_ready")
        ranks_ready = sem("ranks_ready")
        places_ready = sem("places_ready")
        tiles_ready = sem("tiles_ready")
        pads_stored = sem("pads_stored")
        pad_tile_stored = sem("pad_tile_stored")
        pad_rows_ready = sem("pad_rows_ready")
        biased_loaded = sem("norm_ready_b")
        x_gnn_stored = sem("x_gnn_stored")
        conv_sum_ready = sem("x_loaded_b")
        group_normalised = sem("group_normalised")
        group_scales_ready = sem("group_scales_ready")
        row_ids_copied = sem("row_ids_copied")
        answer_added = sem("answer_added")
        conv2_adst_loaded = sem("conv2_adst_loaded")
        first_rows_ready = sem("first_rows_ready")
        tokens_placed = [sem("tokens_placed_a"), sem("tokens_placed_b")]
        expert_weights_loaded = sem("expert_weights_loaded")
        tile_loaded = [sem("tile_loaded_a"), sem("tile_loaded_b")]
        tile_turned = sem("tile_turned")
        tile_turned_copied = sem("tile_turned_copied")
        hidden_half_ready = sem("hidden_half_ready")
        w1_half_ready = sem("w1_half_ready")
        bias_ready = sem("bias_ready")
        gelu_ready = sem("gelu_ready")
        answer_product_ready = sem("answer_product_ready")
        answer_ready = sem("answer_ready")

        def hold(eng, which, s, value):
            eng.wait_ge(s, value)
            if not isinstance(value, int):
                eng.sem_inc(held[which], 1)

        def at_tile(t):
            return slice(t, t + 1) if isinstance(t, int) else bass.ds(t, 1)

        def exists(t):
            return not isinstance(t, int) or t < SLOTS

        V = nc.vector
        srcI = AR[:, 0:C].bitcast(I32)
        dstI = AR[:, C:2 * C].bitcast(I32)
        dstF = AR[:, 2 * C:3 * C]
        blkrow = [AR[:, J * ROWS + i * BLK:J * ROWS + (i + 1) * BLK] for i in range(GRP)]
        scr = AR[:, FB:FB + 1024]
        junk = [AR[:, FB + 1024 + NBLK * m:FB + 1024 + NBLK * (m + 1)] for m in range(GRP)]
        row = AR[:, FB + 1024 + GRP * NBLK:FB + 1024 + GRP * NBLK + RB * 288].rearrange("p (s r) -> p s r", s=RB)
        assert 1024 + GRP * NBLK + RB * 288 <= 5788
        norm_again = [AR[:, 3 * C + g * GRP * D:3 * C + (g + 1) * GRP * D].rearrange("p (t d) -> p t d", d=D) for g in range(2)]
        assert 3 * C + 2 * GRP * D <= J * ROWS
        def cut(a, n):
            return AR[:, FB + a:FB + a + n]

        adst_in = cut(1820, 4 * J * HD).rearrange("p (s j k h) -> p s j k h", s=2, k=2, h=HD)
        adst_edge = cut(3804, J * HD).rearrange("p (j h) -> p j h", h=HD)
        Z = cut(4300, J * HD).rearrange("p (j h) -> p j h", h=HD)
        DW = cut(4796, 2 * J * HD).rearrange("p (k j h) -> p k j h", k=2, h=HD)
        same = cut(5788, C)
        Wc = AR[:, J * ROWS + 4000:J * ROWS + 4576].rearrange("p (k f) -> p k f", k=KD)
        att = AR[:, J * ROWS + 5000:J * ROWS + 5000 + 4 * F].rearrange("p (k f) -> p k f", k=4)
        ln = AR[:, J * ROWS + 4600:J * ROWS + 4600 + 6 * NT].rearrange("p (t s) -> p t s", s=6)
        route_of = sb("route_of", [P, 6, GRP, NEX])
        tix = sb("tix", [P, GRP, 8], mybir.dt.uint32)
        top = sb("top", [P, GRP, 8])
        last1 = cut(1152, ROWS)
        rep = cut(1300, 4 * F).rearrange("p (k q f) -> p k q f", k=2, q=2)
        chunk_last = AR[:, FB:FB + 512].rearrange("p (k e) -> p k e", k=4)
        chunk_diff = AR[:, FB + 512:FB + 768].rearrange("p (k e) -> p k e", k=2)
        chunk_run = AR[:, FB + 768:FB + 1152].rearrange("p (k e) -> p k e", k=3)
        at = 0
        node_states = AR[:, at:at + 4 * GRP * ROWS].rearrange("p (s k t r) -> p s k t r", s=2, k=2, r=ROWS)
        at += 4 * GRP * ROWS
        node_carries = AR[:, at:at + 4 * GRP * ROWS].rearrange("p (s k t r) -> p s k t r", s=2, k=2, r=ROWS)
        at += 4 * GRP * ROWS
        own_rows = AR[:, at:at + 4 * GRP * ROWT].rearrange("p (s k t r) -> p s k t r", s=2, k=2, r=ROWT)
        at += 4 * GRP * ROWT
        norm_x = AR[:, at:at + GRP * D].rearrange("p (t d) -> p t d", d=D)
        at += GRP * D
        assert EARLY1 * KD * HID <= at
        prs = [AR[:, at:at + 2 * GRP * ROWP].rearrange("p (k t r) -> p k t r", k=2, r=ROWP)]
        at += 2 * GRP * ROWP
        assert at <= GW
        at = FB
        conv_sum = AR[:, at:at + GRP * D].rearrange("p (t d) -> p t d", d=D)
        at += GRP * D
        term_buf = AR[:, at:at + GRP * D].rearrange("p (t d) -> p t d", d=D)
        at += GRP * D
        prs.append(AR[:, at:at + 2 * GRP * ROWP].rearrange("p (k t r) -> p k t r", k=2, r=ROWP))
        pr = [prs[1], prs[0]]
        at += 2 * GRP * ROWP
        assert at <= AW, at
        own_score = sb("own_score", [P, NT, 16])
        bare = sb("bare", [P, 2, 2, NT])
        w1s = AR[:, 0:NEX * KD * HID].rearrange("p (e k h) -> p e k h", e=NEX, k=KD)
        w2s = AR[:, NEX * KD * HID:2 * NEX * KD * HID].rearrange("p (e m d) -> p e m d", e=NEX, m=MH)
        at = 2 * NEX * KD * HID
        xs = AR[:, at:at + 2 * ROWP].rearrange("p (s d) -> p s d", s=2)
        at += 2 * ROWP
        xsT = AR[:, at:at + 2 * D].rearrange("p (s k t) -> p s k t", s=2, k=KD)
        at += 2 * D
        w1_cur = AR[:, at:at + KD * HID].rearrange("p (k h) -> p k h", k=KD)
        at += KD * HID
        hsT = [a.rearrange("p (m t) -> p m t", m=MH) for a in (AR[:, at:at + HID], zero[:, :])]
        at += HID
        ys = AR[:, at:at + 2 * D].rearrange("p (s d) -> p s d", s=2)
        at += 2 * D
        assert at <= AW
        for e in range(1, EARLY + 1):
            assert GW <= NEX * KD * HID + e * MH * D and NEX * KD * HID + (e + 1) * MH * D <= GW + (NG - EARLY + e - 1) * GRP * D
        block = ctx.enter_context(nc.Block())

        @block.sync
        def _(sp):
            with nc.allow_non_contiguous_dma(reason="small tables, once"):
                sp.wait_ge(inputs_cleared, 1)
                sp.dma_start(dstI[0:P - 1, :], dst[0:(P - 1) * C].rearrange("(p j) -> p j", j=C)).then_inc(dst_loaded, 16)
                sp.dma_start(dstI[P - 1:P, 0:E - (P - 1) * C], dst[(P - 1) * C:E].rearrange("(a j) -> a j", a=1)).then_inc(dst_loaded, 16)
                sp.wait_ge(dst_numbers_ready, 1)
                sp.dma_start(dstp, dstF).then_inc(dst_numbers_stored, 16)
                sp.wait_ge(dst_numbers_stored, 16)
                sp.dma_start(blk[:, :], dstp.rearrange("p j -> (p j)").rearrange("(a b) -> a b", b=BLK)[:, 0:1].rearrange("a b -> b a")).then_inc(block_firsts_loaded, 16)
                sp.dma_start(srcI[0:P - 1, :], src[0:(P - 1) * C].rearrange("(p j) -> p j", j=C)).then_inc(edges_loaded, 16)
                sp.dma_start(srcI[P - 1:P, 0:E - (P - 1) * C], src[(P - 1) * C:E].rearrange("(a j) -> a j", a=1)).then_inc(edges_loaded, 16)
                sp.dma_start(idx1[:, 0, :], src[0:NP].rearrange("(p j) -> p j", j=J1)).then_inc(edges_loaded, 16)
                sp.dma_start(idx1[:, 1, :], dst[0:NP].rearrange("(p j) -> p j", j=J1)).then_inc(edges_loaded, 16)
                for dstt, v in ((b01[:, 0:F], b0), (b01[:, F:D], b1), (gam[:, :], gamma), (bet[:, :], beta), (bgb[:, :], bg)):
                    sp.dma_start(dstt, v.partition_broadcast(P)).then_inc(params_loaded, 16)
                sp.dma_start(wg[:, :, :], Wg.rearrange("(k p) e -> p k e", p=P)).then_inc(params_loaded, 16)
                sp.dma_start(eb2b[:, :, :], eb2.rearrange("e d -> (e d)").partition_broadcast(P)).then_inc(params_loaded, 16)
                for e in range(NEX):
                    sp.dma_start(eb1T[:, e, :], eb1[e].rearrange("(m p) -> p m", p=P)).then_inc(params_loaded, 16)
                sp.wait_ge(constants_made, 1)
                sp.dma_start(out[NP:NP + P, :], zero[:, 0:D]).then_inc(zeros_stored, 16)
                piece = -(-C * 2 * HD // NT)
                for t in range(NT):
                    sp.wait_ge(row_copied, t + 1)
                    for k in range(2):
                        sp.dma_start(tab[k][t * P:(t + 1) * P, :], row[:, t % RB, ROWT * k:ROWT * (k + 1)]).then_inc(row_stored[t % RB], 16)
                    w = min(piece, C * 2 * HD - t * piece)
                    sp.dma_start(adstart_c[:, t * piece:t * piece + w], zero[:, 0:w]).then_inc(zeros_stored, 16)
                sp.wait_ge(edges_loaded, 64)
                sp.dma_start(srcp, srcI).then_inc(src_stored, 16)
                sp.wait_ge(src_stored, 16)
                sp.dma_start(idx[:, 0, :], srcp[:, 0:J]).then_inc(idx_loaded[0], 16)
                sp.wait_ge(row_kept, NT)
                sp.dma_start(adt.rearrange("(t p) h -> p t h", p=P), adst_all[:, :, :]).then_inc(adst_stored, 16)
                sp.wait_ge(starts_ready, 1)
                sp.dma_start(degd.rearrange("(t p) a -> p (t a)", p=P), node_count[:, 4, :]).then_inc(degrees_stored, 16)
                sp.wait_ge(degrees_stored, 16)
                sp.dma_start(deg1[:, :], degd.rearrange("(p j) a -> p (j a)", p=P)).then_inc(degrees_loaded, 16)
                for g in range(NG):
                    sp.wait_ge(biased_ready, g + 1)
                    sp.dma_start(hbd[g * GRP * P:(g + 1) * GRP * P, :].rearrange("(t p) d -> p t d", p=P), norm_again[g % 2]).then_inc(biased_stored[g % 2], 16)
                sp.wait_ge(chunk_adst_gathered, 32)
                sp.wait_ge(adst_scattered, 16 * NT)
                sp.dma_start(adst_in[:, 1, 0:J1].rearrange("p j k h -> p (j k h)"), adstart[0:NP, :].rearrange("(p j) h -> p (j h)", p=P)).then_inc(conv2_adst_loaded, 16)
                sp.wait_ge(conv2_adst_loaded, 16)
                sp.dma_start(adstart.rearrange("(p j) h -> p j h", p=P)[:, 0, 0:HD], chunk_adst[:, 0, 0:HD]).then_inc(chunk_adst_patched, 16)
                sp.wait_ge(chunk_adst_patched, 16)
                sp.dma_start(adst_in[:, 0].rearrange("p j k h -> p (j k h)"), adstart_c[:, 0:J * 2 * HD]).then_inc(adst_loaded[0], 16)
                sp.wait_ge(conv2_states_ready, 1)
                sp.dma_start(state[1].rearrange("(p j) r -> p j r", p=P), G[1][:, 0:J1, :]).then_inc(conv2_stored, 16)
                def fetch(s, b):
                    sp.dma_start(idx[:, s, :], srcp[:, bass.ds(b * J, J)]).then_inc(idx_loaded[s], 16)
                    sp.dma_start(adst_in[:, s].rearrange("p j k h -> p (j k h)"), adstart_c[:, bass.ds(b * (J * 2 * HD), J * 2 * HD)]).then_inc(adst_loaded[s], 16)

                with sp.Fori(0, NB // 2 - 1) as i:
                    for s in range(2):
                        fetch(1 - s, i * 2 + (s + 1))
                        hold(sp, 0, batch_done, i * 2 + (s + 1))
                        sp.dma_start(states0[:, bass.ds((i * 2 + s) * (J * ROWS), J * ROWS)], G[s].rearrange("p j r -> p (j r)")).then_inc(batch_stored[s], 16)
                sp.dma_start(idx[:, 1, :], srcp[:, (NB - 1) * J:]).then_inc(idx_loaded[1], 16)
                sp.dma_start(adst_in[:, 1].rearrange("p j k h -> p (j k h)"), adstart_c[:, (NB - 1) * J * 2 * HD:]).then_inc(adst_loaded[1], 16)
                sp.wait_ge(batch_done, NB - 1)
                sp.dma_start(states0[:, (NB - 2) * J * ROWS:(NB - 1) * J * ROWS], G[0].rearrange("p j r -> p (j r)")).then_inc(batch_stored[0], 16)
                for q, (a, n) in enumerate(PARTS):
                    sp.wait_ge(batch_done, NB + q)
                    sp.dma_start(states0[:, ((NB - 1) * J + a) * ROWS:((NB - 1) * J + a + n) * ROWS], G[1][:, a:a + n, :].rearrange("p j r -> p (j r)")).then_inc(batch_stored[1], 16)
                def own(g):
                    if g >= 2:
                        sp.wait_ge(conv_sum_ready, g - 1)
                    for k in range(2):
                        sp.dma_start(own_rows[:, g % 2, k, :, :], tab[k][g * GRP * P:(g + 1) * GRP * P, :].rearrange("(t p) r -> p t r", p=P)).then_inc(own_rows_loaded[g % 2], 16)

                for s in range(2):
                    sp.wait_ge(batch_stored[s], 16 * (NB // 2 + s))

                def up_in(e):
                    sp.dma_start(w1s[:, e, :, :], eW1[e].rearrange("(k p) h -> p k h", p=P)).then_inc(expert_weights_loaded, 16)

                def down_in(e):
                    sp.dma_start(w2s[:, e, :, :], eW2[e].rearrange("(m p) d -> p m d", p=P)).then_inc(expert_weights_loaded, 16)

                def biased(g):
                    sp.dma_start(norm_x, hbd[g * GRP * P:(g + 1) * GRP * P, :].rearrange("(t p) d -> p t d", p=P)).then_inc(biased_loaded, 16)

                for s in range(2):
                    sp.wait_ge(biased_stored[s], 16 * ((NG + 1 - s) // 2))
                own(0)
                biased(0)
                for g in range(NG):
                    if g + 1 < NG:
                        own(g + 1)
                        sp.wait_ge(conv_sum_ready, g + 1)
                        biased(g + 1)
                    if g == NG - 1:
                        sp.wait_ge(conv_sum_ready, NG)
                        for e in range(EARLY1):
                            up_in(e)
                    sp.wait_ge(x_gnn_ready, g + 1)
                    if g >= 1:
                        sp.wait_ge(x_gnn_stored, 16 * g)
                    if g >= NG - EARLY:
                        down_in(g - (NG - EARLY) + 1)
                    sp.dma_start(out[g * GRP * P:(g + 1) * GRP * P, :].rearrange("(t p) d -> p t d", p=P), X[:, g * GRP:(g + 1) * GRP, :]).then_inc(x_gnn_stored, 16)
                sp.wait_ge(pad_rows_ready, 1)
                sp.dma_start(placed[NEX * REG:NEX * REG + P, :], padrow[:, :]).then_inc(pad_tile_stored, 16)
                sp.wait_ge(x_gnn_stored, 16 * NG)
                sp.wait_ge(last_group_done, 1)
                sp.wait_ge(group_normalised, 2 * NG)
                sp.wait_ge(tokens_placed[1], 16 * 2 * GRP * (NG // 2))
                for e in range(EARLY1, NEX):
                    up_in(e)
                for e in [0] + list(range(EARLY + 1, NEX)):
                    down_in(e)
                sp.wait_ge(tiles_ready, 1)
                sp.wait_ge(pads_stored, 16 * NEX)
                sp.wait_ge(pad_tile_stored, 16)

                def place_row(t):
                    return sp.value_load(reg[0:1, 1, at_tile(t)], min_val=0, max_val=NEX * REG)

                for s in range(2):
                    sp.dma_start(xs[:, s, :], placed[bass.ds(place_row(s), P), :]).then_inc(tile_loaded[s], 16)

                def tile_after(i, s):
                    r = place_row(i * 2 + (s + 2))
                    hold(sp, 0, tile_turned, i * 2 + (s + 1))
                    hold(sp, 0, row_ids_copied, i * 2 + (s + 1))
                    sp.dma_start(xs[:, s, :], placed[bass.ds(r, P), :]).then_inc(tile_loaded[s], 16)

                with sp.Fori(0, SLOTS // 2 - 1) as i:
                    for s in range(2):
                        tile_after(i, s)
                tile_after(SLOTS // 2 - 1, 0)
                sp.wait_ge(answer_added, 16 * SLOTS)

        @block.gpsimd
        def _(pool):
            g = nc.gpsimd
            g.memset(ones[:, :], 1.0)
            g.memset(ident[:, :], 0.0)
            g.memset(shf[:, :], 0.0)
            g.memset(wrap[:, :], 0.0)
            g.memset(zero[:, :], 0.0).then_inc(constants_made, 1)
            pool.wait_ge(constants_made, 1)
            g.affine_select(out=ident[:, :], in_=ident[:, :], compare_op=ALU.not_equal, fill=1.0, base=0, pattern=[[-1, P]], channel_multiplier=1)
            g.affine_select(out=shf[:, :], in_=shf[:, :], compare_op=ALU.not_equal, fill=1.0, base=1, pattern=[[-1, P]], channel_multiplier=1)
            g.affine_select(out=wrap[:, :], in_=wrap[:, :], compare_op=ALU.not_equal, fill=1.0, base=-(P - 1), pattern=[[-P, P]], channel_multiplier=1)
            g.affine_select(out=tri[:, :], in_=ones[:, :], compare_op=ALU.is_gt, fill=0.0, base=0, pattern=[[1, P]], channel_multiplier=-1)
            g.iota(pidx[:, :], pattern=[[0, 1]], base=0, channel_multiplier=1, allow_small_or_imprecise_dtypes=True)
            g.iota(nid[:, :], pattern=[[P, NT]], base=0, channel_multiplier=1, allow_small_or_imprecise_dtypes=True)
            g.iota(e8[:, :], pattern=[[1, HD]], base=0, channel_multiplier=0, allow_small_or_imprecise_dtypes=True)
            g.memset(padrow[:, :], 0.0)
            g.memset(tot[:, :], 0.0)
            g.iota(slot_id[:, :], pattern=[[P, SLOTS]], base=0, channel_multiplier=0, allow_small_or_imprecise_dtypes=True).then_inc(constants_made, 1)
            pool.wait_ge(dst_numbers_stored, 16)
            dblk = dstp.rearrange("p j -> (p j)").rearrange("(a b) -> a b", b=BLK)
            for t in range(NT):
                if t % GRP == 0:
                    pool.wait_ge(block_found, t // GRP + 1)
                if t >= GRP:
                    pool.wait_ge(block_counted, t - GRP + 1)
                pool.indirect_dma_start(out=blkrow[t % GRP], out_offset=None, in_=dblk,
                                        in_offset=bass.IndirectOffsetOnAxis(ap=node_index[:, 0, t:t + 1], axis=0)).then_inc(block_gathered[t % GRP], 16)
            for q in range(RB):
                pool.wait_ge(row_stored[q], 32 * (-(-(NT - q) // RB)))
            pool.wait_ge(edges_loaded, 64)
            pool.wait_ge(block_counted, NT)
            for j in range(J1):
                pool.indirect_dma_start(out=G[1][:, j, 0:ROWT], out_offset=None, in_=tab[1],
                                        in_offset=bass.IndirectOffsetOnAxis(ap=idx1[:, 0, j:j + 1], axis=0)).then_inc(conv2_gathered, 16)
            pool.wait_ge(starts_ready, 1)
            pool.wait_ge(row_kept, NT)
            pool.wait_ge(zeros_stored, 16 * (NT + 1))
            for t in range(NT):
                pool.indirect_dma_start(out=adstart, out_offset=bass.IndirectOffsetOnAxis(ap=node_index[:, 1, t:t + 1], axis=0),
                                        in_=adst_all[:, t, :], in_offset=None, bounds_check=EP - 1, oob_is_err=False).then_inc(adst_scattered, 16)
            pool.wait_ge(adst_stored, 16)
            for k, a in enumerate((ifirst, ifirst1)):
                pool.indirect_dma_start(out=chunk_adst[:, k, :], out_offset=None, in_=adt,
                                        in_offset=bass.IndirectOffsetOnAxis(ap=a[:, :], axis=0)).then_inc(chunk_adst_gathered, 16)

            def gather_part(s, a, n, done):
                for j in range(a, a + n):
                    pool.indirect_dma_start(out=G[s][:, j, 0:ROWT], out_offset=None, in_=tab[0],
                                            in_offset=bass.IndirectOffsetOnAxis(ap=idx[:, s, j:j + 1], axis=0)).then_inc(done, 16)

            def gather(s):
                gather_part(s, 0, J, batch_gathered[s])

            for s in range(2):
                pool.wait_ge(idx_loaded[s], 16)
                if s == 0:
                    for q in range(2):
                        pool.wait_ge(biased_stored[q], 16 * ((NG + 1 - q) // 2))
                if s == 1:
                    pool.wait_ge(conv2_stored, 16)
                gather(s)
            with pool.Fori(1, NB // 2 - 1) as i:
                for s in range(2):
                    hold(pool, 1, idx_loaded[s], i * 16 + 16)
                    hold(pool, 1, batch_stored[s], i * 16)
                    gather(s)
            for s in range(2):
                pool.wait_ge(idx_loaded[s], 16 * (NB // 2))
                pool.wait_ge(batch_stored[s], 16 * (NB // 2 - 1))
                if s == 0:
                    gather(s)
                else:
                    for (a, n), done in zip(PARTS, (batch_gathered[1], last_part_gathered)):
                        gather_part(s, a, n, done)
            def last_states(n, k):
                for t in range(GRP):
                    pool.indirect_dma_start(out=node_states[:, n % 2, k, t, :], out_offset=None, in_=state[k],
                                            in_offset=bass.IndirectOffsetOnAxis(ap=node_index[:, 2 + k, n * GRP + t:n * GRP + t + 1], axis=0)).then_inc(last_states_gathered[n % 2], 16)

            pool.wait_ge(batch_stored[0], 16 * (NB // 2))
            for n in range(2):
                last_states(n, 1)
            pool.wait_ge(batch_stored[1], 16 * (NB // 2 + 1))

            def place(n):
                pool.wait_ge(places_ready, n + 1)
                for k in range(2):
                    for t in range(GRP):
                        pool.indirect_dma_start(out=placed, out_offset=bass.IndirectOffsetOnAxis(ap=ipos[:, n % 2, k, t:t + 1], axis=0),
                                                in_=pr[n % 2][:, k, t, :], in_offset=None, bounds_check=NEX * REG + P - 1, oob_is_err=False).then_inc(tokens_placed[n % 2], 16)

            last_states(0, 0)
            for n in range(NG):
                if n == 0:
                    last_states(1, 0)
                elif n + 1 < NG:
                    pool.wait_ge(conv_sum_ready, n)
                    for k in range(2):
                        last_states(n + 1, k)
                if n >= 1:
                    place(n - 1)
            place(NG - 1)
            pool.wait_ge(tiles_ready, 1)
            for e in range(NEX):
                pool.indirect_dma_start(out=placed, out_offset=bass.IndirectOffsetOnAxis(ap=ipad[:, e:e + 1], axis=0),
                                        in_=padrow[:, :], in_offset=None, bounds_check=NEX * REG + P - 1, oob_is_err=False).then_inc(pads_stored, 16)
            def add_answer(s):
                pool.indirect_dma_start(out=out, out_offset=bass.IndirectOffsetOnAxis(ap=idb[:, s, :], axis=0),
                                        in_=ys[:, s, :], in_offset=None, bounds_check=NP + P - 1, oob_is_err=True, compute_op=ALU.add).then_inc(answer_added, 16)

            for s in range(2):
                pool.wait_ge(answer_ready, s + 1)
                if s:
                    pool.wait_ge(answer_added, 16)
                add_answer(s)
            with pool.Fori(1, SLOTS // 2) as i:
                for s in range(2):
                    hold(pool, 1, answer_ready, i * 2 + (s + 1))
                    hold(pool, 1, answer_added, i * 32 + 16 * s)
                    add_answer(s)
            pool.wait_ge(answer_ready, SLOTS)
            pool.wait_ge(answer_added, 16 * (SLOTS - 1))
            add_answer(0)

        @block.scalar
        def _(act):
            S = nc.scalar
            with nc.allow_non_contiguous_dma(reason="small tables, once"):
                act.wait_ge(inputs_cleared, 1)
                for k, w in enumerate((W0, W1)):
                    act.dma_start(Wc[:, :, ROWT * k:ROWT * k + F], w.rearrange("(k p) f -> p k f", p=P)).then_inc(proj_weights_loaded, 16)
                for k, a in enumerate((as0, as1, ad0, ad1)):
                    act.dma_start(att[:, k, :], a.rearrange("h c -> (h c)").partition_broadcast(P)).then_inc(proj_weights_loaded, 16)
                for g in range(NG):
                    full = min(GRP, NT - 1 - g * GRP)
                    if g == 1:
                        act.wait_ge(block_firsts_loaded, 16)
                    act.dma_start(X[:, g * GRP:g * GRP + full, :],
                                  x[g * GRP * P:(g * GRP + full) * P, :].rearrange("(t p) d -> p t d", p=P)).then_inc(x_loaded[g], 16)
                act.dma_start(X[0:TAIL, NT - 1, :], x[(NT - 1) * P:N, :]).then_inc(x_loaded[NG - 1], 16)

            def deviation(g):
                act.wait_ge(variances_ready, g + 1)
                S.activation(rstd[:, g * GRP:(g + 1) * GRP], mv[:, g * GRP:(g + 1) * GRP, 1], ACT.Sqrt).then_inc(deviations_ready, 1)

            def turned(t):
                act.wait_ge(norm_turned, t + 1)
                if t >= 2:
                    act.wait_ge(projected, t - 1)
                S.copy(hT[:, t % 2, :], ps[t % 2][:, 0:D]).then_inc(norm_turned_copied, 1)

            def rows(t):
                act.wait_ge(projected, t + 1)
                if t >= RB:
                    act.wait_ge(row_stored[t % RB], 32 * (t // RB))
                    act.wait_ge(row_kept, t - RB + 1)
                S.copy(row[:, t % RB, :], ps[2 + t % 2][:, 0:288]).then_inc(row_copied, 1)

            def within(t):
                act.wait_ge(block_gathered[t % GRP], 16 * (t // GRP + 1))
                S.activation(blkrow[t % GRP], blkrow[t % GRP], ACT.Sign, bias=nidh[:, t:t + 1], scale=-1.0, accum_out=node_count[:, 1, t:t + 1]).then_inc(block_counted, 1)

            act.wait_ge(node_half_ready, 1)
            for t in range(NT + LAG):
                if t % GRP == 0 and t < NT:
                    deviation(t // GRP)
                if t >= LAG:
                    within(t - LAG)
                if 1 <= t <= NT:
                    turned(t - 1)
                if 2 <= t < NT + 2:
                    rows(t - 2)
            for g in range(NG):
                if g >= 2:
                    act.wait_ge(biased_stored[g % 2], 16 * (g // 2))
                for t in range(g * GRP, (g + 1) * GRP):
                    last = S.activation(norm_again[g % 2][:, t % GRP, :], X[:, t, :], ACT.Identity, bias=nmr[:, t:t + 1], scale=rstd[:, t:t + 1])
                last.then_inc(norm_again_ready, 1)
            act.wait_ge(conv2_diffs_ready, 1)
            S.activation(DW[:, :, 0:J1, :], DW[:, :, 0:J1, :], ACT.Exp).then_inc(conv2_exps_ready, 1)
            def carry_exps(n):
                act.wait_ge(carry_diffs_ready, n + 1)
                S.activation(chunk_diff[:, :, :], chunk_diff[:, :, :], ACT.Exp).then_inc(carry_exps_ready, 1)

            carry_exps(0)
            with act.Fori(0, NB - 1) as b:
                hold(act, 2, batch_diffs_ready, b + 1)
                S.activation(DW[:, :, :, :], DW[:, :, :, :], ACT.Exp).then_inc(batch_exps_ready, 1)
            for q, (a, n) in enumerate(PARTS):
                act.wait_ge(batch_diffs_ready, NB + q)
                S.activation(DW[:, :, 0:n, :], DW[:, :, 0:n, :], ACT.Exp).then_inc(batch_exps_ready, 1)
            carry_exps(1)

            def carries(g):
                for n in range(g * GRP, (g + 1) * GRP):
                    m = n % GRP
                    act.wait_ge(carry_picked, n + 1)
                    S.copy(node_carries[:, g % 2].rearrange("p k t r -> p (k t r)")[:, 2 * m * ROWS:2 * (m + 1) * ROWS], ps[4 + n % 2][:, 0:2 * ROWS]).then_inc(carry_copied, 1)

            def share_exps(g):
                act.wait_ge(share_diffs_ready, g + 1)
                S.activation(share_of[:, g % 2, 0:3, :, :, :], share_of[:, g % 2, 0:3, :, :, :], ACT.Exp).then_inc(share_exps_ready, 1)

            def deviations(g, q):
                act.wait_ge(group_variance_ready, 2 * g + q + 1)
                S.activation(group_scale[:, 0, :], group_mv[:, :, 1], ACT.Sqrt).then_inc(group_deviation_ready, 1)
                act.wait_ge(group_scales_ready, 2 * g + q + 1)

            for s in range(2):
                act.wait_ge(batch_stored[s], 16 * (NB // 2 + s))
            carries(0)
            share_exps(0)
            for g in range(NG):
                if g + 1 < NG:
                    if g >= 1:
                        act.wait_ge(conv_sum_ready, g)
                    carries(g + 1)
                deviations(g, 0)
                for t in range(GRP):
                    last = S.activation(conv_sum[:, t, :], conv_sum[:, t, :], ACT.Identity, bias=group_scale[:, 2, t:t + 1], scale=group_scale[:, 1, t:t + 1])
                last.then_inc(group_normalised, 1)
                if g >= 1:
                    act.wait_ge(gate_diff_ready, g)
                    S.activation(gate_w[:, 0, :], gate_w[:, 0, :], ACT.Exp).then_inc(gate_exp_ready, 1)
                if g + 1 < NG:
                    share_exps(g + 1)
                deviations(g, 1)
                if g >= 2:
                    act.wait_ge(tokens_placed[g % 2], 16 * 2 * GRP * (g // 2))
                def row_of(k, t):
                    return S.activation(pr[g % 2][:, k, t, 0:D], X[:, g * GRP + t, :], ACT.Identity, bias=group_scale[:, 2, t:t + 1], scale=group_scale[:, 1, t:t + 1])

                for t in range(GRP):
                    last = row_of(0, t)
                last.then_inc(first_rows_ready, 1)
                for t in range(0, GRP, 2):
                    w = min(2, GRP - t)
                    for q in range(w):
                        last = row_of(1, t + q)
                    if t + w == GRP:
                        last.then_inc(group_normalised, 1)
                    act.wait_ge(tokens_turned, g * 4 + t // 2 + 1)
                    S.copy(hT4[:, (t // 2) % 2, 0:w * D], ps[(t // 2) % 2][:, 0:w * D]).then_inc(tokens_turned_copied, 1)
            act.wait_ge(gate_diff_ready, NG)
            S.activation(gate_w[:, 0, :], gate_w[:, 0, :], ACT.Exp).then_inc(gate_exp_ready, 1)
            def gelu(i, s):
                act.wait_ge(bias_ready, i * 2 + (s + 1))
                if not (isinstance(i, int) and i == 0):
                    act.wait_ge(answer_product_ready, i * 2 + (s - 1))
                for h in range(2):
                    act.wait_ge(hidden_half_ready, i * 4 + (2 * s + h + 1))
                    for m in range(h * MH // 2, (h + 1) * MH // 2):
                        last = S.activation(hsT[s][:, m, :], ps[2 * s + h][:, (m % 4) * P:(m % 4 + 1) * P], ACT.Gelu, bias=bcur[:, s, m:m + 1])
                last.then_inc(gelu_ready, 1)

            for s in range(2):
                gelu(0, s)
            with act.Fori(1, SLOTS // 2) as i:
                for s in range(2):
                    gelu(i, s)
            gelu(SLOTS // 2, 0)

        @block.tensor
        def _(pe):
            T = nc.tensor
            pe.wait_ge(constants_made, 2)
            pe.wait_ge(block_firsts_loaded, 16)
            T.matmul(ps[6][:, 0:NBLK], ones[0:1, :], blk[:, :], start=True, stop=True).then_inc(block_firsts_spread, 1)
            pe.wait_ge(att_weights_ready, 1)

            def project(t):
                pe.wait_ge(norm_turned_copied, t + 1)
                if t >= 2:
                    pe.wait_ge(row_copied, t - 1)
                for k in range(KD):
                    mm = T.matmul(ps[2 + t % 2][:, 0:288], hT[:, t % 2, k * P:(k + 1) * P], Wc[:, k, :], start=(k == 0), stop=(k == KD - 1))
                mm.then_inc(projected, 1)

            for t in range(NT):
                pe.wait_ge(norm_ready, t + 1)
                if t >= 2:
                    pe.wait_ge(norm_turned_copied, t - 1)
                for k in range(KD):
                    mm = T.transpose(ps[t % 2][:, k * P:(k + 1) * P], hrow[:, t % 2, k * P:(k + 1) * P], ident[:, :])
                mm.then_inc(norm_turned, 1)
                if t >= 1:
                    project(t - 1)
            project(NT - 1)
            pe.wait_ge(counts_ready, 1)
            T.matmul(ps[7][:, 0:NT], shf[:, :], node_count[:, 2, :], start=True, stop=False)
            T.matmul(ps[7][:, 1:NT], wrap[:, :], node_count[:, 2, 0:NT - 1], start=False, stop=True).then_inc(counts_shifted, 1)
            T.matmul(ps[6][:, 0:2], shf[:, :], ends[:, 0:2], start=True, stop=True).then_inc(lasts_shifted, 1)
            for n, k in enumerate((1, 0)):
                pe.wait_ge(last_states_spread, n + 1)
                pe.wait_ge(links_ready, 1)
                if n == 1:
                    pe.wait_ge(carry_table_ready, 1)
                last = carry if k == 0 else last1
                lk = sml[:, 8 + k:9 + k]
                T.matmul(ps[0][:, 0:P], bc(lk, [P, P]), ident[:, :], start=True, stop=True)
                T.matmul(ps[0][:, P:2 * P], rep[:, k, 1, :], ident[:, :], start=True, stop=True)
                T.matmul(ps[0][:, 2 * P:3 * P], rep[:, k, 0, :], ident[:, :], start=True, stop=True)
                T.matmul(ps[0][:, 3 * P:4 * P], last[:, 0:F], ident[:, :], start=True, stop=True).then_inc(chunks_turned, 1)
                pe.wait_ge(carries_summed, n + 1)
                for q in range(3):
                    mm = T.transpose(ps[1][:, q * P:(q + 1) * P], chunk_run[:, q, :], ident[:, :])
                mm.then_inc(carries_turned, 1)
            def broadcast(n):
                if n >= 2:
                    pe.wait_ge(one_hot_ready, n - 1)
                g, m = divmod(n, GRP)
                for q in range(2):
                    k, t = divmod(2 * m + q, GRP)
                    mm = T.matmul(ps[2 + n % 2][:, q * P:(q + 1) * P], bc(node_count[:, 5 + k, g * GRP + t:g * GRP + t + 1], [P, P]), ident[:, :], start=True, stop=True)
                mm.then_inc(chunks_spread, 1)

            def carries(g):
                for n in range(g * GRP, (g + 1) * GRP):
                    if n >= g * GRP + 2:
                        broadcast(n)
                    if n >= g * GRP + 1:
                        pick(n - 1)
                pick(g * GRP + GRP - 1)
                if g + 1 < NG:
                    for n in range(2):
                        broadcast((g + 1) * GRP + n)

            def pick(n):
                pe.wait_ge(one_hot_ready, n + 1)
                if n >= 2:
                    pe.wait_ge(carry_copied, n - 1)
                for q in range(2):
                    k = (2 * (n % GRP) + q) // GRP
                    mm = T.matmul(ps[4 + n % 2][:, q * ROWS:(q + 1) * ROWS], one_hot_of[:, n % 2, q * P:(q + 1) * P], carry_tab[:, k, :], start=True, stop=True)
                mm.then_inc(carry_picked, 1)

            def ranks(g):
                pe.wait_ge(mask_ready, g + 1)
                mk = route_of[:, 3, :, :].rearrange("p t e -> p (t e)")
                T.matmul(ps[7][:, 0:GRP * NEX], tri[:, :], mk, start=True, stop=True)
                T.matmul(ps[7][:, GRP * NEX:2 * GRP * NEX], ones[:, :], mk, start=True, stop=True).then_inc(ranks_ready, 1)

            def logits(g, t):
                w = min(2, GRP - t)
                pe.wait_ge(tokens_turned_copied, g * 4 + t // 2 + 1)
                for q in range(w):
                    for k in range(KD):
                        mm = T.matmul(ps[6][:, (t + q) * NEX:(t + q + 1) * NEX], hT4[:, (t // 2) % 2, (q * KD + k) * P:(q * KD + k + 1) * P], wg[:, k, :],
                                      start=(k == 0), stop=(k == KD - 1))
                return mm

            pe.wait_ge(carry_table_ready, 2)
            for n in range(2):
                broadcast(n)
            carries(0)
            for g in range(NG):
                if g + 1 < NG:
                    carries(g + 1)
                if g >= 1:
                    ranks(g - 1)
                pe.wait_ge(first_rows_ready, g + 1)
                for t in range(0, GRP, 2):
                    w = min(2, GRP - t)
                    for q in range(w):
                        for k in range(KD):
                            mm = T.transpose(ps[(t // 2) % 2][:, (q * KD + k) * P:(q * KD + k + 1) * P], pr[g % 2][:, 0, t + q, k * P:(k + 1) * P], ident[:, :])
                    mm.then_inc(tokens_turned, 1)
                    if t >= 2:
                        logits(g, t - 2)
                logits(g, GRP - 1).then_inc(logits_ready, 1)
            ranks(NG - 1)
            def turn(s):
                for k in range(KD):
                    mm = T.transpose(ps[4][:, k * P:(k + 1) * P], xs[:, s, k * P:(k + 1) * P], ident[:, :])
                mm.then_inc(tile_turned, 1)

            def up(s, t):
                for h in range(2):
                    pe.wait_ge(w1_half_ready, t * 2 + (h + 1))
                    for m in range(MH // 2):
                        for k in range(KD):
                            mm = T.matmul(ps[2 * s + h][:, m * P:(m + 1) * P], w1_cur[:, k, (h * 4 + m) * P:(h * 4 + m + 1) * P], xsT[:, s, k, :],
                                          start=(k == 0), stop=(k == KD - 1))
                    mm.then_inc(hidden_half_ready, 1)

            def down(s, e):
                for m in range(MH):
                    mm = T.matmul(ps[5][:, 0:D], hsT[s][:, m, :], AR[:, bass.ds(e * (MH * D) + (NEX * KD * HID + m * D), D)],
                                  start=(m == 0), stop=(m == MH - 1))
                mm.then_inc(answer_product_ready, 1)

            pe.wait_ge(tiles_ready, 1)
            pe.wait_ge(tile_loaded[0], 16)
            turn(0)
            pe.wait_ge(tile_turned_copied, 1)
            pe.wait_ge(tile_loaded[1], 16)
            turn(1)
            up(0, 0)
            pe.wait_ge(expert_weights_loaded, 32 * NEX)

            def one_tile(i, s):
                t = i * 2 + s
                e = pe.value_load(reg[0:1, 0, at_tile(t)], min_val=0, max_val=NEX - 1)
                if exists(t + 1):
                    pe.wait_ge(tile_turned_copied, i * 2 + (s + 2))
                    up(1 - s, i * 2 + (s + 1))
                if exists(t + 2):
                    pe.wait_ge(tile_loaded[s], i * 16 + 32)
                    turn(s)
                pe.wait_ge(gelu_ready, i * 2 + (s + 1))
                if not (isinstance(t, int) and t == 0):
                    pe.wait_ge(answer_ready, t)
                down(s, e)

            for t in range(2):
                one_tile(0, t)
            with pe.Fori(1, SLOTS // 2 - 1) as i:
                for s in range(2):
                    one_tile(i, s)
            for t in range(SLOTS - 3, SLOTS):
                one_tile(t // 2, t % 2)

        @block.vector
        def _(dve):
            dd = dve.drain
            V.memset(X[:, NT - 1, :], 0.0)
            V.memset(dstI[:, :], NP)
            V.memset(srcI[:, :], 0)
            V.memset(carry[:, :], 0.0)
            V.memset(adst_carry[:, :], 0.0)
            V.memset(same[:, 0:1], 0.0)
            V.memset(same1[:, 0:1], 0.0)
            dd()
            V.memset(node_count[:, :, :], 0.0).then_inc(inputs_cleared, 1)
            dve.wait_ge(dst_loaded, 32)
            V.tensor_copy(dstF, dstI).then_inc(dst_numbers_ready, 1)
            dd()
            V.tensor_tensor(same[:, 1:C], dstF[:, 1:C], dstF[:, 0:C - 1], ALU.is_equal)
            V.tensor_scalar(sml[:, 0:1], dstF[:, 0:1], float(NP - 1), None, ALU.min)
            V.tensor_scalar(ends[:, 0:1], dstF[:, C - 1:C], 1.0, None, ALU.add)
            V.tensor_scalar(ends[:, 2:3], dstF[:, 0:1], 1.0, None, ALU.add)
            dd()
            V.tensor_copy(ifirst[:, :], sml[:, 0:1])
            dve.wait_ge(constants_made, 2)
            V.tensor_scalar(nidh[:, :], nid[:, :], 0.5, None, ALU.add).then_inc(node_half_ready, 1)
            dve.wait_ge(proj_weights_loaded, 96)
            for c, (w, a) in enumerate(((0, 0), (1, 1), (0, 2), (1, 3))):
                to = (F, 2 * F + HD, 272, 280)[c]
                for k in range(KD):
                    dd()
                    V.tensor_tensor(scr[:, 0:F], Wc[:, k, ROWT * w:ROWT * w + F], att[:, a, :], ALU.mult)
                    dd()
                    last = V.tensor_reduce(Wc[:, k, to:to + HD], scr[:, 0:F].rearrange("p (h c) -> p h c", h=HD), AX.X, ALU.add)
            last.then_inc(att_weights_ready, 1)
            dd()

            def gather_stats(t):
                if t % GRP == 0:
                    dve.wait_ge(x_loaded[t // GRP], 32 if t // GRP == NG - 1 else 16)
                V.bn_stats(ln[:, t, :], X[:, t, :])

            def close_stats(g):
                dd()
                for t in range(g * GRP, (g + 1) * GRP):
                    V.bn_aggr(mv[:, t, :], ln[:, t, :])
                dd()
                V.tensor_scalar(mv[:, g * GRP:(g + 1) * GRP, 1], mv[:, g * GRP:(g + 1) * GRP, 1], EPS, None, ALU.add).then_inc(variances_ready, 1)

            def scales(g):
                gt = slice(g * GRP, (g + 1) * GRP)
                dve.wait_ge(deviations_ready, g + 1)
                V.reciprocal(rstd[:, gt], rstd[:, gt])
                dd()
                V.scalar_tensor_tensor(nmr[:, gt], mv[:, gt, 0], -1.0, rstd[:, gt], ALU.mult, ALU.mult).then_inc(norm_scales_ready, 1)

            def keep(t):
                dve.wait_ge(row_copied, t + 1)
                V.tensor_copy(asrc_all[:, t, 0:8], row[:, t % RB, F:F + HD])
                V.tensor_copy(asrc_all[:, t, 8:16], row[:, t % RB, 2 * F + HD:2 * F + 2 * HD])
                V.tensor_copy(adst_all[:, t, :], row[:, t % RB, 272:288]).then_inc(row_kept, 1)


            def normalise(t):
                if t % GRP == 0:
                    dd()
                if t >= 2:
                    dve.wait_ge(norm_turned, t - 1)
                V.tensor_scalar(hrow[:, t % 2, :], X[:, t, :], rstd[:, t:t + 1], nmr[:, t:t + 1], ALU.mult, ALU.add).then_inc(norm_ready, 1)

            def search(t):
                V.tensor_scalar(junk[t % GRP], ps[6][:, 0:NBLK], nid[:, t:t + 1], None, ALU.is_le, ALU.add, accum_out=node_count[:, 0, t:t + 1])

            def close_search(g):
                gt = slice(g * GRP, (g + 1) * GRP)
                dd()
                V.tensor_scalar(node_count[:, 0, gt], node_count[:, 0, gt], -1.0, 0.0, ALU.add, ALU.max)
                dd()
                V.tensor_copy(node_index[:, 0, gt], node_count[:, 0, gt]).then_inc(block_found, 1)

            for t in range(GRP):
                gather_stats(t)
            close_stats(0)
            scales(0)
            dve.wait_ge(block_firsts_spread, 1)
            for t in range(NT + 2):
                g, m = divmod(t, GRP)
                if t < NT:
                    normalise(t)
                if t + GRP < NT:
                    gather_stats(t + GRP)
                if t < NT:
                    search(t)
                    if m == GRP - 1:
                        close_search(g)
                        if g + 1 < NG:
                            close_stats(g + 1)
                if 2 <= t < NT + 2:
                    keep(t - 2)
                if m == GRP - 1 and g + 1 < NG:
                    scales(g + 1)
            dve.wait_ge(edges_loaded, 64)
            V.tensor_copy(dst1[:, :], idx1[:, 1, :])
            dd()
            V.tensor_tensor(same1[:, 1:J1], dst1[:, 1:J1], dst1[:, 0:J1 - 1], ALU.is_equal)
            V.tensor_scalar(ends[:, 1:2], dst1[:, J1 - 1:J1], 1.0, None, ALU.add)
            V.tensor_scalar(ends[:, 3:4], dst1[:, 0:1], 1.0, None, ALU.add)
            V.tensor_copy(ifirst1[:, :], dst1[:, 0:1])
            dd()
            dve.wait_ge(block_counted, NT)
            V.tensor_scalar(node_count[:, 1, :], node_count[:, 1, :], 0.5, 0.5 * BLK, ALU.mult, ALU.add)
            dd()
            V.scalar_tensor_tensor(node_count[:, 2, :], node_count[:, 0, :], float(BLK), node_count[:, 1, :], ALU.mult, ALU.add).then_inc(counts_ready, 1)
            dve.wait_ge(counts_shifted, 1)
            V.tensor_copy(node_count[:, 3, :], ps[7][:, 0:NT])
            dd()
            V.tensor_tensor(node_count[:, 4, :], node_count[:, 2, :], node_count[:, 3, :], ALU.subtract)
            dd()
            V.tensor_scalar(scr[:, 0:NT], node_count[:, 4, :], 0.0, float(SKIP), ALU.is_equal, ALU.mult)
            dd()
            V.tensor_tensor(scr[:, 0:NT], scr[:, 0:NT], node_count[:, 3, :], ALU.add)
            dd()
            V.tensor_copy(node_index[:, 1, :], scr[:, 0:NT]).then_inc(starts_ready, 1)
            dd()
            fin_ = scr[:, 64:64 + 8 * NT].rearrange("p (k t) -> p k t", k=8)
            for k in range(2):
                top_ = float(EP if k == 0 else N)
                cc = C if k == 0 else J1
                V.tensor_scalar(fin_[:, 0, :], node_count[:, 2, :], top_, None, ALU.min)
                V.tensor_scalar(fin_[:, 1, :], node_count[:, 3, :], top_, None, ALU.min)
                dd()
                V.tensor_tensor(fin_[:, 2, :], fin_[:, 0, :], fin_[:, 1, :], ALU.is_gt)
                V.tensor_scalar(fin_[:, 3, :], fin_[:, 0, :], -1.0, 0.0, ALU.add, ALU.max)
                dd()
                V.tensor_copy(node_index[:, 2 + k, :], fin_[:, 3, :])
                V.tensor_scalar(bare[:, k, 0, :], fin_[:, 2, :], -1.0, BIG, ALU.add, ALU.mult)
                V.tensor_scalar(fin_[:, 4, :], fin_[:, 3, :], 1.0 / cc, -0.5 + 0.5 / cc, ALU.mult, ALU.add)
                dd()
                V.tensor_scalar(fin_[:, 4, :], fin_[:, 4, :], MAGIC, None, ALU.add)
                dd()
                V.tensor_scalar(fin_[:, 4, :], fin_[:, 4, :], MAGIC, None, ALU.subtract)
                dd()
                V.tensor_scalar(fin_[:, 5, :], fin_[:, 4, :], float(cc), None, ALU.mult)
                dd()
                V.tensor_tensor(fin_[:, 5, :], fin_[:, 1, :], fin_[:, 5, :], ALU.is_lt)
                dd()
                V.tensor_tensor(fin_[:, 5, :], fin_[:, 5, :], fin_[:, 2, :], ALU.mult)
                dd()
                V.tensor_scalar(bare[:, k, 1, :], fin_[:, 5, :], -1.0, BIG, ALU.add, ALU.mult)
                V.tensor_tensor(fin_[:, 5, :], fin_[:, 5, :], fin_[:, 4, :], ALU.mult)
                dd()
                V.tensor_scalar(node_count[:, 5 + k, :], fin_[:, 5, :], -1.0, None, ALU.add)
                dd()
            dve.wait_ge(lasts_shifted, 1)
            V.tensor_tensor(sml[:, 2:4], ps[6][:, 0:2], ends[:, 2:4], ALU.is_equal)
            V.tensor_tensor(sml[:, 4:6], ends[:, 0:2], ends[:, 2:4], ALU.is_equal)
            dd()
            V.tensor_tensor(sml[:, 8:10], sml[:, 2:4], sml[:, 4:6], ALU.mult).then_inc(links_ready, 1)
            V.tensor_tensor(own_score[:, :, :], asrc_all[:, :, :], adst_all[:, :, :], ALU.add)
            dd()
            V.scalar_tensor_tensor(own_score[:, :, :], own_score[:, :, :], 0.2, own_score[:, :, :], ALU.mult, ALU.max)

            def scan_batch(Gs, n, smask, adv, wait_exp, diffs_ready, weight):
                z, r, w = Z[:, 0:n, :], DW[:, 0, 0:n, :], DW[:, 1, 0:n, :]
                ng = neg[:, 0:n]
                V.tensor_scalar(ng, smask, -1.0, BIG, ALU.add, ALU.mult)
                V.tensor_tensor(z, Gs[:, :, F:ROWT], adv, ALU.add)
                dd()
                V.scalar_tensor_tensor(z, z, 0.2, z, ALU.mult, ALU.max)
                dd()
                if weight is not None:
                    V.tensor_tensor(z, z, bc(dneg[:, 0:n].unsqueeze(2), [P, n, HD]), ALU.add)
                    dd()
                for h in range(HD):
                    V.tensor_tensor_scan(Gs[:, :, ROWT + h], ng, z[:, :, h], carry[:, ROWT + h:ROWT + h + 1], ALU.add, ALU.max)
                dd()
                m = Gs[:, :, ROWT:ROWS]
                V.tensor_tensor(r[:, 1:n, :], m[:, 0:n - 1, :], m[:, 1:n, :], ALU.subtract)
                V.tensor_tensor(r[:, 0, :], carry[:, ROWT:ROWS], m[:, 0, :], ALU.subtract)
                V.tensor_tensor(w, z, m, ALU.subtract)
                dd()
                V.tensor_tensor(r, r, bc(ng.unsqueeze(2), [P, n, HD]), ALU.add).then_inc(diffs_ready, 1)
                wait_exp()
                if weight is not None:
                    V.tensor_tensor(w, w, bc(weight.unsqueeze(2), [P, n, HD]), ALU.mult)
                    dd()
                V.tensor_tensor(Gs[:, :, 0:F].rearrange("p j (h c) -> p j h c", h=HD), Gs[:, :, 0:F].rearrange("p j (h c) -> p j h c", h=HD),
                                bc(w.unsqueeze(3), [P, n, HD, CH]), ALU.mult)
                for h in range(HD):
                    V.tensor_tensor_scan(Gs[:, :, F + h], r[:, :, h], w[:, :, h], carry[:, F + h:F + h + 1], ALU.mult, ALU.add)
                dd()
                for f in range(F):
                    V.tensor_tensor_scan(Gs[:, :, f], r[:, :, f // CH], Gs[:, :, f], carry[:, f:f + 1], ALU.mult, ALU.add)
                dd()

            def spread(k, s, n):
                for h in range(HD):
                    V.tensor_tensor_scan(adst_edge[:, 0:n, h], neg[:, 0:n], adst_in[:, s, 0:n, k, h], adst_carry[:, h:h + 1], ALU.mult, ALU.add)
                dd()

            dve.wait_ge(params_loaded, 16 * (7 + NEX))
            for g in range(NG):
                dve.wait_ge(norm_again_ready, g + 1)
                V.tensor_tensor(norm_again[g % 2], norm_again[g % 2], bc(b01[:, :].unsqueeze(1), [P, GRP, D]), ALU.add).then_inc(biased_ready, 1)
                V.tensor_tensor(X[:, g * GRP:(g + 1) * GRP, :], X[:, g * GRP:(g + 1) * GRP, :], bc(bet[:, :].unsqueeze(1), [P, GRP, D]), ALU.add)
            dve.wait_ge(degrees_loaded, 16)
            V.tensor_scalar(dneg[:, :], deg1[:, :], 0.0, -BIG, ALU.is_equal, ALU.mult)
            V.tensor_copy(neg[:, 0:J1], same1[:, :])
            dve.wait_ge(conv2_adst_loaded, 16)
            dve.wait_ge(chunk_adst_gathered, 32)
            V.tensor_copy(adst_in[:, 1, 0, 1, :], chunk_adst[:, 1, HD:2 * HD])
            dd()
            spread(1, 1, J1)
            dve.wait_ge(conv2_gathered, 16 * J1)
            scan_batch(G[1][:, 0:J1, :], J1, same1[:, :], adst_edge[:, 0:J1, :],
                       lambda: dve.wait_ge(conv2_exps_ready, 1), conv2_diffs_ready, deg1[:, :])
            V.tensor_copy(last1, G[1][:, J1 - 1, :]).then_inc(conv2_states_ready, 1)
            dd()

            def carry_table(k, n):
                a = (carry, last1)[k]
                for q in range(2):
                    V.tensor_copy(rep[:, k, q, :].rearrange("p (h c) -> p h c", h=HD),
                                  bc(a[:, F + HD * q:F + HD * (q + 1)].unsqueeze(2), [P, HD, CH]))
                dd()
                V.memset(sml[:, 1:2], 0.0).then_inc(last_states_spread, 1)
                dve.wait_ge(chunks_turned, n + 1)
                V.tensor_copy(chunk_last.rearrange("p k e -> p (k e)"), ps[0][:, :])
                dd()
                V.tensor_scalar(chunk_last[:, 0, :], chunk_last[:, 0, :], -1.0, BIG, ALU.add, ALU.mult)
                dd()
                V.tensor_tensor_scan(chunk_run[:, 0, :], chunk_last[:, 0, :], chunk_last[:, 1, :], 0.0, ALU.add, ALU.max)
                V.memset(chunk_diff[:, 0, 0:1], 0.0)
                dd()
                V.tensor_tensor(chunk_diff[:, 0, 1:P], chunk_run[:, 0, 0:P - 1], chunk_run[:, 0, 1:P], ALU.subtract)
                V.tensor_tensor(chunk_diff[:, 1, :], chunk_last[:, 1, :], chunk_run[:, 0, :], ALU.subtract)
                dd()
                V.tensor_tensor(chunk_diff[:, 0, :], chunk_diff[:, 0, :], chunk_last[:, 0, :], ALU.add).then_inc(carry_diffs_ready, 1)
                dve.wait_ge(carry_exps_ready, n + 1)
                for q in (2, 3):
                    V.tensor_tensor(chunk_last[:, q, :], chunk_last[:, q, :], chunk_diff[:, 1, :], ALU.mult)
                dd()
                V.tensor_tensor_scan(chunk_run[:, 1, :], chunk_diff[:, 0, :], chunk_last[:, 2, :], 0.0, ALU.mult, ALU.add)
                V.tensor_tensor_scan(chunk_run[:, 2, :], chunk_diff[:, 0, :], chunk_last[:, 3, :], 0.0, ALU.mult, ALU.add)
                dd()
                V.memset(sml[:, 1:2], 0.0).then_inc(carries_summed, 1)
                dve.wait_ge(carries_turned, n + 1)
                V.tensor_copy(carry_tab[:, k, 0:F], ps[1][:, 2 * P:3 * P])
                V.tensor_copy(carry_tab[:, k, F:ROWT], ps[1][:, P:2 * P].rearrange("p (h c) -> p h c", h=HD)[:, :, 0])
                V.tensor_copy(carry_tab[:, k, ROWT:ROWS], ps[1][:, 0:P].rearrange("p (h c) -> p h c", h=HD)[:, :, 0])
                dd()
                V.tensor_copy(sml[:, 2:3], sml[:, 8:9]).then_inc(carry_table_ready, 1)
                dd()

            carry_table(1, 0)

            def arrive(s, i, b):
                hold(dve, 4, adst_loaded[s], i * 16 + 16)
                V.tensor_copy(neg[:, :], same[:, bass.ds(b * J, J)])
                dd()
                spread(0, s, J)
                V.tensor_copy(adst_carry[:, :], adst_edge[:, J - 1, :])

            def whole_batch(s, i, b):
                arrive(s, i, b)
                hold(dve, 4, batch_gathered[s], (i + 1) * (16 * J))
                scan_batch(G[s], J, neg[:, :], adst_edge[:, :, :], lambda: hold(dve, 4, batch_exps_ready, b + 1), batch_diffs_ready, None)
                V.tensor_copy(carry[:, :], G[s][:, J - 1, :]).then_inc(batch_done, 1)
                dd()

            with dve.Fori(0, NB // 2 - 1) as i:
                for s in range(2):
                    whole_batch(s, i, i * 2 + s)
            whole_batch(0, NB // 2 - 1, NB - 2)
            arrive(1, NB // 2 - 1, NB - 1)
            for q, (a, n) in enumerate(PARTS):
                if q == 0:
                    dve.wait_ge(batch_gathered[1], (NB // 2 - 1) * 16 * J + 16 * n)
                else:
                    dve.wait_ge(last_part_gathered, 16 * n)
                scan_batch(G[1][:, a:a + n, :], n, neg[:, a:a + n], adst_edge[:, a:a + n, :], lambda: dve.wait_ge(batch_exps_ready, NB + q), batch_diffs_ready, None)
                V.tensor_copy(carry[:, :], G[1][:, a + n - 1, :]).then_inc(batch_done, 1)
                dd()
            carry_table(0, 1)


            def layer_stats(src_, g, q, next_one_hot=None):
                for t in range(GRP):
                    V.bn_stats(group_stats[:, t, :], src_[:, t, :])
                    if next_one_hot is not None and t % 2 == 1:
                        next_one_hot(4 + t // 2)
                dd()
                for t in range(GRP):
                    V.bn_aggr(group_mv[:, t, :], group_stats[:, t, :])
                dd()
                V.tensor_scalar(group_mv[:, :, 1], group_mv[:, :, 1], EPS, None, ALU.add).then_inc(group_variance_ready, 1)
                dve.wait_ge(group_deviation_ready, 2 * g + q + 1)
                V.reciprocal(group_scale[:, 1, :], group_scale[:, 0, :])
                dd()
                V.scalar_tensor_tensor(group_scale[:, 2, :], group_mv[:, :, 0], -1.0, group_scale[:, 1, :], ALU.mult, ALU.mult).then_inc(group_scales_ready, 1)

            def one_hot(n):
                dve.wait_ge(chunks_spread, n + 1)
                if n >= 2:
                    dve.wait_ge(carry_picked, n - 1)
                V.tensor_scalar(one_hot_of[:, n % 2, :], ps[2 + n % 2][:, 0:2 * P], pidx[:, 0:1], None, ALU.is_equal).then_inc(one_hot_ready, 1)

            def shares(g):
                z = share_of[:, g % 2]
                sg, cg = node_states[:, g % 2], node_carries[:, g % 2]
                gt = slice(g * GRP, (g + 1) * GRP)
                dve.wait_ge(last_states_gathered[g % 2], 16 * 2 * GRP * (g // 2 + 1))
                dve.wait_ge(carry_copied, GRP * (g + 1))
                for k in range(2):
                    for q, a in enumerate((sg, cg)):
                        V.tensor_tensor(z[:, q, k, :, :], a[:, k, :, ROWT:ROWS], bc(bare[:, k, q, gt].unsqueeze(2), [P, GRP, HD]), ALU.add)
                dd()
                zk = own_score[:, gt, :].rearrange("p t (k h) -> p k t h", k=2)
                V.tensor_tensor(z[:, 3], z[:, 0], z[:, 1], ALU.max)
                dd()
                V.tensor_tensor(z[:, 3], z[:, 3], zk, ALU.max)
                dd()
                for q in range(2):
                    V.tensor_tensor(z[:, q], z[:, q], z[:, 3], ALU.subtract)
                V.tensor_tensor(z[:, 2], zk, z[:, 3], ALU.subtract).then_inc(share_diffs_ready, 1)

            def choose(g):
                dve.wait_ge(logits_ready, g + 1)
                V.tensor_tensor(route_of[:, 0, :, :], ps[6][:, 0:GRP * NEX].rearrange("p (t e) -> p t e", e=NEX), bc(bgb[:, :].unsqueeze(1), [P, GRP, NEX]), ALU.add).then_inc(logits_copied, 1)
                dd()
                for t in range(GRP):
                    V.max(top[:, t, :], route_of[:, 0, t, :])
                dd()
                for t in range(GRP):
                    V.max_index(tix[:, t, :], top[:, t, :], route_of[:, 0, t, :])
                V.tensor_tensor(gate_w[:, 0, :], top[:, :, 1], top[:, :, 0], ALU.subtract).then_inc(gate_diff_ready, 1)
                dd()
                V.tensor_copy(pos[:, :, :], tix[:, :, 0:2].rearrange("p t k -> p k t"))
                dd()
                for k in range(2):
                    V.tensor_tensor(route_of[:, 1 + k, :, :], bc(pos[:, k, :].unsqueeze(2), [P, GRP, NEX]), bc(e8[:, :].unsqueeze(1), [P, GRP, NEX]), ALU.is_equal)
                dd()
                V.tensor_tensor(route_of[:, 3, :, :], route_of[:, 1, :, :], route_of[:, 2, :, :], ALU.add)
                dd()
                if g == NG - 1:
                    V.tensor_scalar(route_of[:, 3, GRP - 1, :], route_of[:, 3, GRP - 1, :], pcol[:, 0:1], None, ALU.mult)
                    dd()
                V.memset(sml[:, 5:6], 0.0).then_inc(mask_ready, 1)

            def settle(g):
                dve.wait_ge(gate_exp_ready, g + 1)
                V.tensor_scalar(gate_w[:, 1, :], gate_w[:, 0, :], 1.0, None, ALU.add)
                dve.wait_ge(ranks_ready, g + 1)
                for e in range(NEX):
                    V.tensor_tensor_scan(route_of[:, 4, :, e], bc(ones[:, 0:1], [P, GRP]), ps[7][:, GRP * NEX:2 * GRP * NEX].rearrange("p (t e) -> p t e", e=NEX)[:, :, e],
                                         tot[:, e:e + 1], ALU.mult, ALU.add)
                dd()
                V.reciprocal(gate_w[:, 1, :], gate_w[:, 1, :])
                V.tensor_tensor(route_of[:, 5, :, :], route_of[:, 4, :, :], ps[7][:, GRP * NEX:2 * GRP * NEX].rearrange("p (t e) -> p t e", e=NEX), ALU.subtract)
                V.tensor_copy(tot[:, :], route_of[:, 4, GRP - 1, :])
                dd()
                V.tensor_tensor(route_of[:, 5, :, :], route_of[:, 5, :, :], ps[7][:, 0:GRP * NEX].rearrange("p (t e) -> p t e", e=NEX), ALU.add)
                V.tensor_tensor(gate_w[:, 2, :], gate_w[:, 0, :], gate_w[:, 1, :], ALU.mult)
                dd()
                V.tensor_tensor(route_of[:, 5, :, :], route_of[:, 5, :, :], bc(e8r[:, :].unsqueeze(1), [P, GRP, NEX]), ALU.add)
                dd()
                for k in range(2):
                    V.tensor_tensor(route_of[:, 1 + k, :, :], route_of[:, 1 + k, :, :], route_of[:, 5, :, :], ALU.mult)
                dd()
                V.tensor_reduce(pos[:, :, :], route_of[:, 1:3, :, :], AX.X, ALU.add)
                dve.wait_ge(group_normalised, 2 * g + 2)
                for k in range(2):
                    V.tensor_copy(pr[g % 2][:, k, :, D], nid[:, g * GRP:(g + 1) * GRP])
                    V.tensor_copy(pr[g % 2][:, k, :, D + 1], gate_w[:, 1 + k, :])
                dd()
                if g == NG - 1:
                    V.tensor_scalar(pcol[:, :], pcol[:, :], -1.0, -float(SKIP), ALU.add, ALU.mult)
                    dd()
                    V.tensor_scalar(pos[:, :, GRP - 1], pos[:, :, GRP - 1], pcol[:, 0:1], None, ALU.add)
                    dd()
                if g >= 2:
                    dve.wait_ge(tokens_placed[g % 2], 16 * 2 * GRP * (g // 2))
                V.tensor_copy(ipos[:, g % 2, :, :], pos[:, :, :]).then_inc(places_ready, 1)
                dd()

            def combine(g):
                z = share_of[:, g % 2]
                sg, cg, xw = node_states[:, g % 2], node_carries[:, g % 2], own_rows[:, g % 2]
                dve.wait_ge(share_exps_ready, g + 1)
                V.tensor_scalar(z[:, 2, 1], z[:, 2, 1], 2.0, None, ALU.mult)
                V.tensor_tensor(z[:, 3], sg[:, :, :, F:ROWT], z[:, 0], ALU.mult)
                V.tensor_tensor(z[:, 4], cg[:, :, :, F:ROWT], z[:, 1], ALU.mult)
                dd()
                V.tensor_tensor(z[:, 3], z[:, 3], z[:, 4], ALU.add)
                dd()
                V.tensor_tensor(z[:, 3], z[:, 3], z[:, 2], ALU.add)
                dd()
                V.reciprocal(z[:, 4], z[:, 3])
                dd()
                for q in range(3):
                    V.tensor_tensor(z[:, q], z[:, q], z[:, 4], ALU.mult)
                dd()
                dve.wait_ge(own_rows_loaded[g % 2], 32 * (g // 2 + 1))

                def next_one_hot(m):
                    if g + 1 < NG:
                        one_hot((g + 1) * GRP + m)

                def scaled(to, a, q, k):
                    V.tensor_tensor(to[:, :, k * F:(k + 1) * F].rearrange("p t (h c) -> p t h c", h=HD),
                                    a[:, k, :, 0:F].rearrange("p t (h c) -> p t h c", h=HD), bc(z[:, q, k].unsqueeze(3), [P, GRP, HD, CH]), ALU.mult)

                for k in range(2):
                    scaled(conv_sum, sg, 0, k)
                    scaled(term_buf, cg, 1, k)
                dd()
                V.tensor_tensor(conv_sum, conv_sum, term_buf, ALU.add)
                next_one_hot(0)
                dd()
                for k in range(2):
                    scaled(term_buf, xw, 2, k)
                next_one_hot(1)
                dve.wait_ge(biased_loaded, 16 * (g + 1))
                dd()
                V.tensor_tensor(conv_sum, conv_sum, term_buf, ALU.add)
                next_one_hot(2)
                dd()
                V.tensor_tensor(conv_sum, conv_sum, norm_x, ALU.add).then_inc(conv_sum_ready, 1)
                next_one_hot(3)
                dd()
                layer_stats(conv_sum, g, 0, next_one_hot)

            def conclude(g):
                gt = slice(g * GRP, (g + 1) * GRP)
                dve.wait_ge(group_normalised, 2 * g + 1)
                V.tensor_tensor(conv_sum, conv_sum, bc(gam[:, :].unsqueeze(1), [P, GRP, D]), ALU.mult)
                dd()
                V.tensor_tensor(X[:, gt, :], X[:, gt, :], conv_sum, ALU.add).then_inc(x_gnn_ready, 1)
                dd()
                layer_stats(X[:, gt, :], g, 1)
                if g == NG - 1:
                    dd()
                    V.memset(sml[:, 5:6], 0.0).then_inc(last_group_done, 1)

            V.tensor_scalar(pcol[:, :], pidx[:, :], float(TAIL), None, ALU.is_lt)
            V.tensor_scalar(e8r[:, :], e8[:, :], float(REG), None, ALU.mult)
            V.tensor_scalar(padrow[:, D:D + 1], pidx[:, :], float(NP), None, ALU.add).then_inc(pad_rows_ready, 1)
            for n in range(GRP):
                one_hot(n)
            shares(0)
            for g in range(NG):
                combine(g)
                if g >= 1:
                    choose(g - 1)
                if g + 1 < NG:
                    shares(g + 1)
                if g >= 1:
                    settle(g - 1)
                conclude(g)
            choose(NG - 1)
            settle(NG - 1)
            V.tensor_scalar(toff[:, 0, :], tot[:, :], 1.0 / P, 0.5 - 0.5 / P, ALU.mult, ALU.add)
            V.tensor_tensor(toff[:, 3, :], tot[:, :], e8r[:, :], ALU.add)
            dd()
            V.tensor_scalar(toff[:, 3, :], toff[:, 3, :], pidx[:, 0:1], None, ALU.add)
            V.tensor_scalar(toff[:, 0, :], toff[:, 0, :], MAGIC, None, ALU.add)
            dd()
            V.tensor_copy(ipad[:, :], toff[:, 3, :])
            V.tensor_scalar(toff[:, 0, :], toff[:, 0, :], MAGIC, None, ALU.subtract)
            dd()
            V.tensor_scalar(toff[:, 0, :], toff[:, 0, :], float(P), None, ALU.mult)
            dd()
            V.tensor_tensor_scan(toff[:, 1, :], bc(ones[:, 0:1], [P, NEX]), toff[:, 0, :], 0.0, ALU.mult, ALU.add)
            V.tensor_scalar(toff[:, 2, :], toff[:, 0, :], -1.0, float(REG), ALU.mult, ALU.add)
            V.memset(tile_e[:, 0, :], 0.0)
            V.tensor_copy(tile_e[:, 1, :], slot_id[:, :])
            dd()
            for e in range(NEX):
                V.tensor_scalar(tile_e[:, 2, :], slot_id[:, :], toff[0:1, 1, e:e + 1], None, ALU.is_ge)
                dd()
                if e < NEX - 1:
                    V.tensor_tensor(tile_e[:, 0, :], tile_e[:, 0, :], tile_e[:, 2, :], ALU.add)
                    V.scalar_tensor_tensor(tile_e[:, 1, :], tile_e[:, 2, :], toff[0:1, 2, e:e + 1], tile_e[:, 1, :], ALU.mult, ALU.add)
                else:
                    V.scalar_tensor_tensor(tile_e[:, 2, :], tile_e[:, 2, :], float(NEX * REG), tile_e[:, 1, :], ALU.mult, ALU.max)
                dd()
            V.tensor_scalar(tile_e[:, 2, :], tile_e[:, 2, :], float(NEX * REG), None, ALU.min)
            dd()
            V.tensor_copy(reg[:, 0, :], tile_e[:, 0, :])
            V.tensor_copy(reg[:, 1, :], tile_e[:, 2, :]).then_inc(tiles_ready, 1)
            dd()

            def turned(s, value):
                dve.wait_ge(tile_turned, value)
                V.tensor_copy(xsT[:, s, :, :], ps[4][:, 0:D].rearrange("p (k t) -> p k t", k=KD)).then_inc(tile_turned_copied, 1)

            def expert_of(t):
                return dve.value_load(reg[0:1, 0, at_tile(t)], min_val=0, max_val=NEX - 1)

            def take_weights(h, e):
                V.tensor_copy(w1_cur[:, :, h * 512:(h + 1) * 512],
                              w1s[:, bass.ds(e, 1), :, h * 512:(h + 1) * 512].rearrange("p a k h -> p (a k) h")).then_inc(w1_half_ready, 1)

            def take_bias(s, e):
                V.tensor_copy(bcur[:, s, :], eb1T[:, bass.ds(e, 1), :].rearrange("p a m -> p (a m)")).then_inc(bias_ready, 1)

            def rows_of(s):
                V.tensor_copy(idb[:, s, :], xs[:, s, D:D + 1])
                V.tensor_copy(wb[:, s, :], xs[:, s, D + 1:D + 2]).then_inc(row_ids_copied, 1)

            def one_answer(i, s):
                first = isinstance(i, int) and i == 0
                t = i * 2 + s
                if exists(t + 2):
                    e = expert_of(i * 2 + (s + 2))
                    for h in range(2):
                        hold(dve, 4, hidden_half_ready, i * 4 + (2 * s + h + 3))
                        take_weights(h, e)
                    turned(s, t + 3)
                    hold(dve, 4, gelu_ready, t + 1)
                    take_bias(s, e)
                if exists(t + 1):
                    hold(dve, 4, tile_loaded[1 - s], (i + (1 + s)) * 16)
                    if not (first and s == 0):
                        hold(dve, 4, answer_added, t * 16)
                    rows_of(1 - s)
                e = expert_of(t)
                dve.wait_ge(answer_product_ready, t + 1)
                if not first:
                    dve.wait_ge(answer_added, (t - 1) * 16)
                V.tensor_tensor(ys[:, s, :], ps[5][:, 0:D], eb2b[:, bass.ds(e, 1), :].rearrange("p a d -> p (a d)"), ALU.add)
                dd()
                V.tensor_scalar(ys[:, s, :], ys[:, s, :], wb[:, s, 0:1], None, ALU.mult).then_inc(answer_ready, 1)

            turned(0, 1)
            e = expert_of(0)
            dve.wait_ge(expert_weights_loaded, 32 * NEX)
            for s in range(2):
                dve.wait_ge(tokens_placed[s], 16 * 2 * GRP * ((NG + 1 - s) // 2))
            for h in range(2):
                take_weights(h, e)
            take_bias(0, e)
            turned(1, 2)
            e = expert_of(1)
            for h in range(2):
                dve.wait_ge(hidden_half_ready, h + 1)
                take_weights(h, e)
            take_bias(1, e)
            dve.wait_ge(tile_loaded[0], 16)
            rows_of(0)
            for s in range(2):
                one_answer(0, s)
            with dve.Fori(1, SLOTS // 2 - 1) as i:
                for s in range(2):
                    one_answer(i, s)
            for t in range(SLOTS - 3, SLOTS):
                one_answer(t // 2, t % 2)


_INS = ["x", "src", "dst", "L0_gnn_W0", "L0_gnn_as0", "L0_gnn_ad0", "L0_gnn_b0", "L0_gnn_W1", "L0_gnn_as1", "L0_gnn_ad1",
        "L0_gnn_b1", "L0_gnn_gamma", "L0_gnn_beta", "L0_ffn_Wg", "L0_ffn_bg", "L0_ffn_W1", "L0_ffn_b1", "L0_ffn_W2", "L0_ffn_b2"]


def kernel(**inputs):
    import concourse.bacc as bacc
    from concourse.bass_utils import run_bass_kernel_spmd as run

    nc = bacc.Bacc("TRN2", target_bir_lowering=False, num_devices=1)
    arrays, args = {}, []
    for name in _INS:
        a = np.ascontiguousarray(inputs[name])
        arrays[f"in_{name}"] = a
        args.append(nc.dram_tensor(f"in_{name}", a.shape, mybir.dt.from_np(a.dtype), kind="ExternalInput").ap())
    args.append(nc.dram_tensor("out_0", (NP + P, D), F32, kind="ExternalOutput").ap())
    build(nc, *args)
    r = run(nc, [arrays], core_ids=[0])
    return r.results[0]["out_0"][:N]
```
